# Optimizing a Trainium2 kernel written in Bass

```python
import numpy as np
import jax
import jax.numpy as jnp

def _softmax(x, axis=-1):
    return jax.nn.softmax(x, axis=axis)

def _gelu(x):
    return jax.nn.gelu(x, approximate=True)

def _silu(x):
    return jax.nn.silu(x)

def _sigmoid(x):
    return jax.nn.sigmoid(x)

def _layernorm(x, axis=-1, eps=1e-05):
    m = jnp.mean(x, axis=axis, keepdims=True)
    v = jnp.var(x, axis=axis, keepdims=True)
    return (x - m) / jnp.sqrt(v + eps)

def _scatter_add(tgt, idx, src, axis=0):
    return tgt.at[idx].add(src)

def _segment_sum(src, seg, n):
    return jax.ops.segment_sum(src, seg, n)
kernel_name = 'mk_xattn_seq_d4_seqx_r8_98f97c'

def setup_inputs(seed: int=0):
    np.random.seed(seed)
    _w = jnp.asarray

    def _rec_inputs():
        import jax
        import jax.numpy as jnp
        _rk = jax.random.key(seed)
        x = 7.22e-05 + 1 * jax.random.normal(jax.random.fold_in(_rk, 1), (8, 256, 256), jnp.float32)
        _lenS = 256 - jax.random.randint(jax.random.fold_in(_rk, 7), (8,), 0, max(1, 256 // 4) + 1, jnp.int32)
        _lenS2 = 64 - jax.random.randint(jax.random.fold_in(_rk, 8), (8,), 0, max(1, 64 // 4) + 1, jnp.int32)
        _ctx_2048P = jax.random.normal(jax.random.fold_in(_rk, 11), (8, 16, 256), jnp.float32)
        _ctx_2048c = jax.random.dirichlet(jax.random.fold_in(_rk, 511), 0.3 * jnp.ones((16,), jnp.float32), (8, 64))
        _ctx_2048t = jnp.einsum('bsk,bkd->bsd', _ctx_2048c, _ctx_2048P)
        _ctx_2048t = _ctx_2048t * jax.lax.rsqrt(jnp.mean(jnp.square(_ctx_2048t)) + 1e-12) * 0.953939
        ctx_2048 = 4.13588e-05 + 0.999923 * (_ctx_2048t + 0.3 * jax.random.normal(jax.random.fold_in(_rk, 611), (8, 64, 256), jnp.float32))
        _validS = jnp.arange(256)[None, :] < _lenS[:, None]
        _validS2 = jnp.arange(64)[None, :] < _lenS2[:, None]
        _causal = jnp.tril(jnp.ones((256, 256), dtype=bool))
        mask_Bx1xSxS2_ff0 = jnp.where(jnp.ones((8, 1, 256, 64), dtype=bool), 0.0, -1000000000.0).astype(jnp.float32)
        mask_BxS2_ik0 = jnp.where(jnp.broadcast_to(_validS2[:, :], (8, 64)), 0, 1).astype(jnp.int32)
        mask_BxS2_bf1 = jnp.ones((8, 64), dtype=bool)
        return (x, ctx_2048, mask_Bx1xSxS2_ff0, mask_BxS2_ik0, mask_BxS2_bf1)
    x, ctx_2048, mask_Bx1xSxS2_ff0, mask_BxS2_ik0, mask_BxS2_bf1 = _rec_inputs()

    def _L0_xattn_setup():
        import jax, jax.numpy as jnp
        import numpy as np
        H = 256
        NH = 32
        KVH = 8
        HD = H // NH
        GROUPS = NH // KVH
        EPS = 1e-06
        B, L, S = (4, 128, 128)

        def _gqa_forward(hidden_state, encoder_hidden_state, encoder_attention_mask, Wq, bq, Wk, bk, Wv, bv, Wo, bo, gamma, beta):
            b, l, _ = hidden_state.shape
            s = encoder_hidden_state.shape[1]
            q = hidden_state @ Wq + bq
            k = encoder_hidden_state @ Wk + bk
            v = encoder_hidden_state @ Wv + bv
            q = q.reshape(b, l, KVH, GROUPS, HD).transpose(0, 2, 3, 1, 4)
            k = k.reshape(b, s, KVH, HD).transpose(0, 2, 1, 3)
            v = v.reshape(b, s, KVH, HD).transpose(0, 2, 1, 3)
            scale = 1.0 / jnp.sqrt(jnp.asarray(HD, q.dtype))
            scores = jnp.einsum('bkgld,bksd->bkgls', q, k) * scale
            scores = scores + encoder_attention_mask[:, :, None, :, :]
            attn = jax.nn.softmax(scores, axis=-1)
            out = jnp.einsum('bkgls,bksd->bkgld', attn, v)
            out = out.transpose(0, 3, 1, 2, 4).reshape(b, l, H)
            out = out @ Wo + bo
            x = out + hidden_state
            mu = jnp.mean(x, axis=-1, keepdims=True)
            var = jnp.var(x, axis=-1, keepdims=True)
            return (x - mu) * jax.lax.rsqrt(var + EPS) * gamma + beta
        key = jax.random.key(seed)
        ks = jax.random.split(key, 12)
        sd = 0.02
        return {'hidden_state': jax.random.normal(ks[0], (B, L, H), jnp.float32), 'encoder_hidden_state': jax.random.normal(ks[1], (B, S, H), jnp.float32), 'encoder_attention_mask': jnp.zeros((B, 1, L, S), jnp.float32), 'Wq': jax.random.normal(ks[2], (H, H), jnp.float32) * sd, 'bq': jnp.zeros((H,), jnp.float32), 'Wk': jax.random.normal(ks[3], (H, KVH * HD), jnp.float32) * sd, 'bk': jnp.zeros((KVH * HD,), jnp.float32), 'Wv': jax.random.normal(ks[4], (H, KVH * HD), jnp.float32) * sd, 'bv': jnp.zeros((KVH * HD,), jnp.float32), 'Wo': jax.random.normal(ks[5], (H, H), jnp.float32) * sd, 'bo': jnp.zeros((H,), jnp.float32), 'gamma': jnp.ones((H,), jnp.float32), 'beta': jnp.zeros((H,), jnp.float32)}
    _L0_xattn_all = _L0_xattn_setup()
    _L0_xattn_in = {k: v for k, v in _L0_xattn_all.items() if k in ('Wq', 'bq', 'Wk', 'bk', 'Wv', 'bv', 'Wo', 'bo', 'gamma', 'beta')}
    del _L0_xattn_all

    def _L1_xattn_setup():
        import jax, jax.numpy as jnp
        import numpy as np
        B, P, K, H, NH = (4, 256, 32, 256, 16)
        DH = H // NH
        EPS = 1e-06

        def rmsnorm(x, w):
            var = jnp.mean(jnp.square(x), axis=-1, keepdims=True)
            return x * jax.lax.rsqrt(var + EPS) * w
        key = jax.random.key(seed)
        ks = jax.random.split(key, 12)
        s = 0.02
        return {'x': jax.random.normal(ks[0], (B, P, H), jnp.float32), 'latents': jax.random.normal(ks[1], (B, K, H), jnp.float32), 'attention_mask': jax.random.randint(ks[2], (B, P), 0, 2, jnp.int32), 'q_w': s * jax.random.normal(ks[3], (H, H), jnp.float32), 'q_b': jnp.zeros((H,), jnp.float32), 'kv_w': s * jax.random.normal(ks[4], (H, 2 * H), jnp.float32), 'kv_b': jnp.zeros((2 * H,), jnp.float32), 'out_w': s * jax.random.normal(ks[5], (H, H), jnp.float32), 'out_b': jnp.zeros((H,), jnp.float32), 'postnorm_w': jnp.ones((H,), jnp.float32), 'mlp_w1': s * jax.random.normal(ks[6], (H, 4 * H), jnp.float32), 'mlp_b1': jnp.zeros((4 * H,), jnp.float32), 'mlp_w2': s * jax.random.normal(ks[7], (4 * H, H), jnp.float32), 'mlp_b2': jnp.zeros((H,), jnp.float32)}
    _L1_xattn_all = _L1_xattn_setup()
    _L1_xattn_in = {k: v for k, v in _L1_xattn_all.items() if k in ('q_w', 'q_b', 'kv_w', 'kv_b', 'out_w', 'out_b', 'postnorm_w', 'mlp_w1', 'mlp_b1', 'mlp_w2', 'mlp_b2')}
    del _L1_xattn_all

    def _L2_xattn_setup():
        import jax, jax.numpy as jnp
        import numpy as np
        B, P, K, H, NH = (4, 256, 32, 256, 16)
        DH = H // NH
        EPS = 1e-06

        def rmsnorm(x, w):
            var = jnp.mean(jnp.square(x), axis=-1, keepdims=True)
            return x * jax.lax.rsqrt(var + EPS) * w
        key = jax.random.key(seed)
        ks = jax.random.split(key, 12)
        s = 0.02
        return {'x': jax.random.normal(ks[0], (B, P, H), jnp.float32), 'latents': jax.random.normal(ks[1], (B, K, H), jnp.float32), 'attention_mask': jax.random.randint(ks[2], (B, P), 0, 2, jnp.int32), 'q_w': s * jax.random.normal(ks[3], (H, H), jnp.float32), 'q_b': jnp.zeros((H,), jnp.float32), 'kv_w': s * jax.random.normal(ks[4], (H, 2 * H), jnp.float32), 'kv_b': jnp.zeros((2 * H,), jnp.float32), 'out_w': s * jax.random.normal(ks[5], (H, H), jnp.float32), 'out_b': jnp.zeros((H,), jnp.float32), 'postnorm_w': jnp.ones((H,), jnp.float32), 'mlp_w1': s * jax.random.normal(ks[6], (H, 4 * H), jnp.float32), 'mlp_b1': jnp.zeros((4 * H,), jnp.float32), 'mlp_w2': s * jax.random.normal(ks[7], (4 * H, H), jnp.float32), 'mlp_b2': jnp.zeros((H,), jnp.float32)}
    _L2_xattn_all = _L2_xattn_setup()
    _L2_xattn_in = {k: v for k, v in _L2_xattn_all.items() if k in ('q_w', 'q_b', 'kv_w', 'kv_b', 'out_w', 'out_b', 'postnorm_w', 'mlp_w1', 'mlp_b1', 'mlp_w2', 'mlp_b2')}
    del _L2_xattn_all

    def _L3_xattn_setup():
        import jax, jax.numpy as jnp
        import numpy as np
        D = 256
        H = 16
        HD = D // H
        INNER = 4 * D
        EPS = 1e-05

        def layer_norm(x, w, b):
            mu = jnp.mean(x, axis=-1, keepdims=True)
            var = jnp.mean(jnp.square(x - mu), axis=-1, keepdims=True)
            return (x - mu) * jax.lax.rsqrt(var + EPS) * w + b
        key = jax.random.key(seed)
        ks = jax.random.split(key, 12)
        B, LQ, LK = (4, 128, 256)
        std = 0.02
        inp = {'hidden_states': jax.random.normal(ks[0], (B, LQ, D), jnp.float32), 'encoder_hidden_states': jax.random.normal(ks[1], (B, LK, D), jnp.float32), 'encoder_attention_mask': jnp.ones((B, LK), dtype=bool), 'ln1_w': jnp.ones((D,), jnp.float32), 'ln1_b': jnp.zeros((D,), jnp.float32), 'q_w': jax.random.normal(ks[2], (D, D), jnp.float32) * std, 'q_b': jnp.zeros((D,), jnp.float32), 'k_w': jax.random.normal(ks[3], (D, D), jnp.float32) * std, 'k_b': jnp.zeros((D,), jnp.float32), 'v_w': jax.random.normal(ks[4], (D, D), jnp.float32) * std, 'v_b': jnp.zeros((D,), jnp.float32), 'cproj_w': jax.random.normal(ks[5], (D, D), jnp.float32) * std, 'cproj_b': jnp.zeros((D,), jnp.float32), 'ln2_w': jnp.ones((D,), jnp.float32), 'ln2_b': jnp.zeros((D,), jnp.float32), 'fc_w': jax.random.normal(ks[6], (D, INNER), jnp.float32) * std, 'fc_b': jnp.zeros((INNER,), jnp.float32), 'proj_w': jax.random.normal(ks[7], (INNER, D), jnp.float32) * std, 'proj_b': jnp.zeros((D,), jnp.float32)}
        return inp
    _L3_xattn_all = _L3_xattn_setup()
    _L3_xattn_in = {k: v for k, v in _L3_xattn_all.items() if k in ('ln1_w', 'ln1_b', 'q_w', 'q_b', 'k_w', 'k_b', 'v_w', 'v_b', 'cproj_w', 'cproj_b', 'ln2_w', 'ln2_b', 'fc_w', 'fc_b', 'proj_w', 'proj_b')}
    del _L3_xattn_all
    return {'x': x, 'ctx_2048': ctx_2048, 'mask_Bx1xSxS2_ff0': mask_Bx1xSxS2_ff0, 'mask_BxS2_ik0': mask_BxS2_ik0, 'mask_BxS2_bf1': mask_BxS2_bf1, 'L0_xattn_Wq': _L0_xattn_in['Wq'], 'L0_xattn_bq': _L0_xattn_in['bq'], 'L0_xattn_Wk': _L0_xattn_in['Wk'], 'L0_xattn_bk': _L0_xattn_in['bk'], 'L0_xattn_Wv': _L0_xattn_in['Wv'], 'L0_xattn_bv': _L0_xattn_in['bv'], 'L0_xattn_Wo': _L0_xattn_in['Wo'], 'L0_xattn_bo': _L0_xattn_in['bo'], 'L0_xattn_gamma': _L0_xattn_in['gamma'], 'L0_xattn_beta': _L0_xattn_in['beta'], 'L1_xattn_q_w': _L1_xattn_in['q_w'], 'L1_xattn_q_b': _L1_xattn_in['q_b'], 'L1_xattn_kv_w': _L1_xattn_in['kv_w'], 'L1_xattn_kv_b': _L1_xattn_in['kv_b'], 'L1_xattn_out_w': _L1_xattn_in['out_w'], 'L1_xattn_out_b': _L1_xattn_in['out_b'], 'L1_xattn_postnorm_w': _L1_xattn_in['postnorm_w'], 'L1_xattn_mlp_w1': _L1_xattn_in['mlp_w1'], 'L1_xattn_mlp_b1': _L1_xattn_in['mlp_b1'], 'L1_xattn_mlp_w2': _L1_xattn_in['mlp_w2'], 'L1_xattn_mlp_b2': _L1_xattn_in['mlp_b2'], 'L2_xattn_q_w': _L2_xattn_in['q_w'], 'L2_xattn_q_b': _L2_xattn_in['q_b'], 'L2_xattn_kv_w': _L2_xattn_in['kv_w'], 'L2_xattn_kv_b': _L2_xattn_in['kv_b'], 'L2_xattn_out_w': _L2_xattn_in['out_w'], 'L2_xattn_out_b': _L2_xattn_in['out_b'], 'L2_xattn_postnorm_w': _L2_xattn_in['postnorm_w'], 'L2_xattn_mlp_w1': _L2_xattn_in['mlp_w1'], 'L2_xattn_mlp_b1': _L2_xattn_in['mlp_b1'], 'L2_xattn_mlp_w2': _L2_xattn_in['mlp_w2'], 'L2_xattn_mlp_b2': _L2_xattn_in['mlp_b2'], 'L3_xattn_ln1_w': _L3_xattn_in['ln1_w'], 'L3_xattn_ln1_b': _L3_xattn_in['ln1_b'], 'L3_xattn_q_w': _L3_xattn_in['q_w'], 'L3_xattn_q_b': _L3_xattn_in['q_b'], 'L3_xattn_k_w': _L3_xattn_in['k_w'], 'L3_xattn_k_b': _L3_xattn_in['k_b'], 'L3_xattn_v_w': _L3_xattn_in['v_w'], 'L3_xattn_v_b': _L3_xattn_in['v_b'], 'L3_xattn_cproj_w': _L3_xattn_in['cproj_w'], 'L3_xattn_cproj_b': _L3_xattn_in['cproj_b'], 'L3_xattn_ln2_w': _L3_xattn_in['ln2_w'], 'L3_xattn_ln2_b': _L3_xattn_in['ln2_b'], 'L3_xattn_fc_w': _L3_xattn_in['fc_w'], 'L3_xattn_fc_b': _L3_xattn_in['fc_b'], 'L3_xattn_proj_w': _L3_xattn_in['proj_w'], 'L3_xattn_proj_b': _L3_xattn_in['proj_b']}

def reference(x, ctx_2048, mask_Bx1xSxS2_ff0, mask_BxS2_ik0, mask_BxS2_bf1, L0_xattn_Wq, L0_xattn_bq, L0_xattn_Wk, L0_xattn_bk, L0_xattn_Wv, L0_xattn_bv, L0_xattn_Wo, L0_xattn_bo, L0_xattn_gamma, L0_xattn_beta, L1_xattn_q_w, L1_xattn_q_b, L1_xattn_kv_w, L1_xattn_kv_b, L1_xattn_out_w, L1_xattn_out_b, L1_xattn_postnorm_w, L1_xattn_mlp_w1, L1_xattn_mlp_b1, L1_xattn_mlp_w2, L1_xattn_mlp_b2, L2_xattn_q_w, L2_xattn_q_b, L2_xattn_kv_w, L2_xattn_kv_b, L2_xattn_out_w, L2_xattn_out_b, L2_xattn_postnorm_w, L2_xattn_mlp_w1, L2_xattn_mlp_b1, L2_xattn_mlp_w2, L2_xattn_mlp_b2, L3_xattn_ln1_w, L3_xattn_ln1_b, L3_xattn_q_w, L3_xattn_q_b, L3_xattn_k_w, L3_xattn_k_b, L3_xattn_v_w, L3_xattn_v_b, L3_xattn_cproj_w, L3_xattn_cproj_b, L3_xattn_ln2_w, L3_xattn_ln2_b, L3_xattn_fc_w, L3_xattn_fc_b, L3_xattn_proj_w, L3_xattn_proj_b):
    import jax
    import jax.numpy as jnp

    def _L0_xattn_ref(hidden_state, encoder_hidden_state, encoder_attention_mask, Wq, bq, Wk, bk, Wv, bv, Wo, bo, gamma, beta):
        import jax, jax.numpy as jnp
        import numpy as np
        H = 256
        NH = 32
        KVH = 8
        HD = H // NH
        GROUPS = NH // KVH
        EPS = 1e-06
        B, L, S = (4, 128, 128)

        def _gqa_forward(hidden_state, encoder_hidden_state, encoder_attention_mask, Wq, bq, Wk, bk, Wv, bv, Wo, bo, gamma, beta):
            b, l, _ = hidden_state.shape
            s = encoder_hidden_state.shape[1]
            q = hidden_state @ Wq + bq
            k = encoder_hidden_state @ Wk + bk
            v = encoder_hidden_state @ Wv + bv
            q = q.reshape(b, l, KVH, GROUPS, HD).transpose(0, 2, 3, 1, 4)
            k = k.reshape(b, s, KVH, HD).transpose(0, 2, 1, 3)
            v = v.reshape(b, s, KVH, HD).transpose(0, 2, 1, 3)
            scale = 1.0 / jnp.sqrt(jnp.asarray(HD, q.dtype))
            scores = jnp.einsum('bkgld,bksd->bkgls', q, k) * scale
            scores = scores + encoder_attention_mask[:, :, None, :, :]
            attn = jax.nn.softmax(scores, axis=-1)
            out = jnp.einsum('bkgls,bksd->bkgld', attn, v)
            out = out.transpose(0, 3, 1, 2, 4).reshape(b, l, H)
            out = out @ Wo + bo
            x = out + hidden_state
            mu = jnp.mean(x, axis=-1, keepdims=True)
            var = jnp.var(x, axis=-1, keepdims=True)
            return (x - mu) * jax.lax.rsqrt(var + EPS) * gamma + beta
        return _gqa_forward(hidden_state, encoder_hidden_state, encoder_attention_mask, Wq, bq, Wk, bk, Wv, bv, Wo, bo, gamma, beta)

    def _L1_xattn_ref(x, latents, attention_mask, q_w, q_b, kv_w, kv_b, out_w, out_b, postnorm_w, mlp_w1, mlp_b1, mlp_w2, mlp_b2):
        import jax, jax.numpy as jnp
        import numpy as np
        B, P, K, H, NH = (4, 256, 32, 256, 16)
        DH = H // NH
        EPS = 1e-06

        def rmsnorm(x, w):
            var = jnp.mean(jnp.square(x), axis=-1, keepdims=True)
            return x * jax.lax.rsqrt(var + EPS) * w
        b, p, _ = x.shape
        k_len = latents.shape[1]
        residual = latents
        h = jnp.concatenate([x, latents], axis=1)
        q = (latents @ q_w + q_b).reshape(b, k_len, NH, DH)
        kv = (h @ kv_w + kv_b).reshape(b, p + k_len, NH, DH, 2)
        kmat, v = (kv[..., 0], kv[..., 1])
        attn = jnp.einsum('bkhd,bnhd->bhkn', q, kmat) / DH
        full_mask = jnp.concatenate([attention_mask.astype(bool), jnp.ones((b, k_len), bool)], axis=-1)
        attn = jnp.where(full_mask[:, None, None, :], attn, -jnp.inf)
        attn = jax.nn.softmax(attn.astype(jnp.float32), axis=-1).astype(q.dtype)
        attn_out = jnp.einsum('bhkn,bnhd->bkhd', attn, v).reshape(b, k_len, H)
        attn_out = attn_out @ out_w + out_b + residual
        out = rmsnorm(attn_out, postnorm_w)
        out = jax.nn.gelu(out @ mlp_w1 + mlp_b1) @ mlp_w2 + mlp_b2
        return out + residual

    def _L2_xattn_ref(x, latents, attention_mask, q_w, q_b, kv_w, kv_b, out_w, out_b, postnorm_w, mlp_w1, mlp_b1, mlp_w2, mlp_b2):
        import jax, jax.numpy as jnp
        import numpy as np
        B, P, K, H, NH = (4, 256, 32, 256, 16)
        DH = H // NH
        EPS = 1e-06

        def rmsnorm(x, w):
            var = jnp.mean(jnp.square(x), axis=-1, keepdims=True)
            return x * jax.lax.rsqrt(var + EPS) * w
        b, p, _ = x.shape
        k_len = latents.shape[1]
        residual = latents
        h = jnp.concatenate([x, latents], axis=1)
        q = (latents @ q_w + q_b).reshape(b, k_len, NH, DH)
        kv = (h @ kv_w + kv_b).reshape(b, p + k_len, NH, DH, 2)
        kmat, v = (kv[..., 0], kv[..., 1])
        attn = jnp.einsum('bkhd,bnhd->bhkn', q, kmat) / DH
        full_mask = jnp.concatenate([attention_mask.astype(bool), jnp.ones((b, k_len), bool)], axis=-1)
        attn = jnp.where(full_mask[:, None, None, :], attn, -jnp.inf)
        attn = jax.nn.softmax(attn.astype(jnp.float32), axis=-1).astype(q.dtype)
        attn_out = jnp.einsum('bhkn,bnhd->bkhd', attn, v).reshape(b, k_len, H)
        attn_out = attn_out @ out_w + out_b + residual
        out = rmsnorm(attn_out, postnorm_w)
        out = jax.nn.gelu(out @ mlp_w1 + mlp_b1) @ mlp_w2 + mlp_b2
        return out + residual

    def _L3_xattn_ref(hidden_states, encoder_hidden_states, encoder_attention_mask, ln1_w, ln1_b, q_w, q_b, k_w, k_b, v_w, v_b, cproj_w, cproj_b, ln2_w, ln2_b, fc_w, fc_b, proj_w, proj_b):
        import jax, jax.numpy as jnp
        import numpy as np
        D = 256
        H = 16
        HD = D // H
        INNER = 4 * D
        EPS = 1e-05

        def layer_norm(x, w, b):
            mu = jnp.mean(x, axis=-1, keepdims=True)
            var = jnp.mean(jnp.square(x - mu), axis=-1, keepdims=True)
            return (x - mu) * jax.lax.rsqrt(var + EPS) * w + b
        B, LQ, _ = hidden_states.shape
        LK = encoder_hidden_states.shape[1]
        residual = hidden_states
        x = layer_norm(hidden_states, ln1_w, ln1_b)
        q = (x @ q_w + q_b).reshape(B, LQ, H, HD).transpose(0, 2, 1, 3)
        k = (encoder_hidden_states @ k_w + k_b).reshape(B, LK, H, HD).transpose(0, 2, 1, 3)
        v = (encoder_hidden_states @ v_w + v_b).reshape(B, LK, H, HD).transpose(0, 2, 1, 3)
        scale = 1.0 / np.sqrt(HD).astype(np.float32)
        scores = jnp.einsum('bhqd,bhkd->bhqk', q, k) * scale
        mask = encoder_attention_mask[:, None, None, :]
        mask_value = jnp.finfo(scores.dtype).min
        scores = jnp.where(mask, scores, mask_value)
        attn = jax.nn.softmax(scores, axis=-1)
        out = jnp.einsum('bhqk,bhkd->bhqd', attn, v)
        out = out.transpose(0, 2, 1, 3).reshape(B, LQ, D)
        out = out @ cproj_w + cproj_b
        hidden = out + residual
        residual = hidden
        y = layer_norm(hidden, ln2_w, ln2_b)
        y = jax.nn.gelu(y @ fc_w + fc_b, approximate=True)
        y = y @ proj_w + proj_b
        return residual + y
    x = _L0_xattn_ref(x, ctx_2048, mask_Bx1xSxS2_ff0, L0_xattn_Wq, L0_xattn_bq, L0_xattn_Wk, L0_xattn_bk, L0_xattn_Wv, L0_xattn_bv, L0_xattn_Wo, L0_xattn_bo, L0_xattn_gamma, L0_xattn_beta)
    x = _L1_xattn_ref(ctx_2048, x, mask_BxS2_ik0, L1_xattn_q_w, L1_xattn_q_b, L1_xattn_kv_w, L1_xattn_kv_b, L1_xattn_out_w, L1_xattn_out_b, L1_xattn_postnorm_w, L1_xattn_mlp_w1, L1_xattn_mlp_b1, L1_xattn_mlp_w2, L1_xattn_mlp_b2)
    x = _L2_xattn_ref(ctx_2048, x, mask_BxS2_ik0, L2_xattn_q_w, L2_xattn_q_b, L2_xattn_kv_w, L2_xattn_kv_b, L2_xattn_out_w, L2_xattn_out_b, L2_xattn_postnorm_w, L2_xattn_mlp_w1, L2_xattn_mlp_b1, L2_xattn_mlp_w2, L2_xattn_mlp_b2)
    x = _L3_xattn_ref(x, ctx_2048, mask_BxS2_bf1, L3_xattn_ln1_w, L3_xattn_ln1_b, L3_xattn_q_w, L3_xattn_q_b, L3_xattn_k_w, L3_xattn_k_b, L3_xattn_v_w, L3_xattn_v_b, L3_xattn_cproj_w, L3_xattn_cproj_b, L3_xattn_ln2_w, L3_xattn_ln2_b, L3_xattn_fc_w, L3_xattn_fc_b, L3_xattn_proj_w, L3_xattn_proj_b)
    return x

_drawn_inputs = setup_inputs


def setup_inputs(seed=0):
    import zlib

    import numpy as np

    out = dict(_drawn_inputs(seed))
    spreads = {'L0_xattn_bq': (0.0, 0.8),
     'L0_xattn_bk': (0.0, 0.8),
     'L0_xattn_bv': (0.0, 0.1),
     'L0_xattn_bo': (0.0, 0.1),
     'L0_xattn_gamma': (1.0, 0.2),
     'L0_xattn_beta': (0.0, 0.1),
     'L1_xattn_q_b': (0.0, 0.8),
     'L1_xattn_kv_b': (0.0, 0.8),
     'L1_xattn_out_b': (0.0, 0.8),
     'L1_xattn_postnorm_w': (1.0, 0.6),
     'L1_xattn_mlp_b1': (0.0, 0.1),
     'L1_xattn_mlp_b2': (0.0, 0.1),
     'L2_xattn_q_b': (0.0, 0.8),
     'L2_xattn_kv_b': (0.0, 0.8),
     'L2_xattn_out_b': (0.0, 0.713),
     'L2_xattn_postnorm_w': (1.0, 0.6),
     'L2_xattn_mlp_b1': (0.0, 0.1),
     'L2_xattn_mlp_b2': (0.0, 0.1),
     'L3_xattn_ln1_w': (1.0, 0.6),
     'L3_xattn_ln1_b': (0.0, 0.8),
     'L3_xattn_q_b': (0.0, 0.8),
     'L3_xattn_k_b': (0.0, 0.8),
     'L3_xattn_v_b': (0.0, 0.1),
     'L3_xattn_cproj_b': (0.0, 0.1),
     'L3_xattn_ln2_w': (1.0, 0.6),
     'L3_xattn_ln2_b': (0.0, 0.737),
     'L3_xattn_fc_b': (0.0, 0.1),
     'L3_xattn_proj_b': (0.0, 0.1)}
    factors = {'L0_xattn_Wq': 8.0,
     'L0_xattn_Wk': 8.0,
     'L1_xattn_q_w': 8.0,
     'L1_xattn_kv_w': 8.0,
     'L1_xattn_out_w': 8.0,
     'L2_xattn_q_w': 8.0,
     'L2_xattn_kv_w': 8.0,
     'L2_xattn_out_w': 8.0,
     'L3_xattn_q_w': 8.0,
     'L3_xattn_k_w': 8.0}
    for name, (base, spread) in spreads.items():
        noise = np.random.default_rng([zlib.crc32(name.encode()), seed]).standard_normal(out[name].shape)
        drawn = base * np.exp(spread * noise) if base else spread * noise
        out[name] = jnp.asarray(drawn.astype(out[name].dtype))
    for name, factor in factors.items():
        out[name] = (out[name] * factor).astype(out[name].dtype)
    return out
```

```python
from contextlib import ExitStack

import concourse.bass as bass
from concourse import mybir

F32 = mybir.dt.float32
F32R = mybir.dt.float32r
BF16 = mybir.dt.bfloat16
I32 = mybir.dt.int32
U8 = mybir.dt.uint8
ACT = mybir.ActivationFunctionType
ALU = mybir.AluOpType
AX = mybir.AxisListType

P = 128
B = 8
S = 256
SC = 64
D = 256
DC = D // P
QT = S // P
FF = 4 * D
FC = FF // P
ROWS = 16
NTERM = 3
Q_TERMS = (0, 1, 2, 0, 1, 0)
K_TERMS = (0, 0, 0, 1, 1, 2)
MASK_ROW = 96
MAX_ROW = 97
KS = MASK_ROW + 1
KST = MAX_ROW + 2
NEG = -1.0e30
VW = 32
ONES = 16
MAGIC = float(0x5F3759DF)
TWO_ONES = (0x3F803F80 & 0x7FFFFF | 0x800000) / 2.0 ** 23


class Cfg:

    def __init__(self, n, heads, kvheads, latent, scale, norm, eps, mlp, pre_norm, mask):
        self.n, self.heads, self.kvheads, self.latent = n, heads, kvheads, latent
        self.scale, self.norm, self.eps, self.mlp = scale, norm, eps, mlp
        self.pre_norm, self.mask = pre_norm, mask
        self.dh = D // heads
        self.kvw = kvheads * self.dh
        self.keys = S + SC if latent else SC
        self.c0 = S if latent else 0
        self.groups = heads // 4
        self.rowvs = 2 if mlp else 3
        self.spu = 1 if latent else 8
        self.s_uses = QT * heads // self.spu
        self.st_group = 5 if latent else 1
        self.r_uses = self.s_uses + QT + self.st_group * self.groups
        self.a_uses = 4 if latent else 2
        self.ot_uses = self.groups // 2
        self.m_uses = self.ot_uses + 2 + (6 if mlp else 0)
        self.o_uses = self.groups
        off, self.w = 0, {}
        kv = [("k", DC, D), ("v", DC, D)] if self.kvw == D else [("kv", DC, P)]
        for name, k, cols in [("q", DC, D)] + kv + [("o", DC, D)] + (
                [("w1", DC, FF), ("w2", FC, D)] if mlp else []):
            self.w[name] = (off, k, cols)
            off += k * cols
        self.wcols = off


LAYERS = [
    Cfg(0, 32, 8, False, 8 ** -0.5, "ln", 1e-6, False, False, "add"),
    Cfg(1, 16, 16, True, 1 / 16, "rms", 1e-6, True, False, "int"),
    Cfg(2, 16, 16, True, 1 / 16, "rms", 1e-6, True, False, "int"),
    Cfg(3, 16, 16, False, 0.25, "ln", 1e-5, True, True, "bool"),
]
COLS = {"bq": 0, "bk": 2, "bv": 4, "n_w": 6, "n_b": 8, "p_w": 10, "p_b": 12, "b1": 14}
NCOLS = 22
ROWV = {"bo": 0, "b2": 1, "g": 1, "b": 2}



class Seq:

    def __init__(self, j, k):
        self.j, self.k, self.par = j, k, k % 2

    def count(self, per, more=0):
        c = per * (self.k + 1) + more
        return c if isinstance(self.j, int) else self.j * (2 * per) + c

    def count_par(self, per, more=0):
        c = per * (self.k // 2 + 1) + more
        return c if isinstance(self.j, int) else self.j * per + c

    def index(self):
        return self.k if isinstance(self.j, int) else self.j * 2 + self.k

    def before(self, n):
        return Seq(self.j, self.k - n)


def program(nc, x, ctx_t, w, cols, rows, mask_q, mask_k, mask_i, mask_b, out):
    top = ExitStack()
    with top:
        x_all = top.enter_context(nc.sbuf_tensor("x_all", [P, B * QT, D], F32))
        ident = top.enter_context(nc.sbuf_tensor("ident", [P, P], F32))
        ident16 = top.enter_context(nc.sbuf_tensor("ident16", [P, P], BF16))
        banks = [top.enter_context(nc.psum_tensor(f"bank{i}", [P, 512], F32)) for i in range(8)]
        for cfg in LAYERS:
            layer(nc, cfg, banks, x_all, ident, ident16, x, ctx_t, w[cfg.n], cols[cfg.n], rows[cfg.n],
                  mask_q, mask_k, mask_i, mask_b, out)


def layer(nc, cfg, banks, x_all, ident, ident16, x, ctx_t, w_in, cols_in, rows_in,
          mask_q, mask_k, mask_i, mask_b, out):
    L = f"L{cfg.n}_"
    H, DH, G, KV = cfg.heads, cfg.dh, cfg.groups, cfg.kvheads
    lay = ExitStack()
    with lay:
        def sb(name, shape, dt=F32):
            return lay.enter_context(nc.sbuf_tensor(L + name, shape, dt))

        taken = []

        def sem(name):
            s = lay.enter_context(nc.semaphore(L + name))
            taken.append(s)
            return s

        w_hi = sb("w_hi", [P, cfg.wcols], F32R)
        w_lo = sb("w_lo", [P, cfg.wcols], F32R)
        col = sb("col", [P, NCOLS])
        row = sb("row", [P, cfg.rowvs, D])
        bq_scaled = sb("bq_scaled", [P, DC])
        stack_q = [sb(f"stack_q{i}", [P, H, S], BF16) for i in range(2)]
        stack_k = [sb(f"stack_k{i}", [P, KV, cfg.keys], BF16) for i in range(2)]
        v_ctx = sb("v_ctx", [P, B, cfg.kvw])
        va_ctx = [sb(f"va_ctx{i}", [P, H, VW]) for i in range(2)]
        q_dram = nc.dram_tensor(L + "q_terms", (B, NTERM, D, S), BF16, kind="Internal").ap()
        k_dram = nc.dram_tensor(L + "k_terms", (B, NTERM, cfg.kvw, cfg.keys), BF16, kind="Internal").ap()
        mask_dram = nc.dram_tensor(L + "mask_rows", (B, SC), BF16, kind="Internal").ap()

        def wgt(part, name, k, c0=0, n=None):
            off, _, width = cfg.w[name]
            return part[:, off + k * width + c0:off + k * width + c0 + (n or width)]

        rise = {}

        def counted(name, per=1):
            s = sem(name)
            rise[name] = (s, per)
            return s

        R0, O0, A0, M0 = 0, 2, 4, 6
        USES = {R0: cfg.r_uses, O0: cfg.o_uses, A0: cfg.a_uses, M0: cfg.m_uses}
        bank_full = [counted(f"bank_full{i}", USES[i // 2 * 2] // 2) for i in range(8)]
        xc_ready, xn_ready = counted("xc_ready"), counted("xn_ready")
        X_PARTS = DC if cfg.pre_norm else 1
        x_full_ready = counted("x_full_ready", X_PARTS)
        x_hi_ready, x_lo_ready = counted("x_hi_ready"), counted("x_lo_ready")
        q_full_ready, q_h, q_r, q_m, q_l = counted("q_full_ready", DC), *map(counted, ("q_h", "q_r", "q_m", "q_l"))
        k_full_ready, k_h, k_r, k_m, k_l = counted("k_full_ready", DC), *map(counted, ("k_h", "k_r", "k_m", "k_l"))
        va_ready, va_ctx_ready = counted("va_ready"), counted("va_ctx_ready", 2)
        q_written, k_written = counted("q_written", 16), counted("k_written", 16)
        n_stack = len(Q_TERMS) + len(K_TERMS) + (cfg.mask != "add")
        STACK = 16 * n_stack
        stack_loaded = [counted(f"stack_loaded{i}", STACK) for i in range(2)]
        masks_loaded = [counted(f"masks_loaded{i}", 48) for i in range(2)]
        max_loaded = [counted(f"max_loaded{i}", 32) for i in range(2)]
        s_masked, peak_done = counted("s_masked", cfg.s_uses), counted("peak_done", cfg.s_uses)
        neg_h, neg_done = counted("neg_h", QT), counted("neg_done", QT)
        peak_t_ready = counted("peak_t_ready", QT)
        st_masked = counted("st_masked", G)
        EXPS = cfg.st_group * G
        exp_done = counted("exp_done", EXPS)
        o_t_ready = counted("o_t_ready", G)
        rec_ready, o_tok_ready = counted("rec_ready", cfg.ot_uses), counted("o_tok_ready", cfg.ot_uses)
        o_full_ready, o_hi_ready, o_lo_ready = counted("o_full_ready", DC), counted("o_hi_ready"), counted("o_lo_ready")
        xb_ready, xb2_ready = counted("xb_ready", QT), counted("xb2_ready", QT)
        att_ready, y_ready = counted("att_ready"), counted("y_ready")
        y_full_ready, y_hi_ready, y_lo_ready = counted("y_full_ready", DC), counted("y_hi_ready"), counted("y_lo_ready")
        h_full_ready, h_hi_ready, h_lo_ready = counted("h_full_ready", FC), counted("h_hi_ready", 4), counted("h_lo_ready", 4)
        g_ready, x_new = counted("g_ready"), counted("x_new")
        NORM = 14 if cfg.norm == "ln" else 15
        norm_step, pre_step = counted("norm_step", NORM), counted("pre_step", NORM)
        stored = [counted(f"stored{i}", 16) for i in range(2)]
        ones_ready = sem("ones_ready")

        prepare(nc, cfg, banks, x_all, ident, ident16, x, ctx_t, w_in, cols_in, rows_in, mask_i, mask_b,
                w_hi, w_lo, col, row, bq_scaled, stack_q, stack_k, v_ctx, va_ctx, k_dram, mask_dram, wgt, rise)

        xc = sb("xc", [P, QT, D])
        xb = [sb(f"xb{i}", [P, QT, D]) for i in range(2)]
        x_t = [sb(f"x_t_{p}", [P, DC, S], F32R) for p in ("hi", "lo")]
        x_full = sb("x_full", [P, DC, S])
        q_full = sb("q_full", [P, DC, S])
        q_rest = sb("q_rest", [P, DC, S])
        q_term = sb("q_term", [P, NTERM, DC, S], BF16)
        if cfg.latent:
            k_full = sb("k_full", [P, DC, S])
            k_rest = sb("k_rest", [P, DC, S])
            k_term = sb("k_term", [P, NTERM, DC, S], BF16)
            va = [sb(f"va{i}", [P, QT, H, VW]) for i in range(2)]
            p_lat = sb("p_lat", [P, 6, QT, S])
        p_ctx = sb("p_ctx", [P, 2, 2, S])
        peak = sb("peak", [P, QT, H])
        neg_peak = sb("neg_peak", [P, QT, 2, H], BF16)
        peak_t = sb("peak_t", [H, 2, QT, P], BF16)
        o_t = sb("o_t", [P, G, S])
        o_rec = sb("o_rec", [P, 2, 2, QT, 4])
        o_tok = sb("o_tok", [P, QT, D])
        o_full = sb("o_full", [P, DC, S])
        o_f = [sb(f"o_f_{p}", [P, DC, S], F32R) for p in ("hi", "lo")]
        att = sb("att", [P, QT, D])
        y = o_tok
        st6 = sb("st6", [P, QT, 6])
        mv = sb("mv", [P, QT, 2])
        nw = sb("nw", [P, 5, QT])
        if cfg.pre_norm:
            xn = sb("xn", [P, QT, D])
        if cfg.mask == "add":
            mq = [sb(f"mq{i}", [P, QT, SC]) for i in range(2)]
            mk = [sb(f"mk{i}", [P, S]) for i in range(2)]
            s_tmp = sb("s_tmp", [P, 2, 8, SC])
            st_tmp = sb("st_tmp", [P, 2, 2, S])
        if cfg.mlp:
            y_full = o_full
            y_t = [sb(f"y_t_{p}", [P, DC, S], F32R) for p in ("hi", "lo")]
            h_full = sb("h_full", [P, 2, 2, S])
            h_t = [sb(f"h_t_{p}", [P, FC, S], F32R) for p in ("hi", "lo")]
            xb2 = sb("xb2", [P, QT, D])
        if cfg.n == 3:
            y_out = [sb(f"y_out{i}", [P, QT, D]) for i in range(2)]

        M_BACK = cfg.ot_uses
        M_PROJ, M_NT, M_H, M_OUT = M_BACK + 1, M_BACK + 2, M_BACK + 3, M_BACK + 7
        NEG0 = cfg.s_uses
        ST0 = NEG0 + QT

        def read_out(stage, n):
            if stage == A0:
                return [(x_full_ready, X_PARTS, X_PARTS), (q_full_ready, DC, DC),
                        (k_full_ready, DC, DC), (va_ready, 1, 1)][n]
            if stage == O0:
                return o_t_ready, G, n + 1
            if stage == R0:
                if n < NEG0:
                    return (s_masked if cfg.mask == "add" else peak_done), cfg.s_uses, n + 1
                if n < ST0:
                    return peak_t_ready, QT, n - NEG0 + 1
                if cfg.mask == "add":
                    return st_masked, G, n - ST0 + 1
                return exp_done, EXPS, n - ST0 + 1
            if n < M_BACK:
                return o_tok_ready, cfg.ot_uses, n + 1
            if n == M_BACK:
                return o_full_ready, DC, DC
            if n == M_PROJ:
                return att_ready, 1, 1
            if n == M_NT:
                return y_full_ready, DC, DC
            if n < M_OUT:
                return h_full_ready, FC, 2 * (n - M_H + 1)
            return x_new, 1, 1

        def slot(stage, n):
            return stage + n % 2

        def tile(stage, n):
            return banks[slot(stage, n)]

        def wait_free(eng, s, stage, n):
            if n >= 2:
                which, per, count = read_out(stage, n - 2)
                eng.wait_ge(which, s.count(per, count))
            else:
                which, per, count = read_out(stage, n - 2 + USES[stage])
                if s.index() != 0 if isinstance(s.j, int) else True:
                    eng.wait_ge(which, s.before(1).count(per, count))

        def wait_full(eng, s, stage, n):
            eng.wait_ge(bank_full[slot(stage, n)], s.count(USES[stage] // 2, n // 2 + 1))

        m_steps = [("ot", n) for n in range(cfg.ot_uses)] + [("back", 0), ("proj", 0), ("norm", 0)]
        if cfg.mlp:
            m_steps += [("norm_t", 0)] + [("mlp1", n) for n in range(4)] + [("mlp2", 0)]

        def order(with_s, with_m):
            ss = [("s", n) for n in range(cfg.s_uses)] if with_s else []
            ms = m_steps if with_m else []
            merged, done = [], 0
            for i, m in enumerate(ms):
                upto = (i + 1) * len(ss) // (len(ms) + 1)
                merged += ss[done:upto] + [m]
                done = upto
            return merged + ss[done:]

        def run(eng, stage_s_m, stage_max, stage_in, stage_out, early=None):
            def turn(i, first=False, last=False):
                after = Seq(i.j, i.k + 1)
                if early and not last:
                    early(after)
                stage_s_m(i, i.before(1), True, not first)
                stage_max(i)
                if not last:
                    stage_in(after)
                stage_out(i)
            if early:
                early(Seq(0, 0))
            stage_in(Seq(0, 0))
            turn(Seq(0, 0), first=True)
            with eng.Fori(0, (B - 2) // 2) as j:
                turn(Seq(j, 1))
                turn(Seq(j, 2))
            turn(Seq(0, B - 1), last=True)
            stage_s_m(None, Seq(0, B - 1), False, True)

        def nothing(*_):
            pass

        block = lay.enter_context(nc.Block())

        @block.tensor
        def _(pe):
            def mm3(dst, a, b, first, last):
                pe.matmul(dst, a[0], b[0], start=first, stop=False)
                pe.matmul(dst, a[0], b[1], start=False, stop=False)
                return pe.matmul(dst, a[1], b[0], start=False, stop=last)

            def feature_major(bank, name, c0, act):
                for i in range(2):
                    for k in range(DC):
                        c = c0 + i * P
                        last = mm3(bank[:, i * S:(i + 1) * S],
                                   (wgt(w_hi, name, k, c, P), wgt(w_lo, name, k, c, P)),
                                   (act[0][:, k, :], act[1][:, k, :]), k == 0, k == DC - 1)
                return last

            def token_major(bank, name, act, chunks=DC):
                for t in range(QT):
                    for k in range(chunks):
                        last = mm3(bank[:, t * D:(t + 1) * D],
                                   (act[0][:, k, t * P:(t + 1) * P], act[1][:, k, t * P:(t + 1) * P]),
                                   (wgt(w_hi, name, k), wgt(w_lo, name, k)), k == 0, k == chunks - 1)
                return last

            def turn_to_features(bank, src):
                for t in range(QT):
                    for c in range(DC):
                        last = pe.transpose(bank[:, c * S + t * P:c * S + (t + 1) * P],
                                            src[:, t, c * P:(c + 1) * P], ident[:, :])
                return last

            def stage_in(s):
                if cfg.pre_norm:
                    pe.wait_ge(xn_ready, s.count(1, 1))
                else:
                    pe.wait_ge(xc_ready, s.count(1, 1))
                wait_free(pe, s, A0, 0)
                turn_to_features(tile(A0, 0), xn if cfg.pre_norm else xc).then_inc(bank_full[slot(A0, 0)], 1)
                wait_free(pe, s, A0, 1)
                pe.wait_ge(x_hi_ready, s.count(1, 1))
                pe.wait_ge(x_lo_ready, s.count(1, 1))
                feature_major(tile(A0, 1), "q", 0, x_t).then_inc(bank_full[slot(A0, 1)], 1)
                if cfg.latent:
                    wait_free(pe, s, A0, 2)
                    feature_major(tile(A0, 2), "k", 0, x_t).then_inc(bank_full[slot(A0, 2)], 1)
                    wait_free(pe, s, A0, 3)
                    token_major(tile(A0, 3), "v", x_t).then_inc(bank_full[slot(A0, 3)], 1)

            def scores(s, n):
                if n == 0:
                    pe.wait_ge(stack_loaded[s.par], s.count_par(STACK, STACK))
                wait_free(pe, s, R0, n)
                per_tile = H // cfg.spu
                t, h0 = n // per_tile, n % per_tile * cfg.spu
                for i in range(cfg.spu):
                    last = pe.matmul(tile(R0, n)[:, i * cfg.keys:(i + 1) * cfg.keys],
                                     stack_q[s.par][0:KS, h0 + i, t * P:(t + 1) * P],
                                     stack_k[s.par][0:KS, (h0 + i) * KV // H, :], start=True, stop=True)
                last.then_inc(bank_full[slot(R0, n)], 1)

            def m_step(s, kind, n):
                if kind == "ot":
                    pe.wait_ge(o_t_ready, s.count(G, 2 * n + 2))
                    wait_free(pe, s, M0, n)
                    for g in range(2):
                        for t in range(QT):
                            last = pe.transpose(tile(M0, n)[:, (g * QT + t) * P:(g * QT + t + 1) * P],
                                                o_t[:, 2 * n + g, t * P:(t + 1) * P], ident[:, :])
                    last.then_inc(bank_full[slot(M0, n)], 1)
                elif kind == "back":
                    wait_free(pe, s, M0, M_BACK)
                    pe.wait_ge(o_tok_ready, s.count(cfg.ot_uses, cfg.ot_uses))
                    turn_to_features(tile(M0, M_BACK), o_tok).then_inc(bank_full[slot(M0, M_BACK)], 1)
                elif kind == "proj":
                    wait_free(pe, s, M0, M_PROJ)
                    pe.wait_ge(o_hi_ready, s.count(1, 1))
                    pe.wait_ge(o_lo_ready, s.count(1, 1))
                    token_major(tile(M0, M_PROJ), "o", o_f).then_inc(bank_full[slot(M0, M_PROJ)], 1)
                elif kind == "norm_t":
                    wait_free(pe, s, M0, M_NT)
                    pe.wait_ge(y_ready, s.count(1, 1))
                    turn_to_features(tile(M0, M_NT), y).then_inc(bank_full[slot(M0, M_NT)], 1)
                elif kind == "mlp1":
                    wait_free(pe, s, M0, M_H + n)
                    if n == 0:
                        pe.wait_ge(y_hi_ready, s.count(1, 1))
                        pe.wait_ge(y_lo_ready, s.count(1, 1))
                    feature_major(tile(M0, M_H + n), "w1", 2 * n * P, y_t)\
                        .then_inc(bank_full[slot(M0, M_H + n)], 1)
                elif kind == "mlp2":
                    wait_free(pe, s, M0, M_OUT)
                    pe.wait_ge(h_hi_ready, s.count(4, 4))
                    pe.wait_ge(h_lo_ready, s.count(4, 4))
                    token_major(tile(M0, M_OUT), "w2", h_t, FC).then_inc(bank_full[slot(M0, M_OUT)], 1)

            def stage_s_m(s, prev, with_s, with_m):
                for kind, n in order(with_s, with_m):
                    if kind == "s":
                        scores(s, n)
                    else:
                        m_step(prev, kind, n)

            def stage_max(s):
                for t in range(QT):
                    wait_free(pe, s, R0, NEG0 + t)
                    pe.wait_ge(neg_done, s.count(QT, t + 1))
                    for a in range(2):
                        last = pe.transpose(tile(R0, NEG0 + t)[:, :].bitcast(BF16)[0:H, a * P:(a + 1) * P],
                                            neg_peak[:, t, a, :], ident16[:, :])
                    last.then_inc(bank_full[slot(R0, NEG0 + t)], 1)

            def stage_out(s):
                pe.wait_ge(max_loaded[s.par], s.count_par(32, 32))

                def keys_of(h, c0, n):
                    return stack_k[s.par][0:KST, h * KV // H, c0:c0 + n]

                def transposed_scores(g):
                    n = ST0 + cfg.st_group * g
                    wait_free(pe, s, R0, n)
                    for i in range(4):
                        half = i % 2 * SC
                        last = pe.matmul(tile(R0, n)[half:half + SC, i // 2 * S:(i // 2 + 1) * S],
                                         keys_of(4 * g + i, cfg.c0, SC), stack_q[s.par][0:KST, 4 * g + i, :],
                                         start=True, stop=True)
                    last.then_inc(bank_full[slot(R0, n)], 1)
                    if cfg.latent:
                        for i in range(4):
                            n += 1
                            wait_free(pe, s, R0, n)
                            for t in range(QT):
                                last = pe.matmul(tile(R0, n)[:, t * S:(t + 1) * S], keys_of(4 * g + i, t * P, P),
                                                 stack_q[s.par][0:KST, 4 * g + i, :], start=True, stop=True)
                            last.then_inc(bank_full[slot(R0, n)], 1)

                def values(g):
                    wait_free(pe, s, O0, g)
                    pe.wait_ge(exp_done, s.count(EXPS, cfg.st_group * (g + 1)))
                    if g == 0:
                        pe.wait_ge(va_ctx_ready, s.count(2, 2))
                        if cfg.latent:
                            pe.wait_ge(va_ready, s.count(1, 1))
                    parts = (QT if cfg.latent else 0) + 1
                    for t in range(parts):
                        for i in range(4):
                            h = 4 * g + i
                            if t == parts - 1:
                                a, b = va_ctx[s.par][:, h, :], p_ctx[:, g % 2, i // 2, :]
                            else:
                                a, b = va[s.par][:, t, h, :], p_lat[:, h % 6, t, :]
                            last = pe.matmul(tile(O0, g)[VW * i:VW * (i + 1), 0:S], a, b,
                                             start=(t == 0), stop=(t == parts - 1), tile_position=(0, VW * i))
                    last.then_inc(bank_full[slot(O0, g)], 1)

                for g in range(G):
                    transposed_scores(g)
                    if g:
                        values(g - 1)
                values(G - 1)

            pe.wait_ge(ones_ready, 1)
            run(pe, stage_s_m, stage_max, stage_in, stage_out)

        @block.scalar
        def _(act):
            def column(name, c):
                return col[:, COLS[name] + c:COLS[name] + c + 1]

            def early(s):
                if s.index() != 0 if isinstance(s.j, int) else True:
                    b = s.before(1)
                    wait_full(act, b, A0, 0)
                    act.wait_ge(xb_ready, b.count(QT, QT))
                    if cfg.pre_norm:
                        act.wait_ge(xn_ready, b.count(1, 1))
                src = x_all[:, QT * s.index():QT * s.index() + QT, :] if isinstance(s.j, int) else \
                    x_all[:, bass.ds(s.index() * QT, QT), :]
                act.activation(xc[:, :, :], src, ACT.Copy).then_inc(xc_ready, 1)

            def stage_in(s):
                act.wait_ge(x_lo_ready, s.count(1))
                wait_full(act, s, A0, 0)
                if cfg.pre_norm:
                    for c in range(DC):
                        act.activation(x_full[:, c, :], tile(A0, 0)[:, c * S:(c + 1) * S], ACT.Identity,
                                       scale=column("p_w", c), bias=column("p_b", c)).then_inc(x_full_ready, 1)
                else:
                    act.activation(x_full[:, :, :].rearrange("p c s -> p (c s)"), tile(A0, 0)[:, :], ACT.Copy)\
                        .then_inc(x_full_ready, 1)
                act.wait_ge(q_r, s.count(1))
                wait_full(act, s, A0, 1)
                for c in range(DC):
                    act.activation(q_full[:, c, :], tile(A0, 1)[:, c * S:(c + 1) * S], ACT.Identity,
                                   scale=cfg.scale, bias=bq_scaled[:, c:c + 1]).then_inc(q_full_ready, 1)
                if cfg.latent:
                    wait_full(act, s, A0, 2)
                    for c in range(DC):
                        act.activation(k_full[:, c, :], tile(A0, 2)[:, c * S:(c + 1) * S], ACT.Identity,
                                       bias=column("bk", c)).then_inc(k_full_ready, 1)
                    act.wait_ge(k_full_ready, s.count(DC, DC))
                    act.wait_ge(k_written, s.count(16))
                    act.activation(k_term[:, 0, :, :], k_full[:, :, :], ACT.Copy).then_inc(k_h, 1)
                    act.wait_ge(k_r, s.count(1, 1))
                    act.activation(k_term[:, 1, :, :], k_rest[:, :, :], ACT.Copy).then_inc(k_m, 1)
                if not isinstance(s.j, int) or s.k >= 2:
                    wait_full(act, s.before(2), O0, G - 1)
                rep = H // KV
                for half in range(2):
                    rows_ = slice(half * SC, (half + 1) * SC)
                    if isinstance(s.j, int):
                        src = v_ctx[rows_, s.index(), :]
                    else:
                        src = v_ctx[rows_, bass.ds(s.index(), 1), :].rearrange("p a c -> p (a c)")
                    if rep == 1:
                        src = src.rearrange("p (h d) -> p h d", d=DH)[:, half::2, :]
                        dst = va_ctx[s.par][rows_, half::2, 0:DH]
                    else:
                        src = src.rearrange("p (k d) -> p k d", d=DH).unsqueeze(2)\
                            .to_broadcast([SC, KV, rep // 2, DH])
                        dst = va_ctx[s.par][rows_, :, :].rearrange("p (k r) v -> p k r v", r=rep)[:, :, half::2, 0:DH]
                    act.activation(dst, src, ACT.Copy).then_inc(va_ctx_ready, 1)

            def stage_s_m(s, prev, with_s, with_m):
                for kind, n in order(False, with_m):
                    if kind == "back":
                        act.wait_ge(o_lo_ready, prev.count(1))
                        if cfg.mlp:
                            act.wait_ge(y_lo_ready, prev.count(1))
                        wait_full(act, prev, M0, M_BACK)
                        for c in range(DC):
                            act.activation(o_full[:, c, :], tile(M0, M_BACK)[:, c * S:(c + 1) * S],
                                           ACT.Identity, bias=column("bv", c)).then_inc(o_full_ready, 1)
                    elif kind == "norm_t":
                        act.wait_ge(o_lo_ready, prev.count(1, 1))
                        wait_full(act, prev, M0, M_NT)
                        for c in range(DC):
                            act.activation(y_full[:, c, :], tile(M0, M_NT)[:, c * S:(c + 1) * S],
                                           ACT.Identity, scale=column("n_w", c), bias=column("n_b", c))\
                                .then_inc(y_full_ready, 1)
                    elif kind == "mlp1":
                        act.wait_ge(h_lo_ready, prev.count(4, n - 1))
                        wait_full(act, prev, M0, M_H + n)
                        for i in range(2):
                            act.activation(h_full[:, n % 2, i, :], tile(M0, M_H + n)[:, i * S:(i + 1) * S],
                                           ACT.Gelu_apprx_tanh, bias=column("b1", 2 * n + i))\
                                .then_inc(h_full_ready, 1)

            def stage_out(s):
                for g in range(G):
                    n = ST0 + cfg.st_group * g
                    act.wait_ge(bank_full[slot(O0, g)], s.count(USES[O0] // 2, g // 2))
                    if cfg.mask == "add":
                        act.wait_ge(st_masked, s.count(G, g + 1))
                        src = st_tmp[:, g % 2, :, :].rearrange("p a s -> p (a s)")
                    else:
                        wait_full(act, s, R0, n)
                        src = tile(R0, n)[:, :]
                    act.activation(p_ctx[:, g % 2, :, :].rearrange("p a s -> p (a s)"), src, ACT.Exp)\
                        .then_inc(exp_done, 1)
                    if cfg.latent:
                        for i in range(4):
                            n += 1
                            h = 4 * g + i
                            if h >= 6:
                                wait_full(act, s, O0, (h - 6) // 4)
                            elif h == 0:
                                act.wait_ge(bank_full[slot(O0, G - 1)], s.count(USES[O0] // 2))
                            wait_full(act, s, R0, n)
                            act.activation(p_lat[:, h % 6, :, :].rearrange("p a s -> p (a s)"),
                                           tile(R0, n)[:, :], ACT.Exp).then_inc(exp_done, 1)

            run(act, stage_s_m, nothing, stage_in, stage_out, early)

        @block.vector
        def _(dve):
            def norm(s, src, dst, stepped, done):
                at = [0]

                def step(ins):
                    at[0] += 1
                    ins.then_inc(stepped, 1)
                    dve.wait_ge(stepped, s.count(NORM, at[0]))

                for t in range(QT):
                    ins = dve.bn_stats(st6[:, t, :], src[:, t, :])
                step(ins)
                at[0] += 1
                dve.sem_inc(stepped, 1)
                for t in range(QT):
                    ins = dve.bn_aggr(mv[:, t, :], st6[:, t, :])
                step(ins)
                mean, var = mv[:, :, 0], mv[:, :, 1]
                v, r, a, sq = nw[:, 0, :], nw[:, 1, :], nw[:, 2, :], nw[:, 3, :]
                if cfg.norm == "rms":
                    step(dve.tensor_tensor(sq, mean, mean, ALU.mult))
                    step(dve.scalar_tensor_tensor(out=v, in0=sq, scalar=cfg.eps, in1=var,
                                                  op0=ALU.add, op1=ALU.add))
                else:
                    step(dve.tensor_scalar(v, var, cfg.eps, None, ALU.add))
                step(dve.tensor_scalar(r.bitcast(I32), v.bitcast(I32), -0.5, MAGIC, ALU.mult, ALU.add))
                for _ in range(3):
                    step(dve.scalar_tensor_tensor(out=a, in0=r, scalar=-0.5, in1=v, op0=ALU.mult, op1=ALU.mult))
                    step(dve.tensor_tensor(sq, a, r, ALU.mult))
                    step(dve.scalar_tensor_tensor(out=r, in0=sq, scalar=1.5, in1=r, op0=ALU.add, op1=ALU.mult))
                assert at[0] == NORM
                for t in range(QT):
                    rt = nw[:, 1, t:t + 1]
                    if cfg.norm == "rms":
                        ins = dve.tensor_scalar(dst[:, t, :], src[:, t, :], rt, None, ALU.mult)
                    else:
                        ins = dve.tensor_scalar(dst[:, t, :], src[:, t, :], mv[:, t, 0:1], rt,
                                                ALU.subtract, ALU.mult)
                ins.then_inc(done, 1)

            def stage_in(s):
                if cfg.pre_norm:
                    dve.wait_ge(xc_ready, s.count(1, 1))
                    norm(s, xc, xn, pre_step, xn_ready)
                dve.wait_ge(x_full_ready, s.count(X_PARTS, X_PARTS))
                dve.tensor_copy(x_t[0][:, :, :], x_full[:, :, :]).then_inc(x_hi_ready, 1)
                dve.wait_ge(q_full_ready, s.count(DC, DC))
                dve.wait_ge(q_written, s.count(16))
                dve.tensor_copy(q_term[:, 0, :, :], q_full[:, :, :]).then_inc(q_h, 1)
                dve.wait_ge(q_h, s.count(1, 1))
                dve.tensor_tensor(q_rest[:, :, :], q_full[:, :, :], q_term[:, 0, :, :], ALU.subtract)\
                    .then_inc(q_r, 1)
                dve.wait_ge(q_r, s.count(1, 1))
                dve.tensor_copy(q_term[:, 1, :, :], q_rest[:, :, :]).then_inc(q_m, 1)
                dve.wait_ge(q_m, s.count(1, 1))
                dve.tensor_tensor(q_term[:, 2, :, :], q_rest[:, :, :], q_term[:, 1, :, :], ALU.subtract)\
                    .then_inc(q_l, 1)
                if cfg.latent:
                    wait_full(dve, s, A0, 3)
                    if not isinstance(s.j, int) or s.k >= 2:
                        wait_full(dve, s.before(2), O0, G - 1)
                    dve.tensor_copy(va[s.par][:, :, :, 0:DH],
                                    tile(A0, 3)[:, :].rearrange("p (t h d) -> p t h d", t=QT, h=H))\
                        .then_inc(va_ready, 1)

            def maximum(s, n):
                per_tile = H // cfg.spu
                t, h0 = n // per_tile, n % per_tile * cfg.spu
                wait_full(dve, s, R0, n)
                if cfg.mask == "add":
                    if n == 0:
                        dve.wait_ge(masks_loaded[s.par], s.count_par(48, 48))
                    scored = tile(R0, n)[:, :].rearrange("p (h k) -> p h k", k=SC)
                    m = mq[s.par][:, t, :].unsqueeze(1).to_broadcast([P, 8, SC])
                    dve.tensor_tensor(s_tmp[:, n % 2, :, :], scored, m, ALU.add).then_inc(s_masked, 1)
                    dve.wait_ge(s_masked, s.count(cfg.s_uses, n + 1))
                    src = s_tmp[:, n % 2, :, :]
                elif cfg.spu > 1:
                    src = tile(R0, n)[:, :].rearrange("p (h k) -> p h k", k=SC)
                else:
                    src = tile(R0, n)[:, 0:cfg.keys]
                dve.tensor_reduce(peak[:, t, h0:h0 + cfg.spu], src, AX.X, ALU.max).then_inc(peak_done, 1)

            def m_step(s, kind, n):
                if kind == "ot":
                    wait_full(dve, s, M0, n)
                    o = tile(M0, n)[:, :].rearrange("p (g t h v) -> p g t h v", g=2, t=QT, v=VW)
                    for g in range(2):
                        ins = dve.reciprocal(o_rec[:, n % 2, g, :, :], o[:, g, :, :, ONES])
                    ins.then_inc(rec_ready, 1)
                    dve.wait_ge(rec_ready, s.count(cfg.ot_uses, n + 1))
                    for g in range(2):
                        h0 = 4 * (2 * n + g) * DH
                        ins = dve.tensor_tensor(
                            o_tok[:, :, h0:h0 + 4 * DH].rearrange("p t (h d) -> p t h d", h=4),
                            o[:, g, :, :, 0:DH],
                            o_rec[:, n % 2, g, :, :].unsqueeze(3).to_broadcast([P, QT, 4, DH]), ALU.mult)
                    ins.then_inc(o_tok_ready, 1)
                elif kind == "back":
                    dve.wait_ge(o_full_ready, s.count(DC, DC))
                    dve.tensor_copy(o_f[0][:, :, :], o_full[:, :, :]).then_inc(o_hi_ready, 1)
                elif kind == "proj":
                    wait_full(dve, s, M0, M_PROJ)
                    dve.wait_ge(xb_ready, s.count(QT, QT))
                    if cfg.n == 3:
                        dve.wait_ge(xb2_ready, s.count(QT))
                    dve.tensor_tensor(att[:, :, :], tile(M0, M_PROJ)[:, :].rearrange("p (t d) -> p t d", t=QT),
                                      xb[s.par][:, :, :], ALU.add).then_inc(att_ready, 1)
                elif kind == "norm":
                    dve.wait_ge(att_ready, s.count(1, 1))
                    norm(s, att, y, norm_step, y_ready)
                    if not cfg.mlp:
                        dve.wait_ge(y_ready, s.count(1, 1))
                        for t in range(QT):
                            ins = dve.tensor_tensor(att[:, t, :], y[:, t, :], row[:, ROWV["g"], :], ALU.mult)
                        ins.then_inc(g_ready, 1)
                        dve.wait_ge(g_ready, s.count(1, 1))
                        for t in range(QT):
                            at = x_all[:, QT * s.index() + t, :] if isinstance(s.j, int) else \
                                x_all[:, bass.ds(s.index() * QT + t, 1), :].rearrange("p a d -> p (a d)")
                            ins = dve.tensor_tensor(at, att[:, t, :], row[:, ROWV["b"], :], ALU.add)
                        ins.then_inc(x_new, 1)
                elif kind == "norm_t":
                    dve.wait_ge(y_full_ready, s.count(DC, DC))
                    dve.tensor_copy(y_t[0][:, :, :], y_full[:, :, :]).then_inc(y_hi_ready, 1)
                elif kind == "mlp1":
                    dve.wait_ge(h_full_ready, s.count(FC, 2 * n + 2))
                    dve.tensor_copy(h_t[0][:, 2 * n:2 * n + 2, :], h_full[:, n % 2, :, :]).then_inc(h_hi_ready, 1)
                elif kind == "mlp2":
                    wait_full(dve, s, M0, M_OUT)
                    dve.wait_ge(xb2_ready, s.count(QT, QT))
                    if cfg.n == 3:
                        dve.wait_ge(stored[s.par], s.count_par(16))
                        at = y_out[s.par][:, :, :]
                    else:
                        at = x_all[:, QT * s.index():QT * s.index() + QT, :] if isinstance(s.j, int) else \
                            x_all[:, bass.ds(s.index() * QT, QT), :]
                    dve.tensor_tensor(at, tile(M0, M_OUT)[:, :].rearrange("p (t d) -> p t d", t=QT),
                                      xb2[:, :, :], ALU.add).then_inc(x_new, 1)

            def stage_s_m(s, prev, with_s, with_m):
                for kind, n in order(with_s, with_m):
                    if kind == "s":
                        maximum(s, n)
                    else:
                        m_step(prev, kind, n)

            def stage_max(s):
                dve.wait_ge(peak_done, s.count(cfg.s_uses, cfg.s_uses))
                for t in range(QT):
                    dve.tensor_scalar(neg_peak[:, t, 0, :], peak[:, t, :], -1.0, None, ALU.mult).then_inc(neg_h, 1)
                dve.wait_ge(neg_h, s.count(QT, QT))
                for t in range(QT):
                    dve.scalar_tensor_tensor(out=neg_peak[:, t, 1, :], in0=peak[:, t, :], scalar=-1.0,
                                             in1=neg_peak[:, t, 0, :], op0=ALU.mult, op1=ALU.subtract)\
                        .then_inc(neg_done, 1)
                b = s.before(1)
                if not isinstance(s.j, int) or s.k >= 1:
                    dve.wait_ge(max_loaded[b.par], b.count_par(32, 32))
                for t in range(QT):
                    wait_full(dve, s, R0, NEG0 + t)
                    dve.tensor_copy(peak_t[:, :, t, :], tile(R0, NEG0 + t)[:, :].bitcast(BF16)[0:H, 0:2 * P]
                                    .rearrange("h (a q) -> h a q", a=2))\
                        .then_inc(peak_t_ready, 1)

            def stage_out(s):
                def mask_transposed(g):
                    wait_full(dve, s, R0, ST0 + g)
                    dve.wait_ge(exp_done, s.count(EXPS, g - 1))
                    dve.tensor_tensor(st_tmp[:, g % 2, :, :],
                                      tile(R0, ST0 + g)[:, :].rearrange("p (a s) -> p a s", a=2),
                                      mk[s.par][:, :].unsqueeze(1).to_broadcast([P, 2, S]), ALU.add)\
                        .then_inc(st_masked, 1)

                def output(g):
                    wait_full(dve, s, O0, g)
                    dve.tensor_copy(o_t[:, g, :], tile(O0, g)[:, 0:S]).then_inc(o_t_ready, 1)

                for g in range(G):
                    if cfg.mask == "add":
                        mask_transposed(g)
                    if g >= 2:
                        output(g - 2)
                for g in range(G - 2, G):
                    output(g)

            run(dve, stage_s_m, stage_max, stage_in, stage_out)

        @block.gpsimd
        def _(pool):
            if cfg.latent:
                for i in range(2):
                    ins = pool.memset(va[i][:, :, :, DH:VW], 1.0)
                ins.then_inc(ones_ready, 1)
            else:
                pool.sem_inc(ones_ready, 1)

            def stage_in(s):
                pool.wait_ge(xc_ready, s.count(1, 1))
                if not isinstance(s.j, int) or s.k >= 2:
                    pool.wait_ge(att_ready, s.before(2).count(1, 1))
                for t in range(QT):
                    pool.tensor_tensor(xb[s.par][:, t, :], xc[:, t, :], row[:, ROWV["bo"], :], ALU.add)\
                        .then_inc(xb_ready, 1)
                pool.wait_ge(x_hi_ready, s.count(1, 1))
                pool.tensor_tensor(x_t[1][:, :, :], x_full[:, :, :], x_t[0][:, :, :].bitcast(F32), ALU.subtract)\
                    .then_inc(x_lo_ready, 1)
                if cfg.latent:
                    pool.wait_ge(k_h, s.count(1, 1))
                    pool.tensor_tensor(k_rest[:, :, :], k_full[:, :, :], k_term[:, 0, :, :], ALU.subtract)\
                        .then_inc(k_r, 1)
                    pool.wait_ge(k_m, s.count(1, 1))
                    pool.tensor_tensor(k_term[:, 2, :, :], k_rest[:, :, :], k_term[:, 1, :, :], ALU.subtract)\
                        .then_inc(k_l, 1)

            def stage_s_m(s, prev, with_s, with_m):
                for kind, n in order(False, with_m):
                    if kind == "back":
                        pool.wait_ge(o_hi_ready, prev.count(1, 1))
                        pool.tensor_tensor(o_f[1][:, :, :], o_full[:, :, :], o_f[0][:, :, :].bitcast(F32),
                                           ALU.subtract).then_inc(o_lo_ready, 1)
                    elif kind == "norm" and cfg.mlp:
                        pool.wait_ge(x_new, prev.count(1))
                        if cfg.n == 3:
                            pool.wait_ge(att_ready, prev.count(1, 1))
                        for t in range(QT):
                            if cfg.n == 3:
                                residual = att[:, t, :]
                            elif isinstance(prev.j, int):
                                residual = x_all[:, QT * prev.index() + t, :]
                            else:
                                residual = x_all[:, bass.ds(prev.index() * QT + t, 1), :]\
                                    .rearrange("p a d -> p (a d)")
                            pool.tensor_tensor(xb2[:, t, :], residual, row[:, ROWV["b2"], :], ALU.add)\
                                .then_inc(xb2_ready, 1)
                    elif kind == "norm_t":
                        pool.wait_ge(y_hi_ready, prev.count(1, 1))
                        pool.tensor_tensor(y_t[1][:, :, :], y_full[:, :, :], y_t[0][:, :, :].bitcast(F32),
                                           ALU.subtract).then_inc(y_lo_ready, 1)
                    elif kind == "mlp1":
                        pool.wait_ge(h_hi_ready, prev.count(4, n + 1))
                        pool.tensor_tensor(h_t[1][:, 2 * n:2 * n + 2, :], h_full[:, n % 2, :, :],
                                           h_t[0][:, 2 * n:2 * n + 2, :].bitcast(F32), ALU.subtract)\
                            .then_inc(h_lo_ready, 1)

            run(pool, stage_s_m, nothing, stage_in, nothing)

        @block.sync
        def _(sp):
            def of(dram, s):
                return dram[s.index()] if isinstance(s.j, int) else \
                    dram[bass.ds(s.index(), 1)].rearrange("a ... -> (a ...)") if False else \
                    squeeze(dram[bass.ds(s.index(), 1)])

            def squeeze(ap):
                names = "bcde"[:len(ap.shape) - 1]
                first = names[0]
                return ap.rearrange(f"a {' '.join(names)} -> (a {first}) {' '.join(names[1:])}")

            def stage_in(s):
                sp.wait_ge(q_l, s.count(1, 1))
                sp.dma_start(of(q_dram, s).rearrange("t (c p) s -> p t c s", p=P), q_term[:, :, :, :])\
                    .then_inc(q_written, 16)
                if cfg.latent:
                    sp.wait_ge(k_l, s.count(1, 1))
                    sp.dma_start(of(k_dram, s)[:, :, 0:S].rearrange("t (c p) s -> p t c s", p=P),
                                 k_term[:, :, :, :]).then_inc(k_written, 16)
                if not isinstance(s.j, int) or s.k >= 2:
                    wait_full(sp, s.before(2), O0, G - 1)
                loaded = stack_loaded[s.par]
                if cfg.mask == "add":
                    sp.dma_start(mq[s.par][:, :, :], of(mask_q, s).rearrange("(t p) k -> p t k", p=P))\
                        .then_inc(masks_loaded[s.par], 16)
                    for half in range(2):
                        sp.dma_start(mk[s.par][half * SC:(half + 1) * SC, :], of(mask_k, s))\
                            .then_inc(masks_loaded[s.par], 16)
                else:
                    sp.dma_start(stack_k[s.par][MASK_ROW:MASK_ROW + 1, :, cfg.c0:cfg.c0 + SC],
                                 mask_dram[s.index():s.index() + 1, :].unsqueeze(1).to_broadcast([1, KV, SC])
                                 if isinstance(s.j, int) else
                                 mask_dram[bass.ds(s.index(), 1), :].unsqueeze(1).to_broadcast([1, KV, SC]))\
                        .then_inc(loaded, 16)
                sp.wait_ge(q_written, s.count(16, 16))
                for i, term in enumerate(Q_TERMS):
                    sp.dma_start(stack_q[s.par][ROWS * i:ROWS * i + DH, :, :],
                                 of(q_dram, s)[term].rearrange("(h d) s -> d h s", d=DH)).then_inc(loaded, 16)
                if cfg.latent:
                    sp.wait_ge(k_written, s.count(16, 16))
                for i, term in enumerate(K_TERMS):
                    sp.dma_start(stack_k[s.par][ROWS * i:ROWS * i + DH, :, :],
                                 of(k_dram, s)[term].rearrange("(h d) s -> d h s", d=DH)).then_inc(loaded, 16)

            def stage_max(s):
                sp.wait_ge(peak_t_ready, s.count(QT, QT))
                for a in range(2):
                    sp.dma_start(stack_q[s.par][MAX_ROW + a:MAX_ROW + a + 1, :, :],
                                 peak_t[:, a, :, :].rearrange("h t q -> h (t q)"))\
                        .then_inc(max_loaded[s.par], 16)

            def stage_s_m(s, prev, with_s, with_m):
                if with_m and cfg.n == 3:
                    sp.wait_ge(x_new, prev.count(1, 1))
                    sp.dma_start(of(out, prev).rearrange("(t p) d -> p t d", p=P), y_out[prev.par][:, :, :])\
                        .then_inc(stored[prev.par], 16)

            run(sp, stage_s_m, stage_max, stage_in, nothing)
            if cfg.n == 3:
                for i in range(2):
                    sp.wait_ge(stored[i], 16 * (B // 2 + 1))
    clear(nc, taken)


def clear(nc, taken):
    with nc.Block() as block:
        @block.sync
        def _(sp):
            for s in taken:
                sp.sem_clear(s)


def prepare(nc, cfg, banks, x_all, ident, ident16, x, ctx_t, w_in, cols_in, rows_in, mask_i, mask_b,
            w_hi, w_lo, col, row, bq_scaled, stack_q, stack_k, v_ctx, va_ctx, k_dram, mask_dram, wgt, rise):
    L = f"L{cfg.n}p_"
    KW = min(P, cfg.kvw)
    KC = cfg.kvw // KW
    with ExitStack() as pre:
        def sb(name, shape, dt=F32):
            return pre.enter_context(nc.sbuf_tensor(L + name, shape, dt))

        taken = []

        def sem(name):
            s = pre.enter_context(nc.semaphore(L + name))
            taken.append(s)
            return s

        raw = sb("raw", [P, cfg.wcols])
        ctx = sb("ctx", [P, DC, B, 2, SC])
        c_t = [sb(f"c_t_{p}", [P, DC, B, 2, SC], F32R) for p in ("hi", "lo")]
        k_full = sb("k_full", [P, KC, B * SC])
        k_rest = sb("k_rest", [P, KC, B * SC])
        k_term = sb("k_term", [P, NTERM, KC, B * SC], BF16)
        m_raw = sb("m_raw", [B, SC], I32 if cfg.mask == "int" else U8)
        m_f = sb("m_f", [B, SC])
        m_z = sb("m_z", [B, SC])
        m_row = sb("m_row", [B, SC], BF16)

        w_loaded, ctx_loaded, small_loaded, mask_loaded, x_loaded = (
            sem(n) for n in ("w_loaded", "ctx_loaded", "small_loaded", "mask_loaded", "x_loaded"))
        w_ready, ctx_ready, ident_zero, ident_ready, fill, fill_k = (
            sem(n) for n in ("w_ready", "ctx_ready", "ident_zero", "ident_ready", "fill", "fill_k"))
        k_done, v_done, k_full_ready, k_part, m_part, written, bq_done, v_read = (
            sem(n) for n in ("k_done", "v_done", "k_full_ready", "k_part", "m_part", "written", "bq_done", "v_read"))
        block = pre.enter_context(nc.Block())

        @block.sync
        def _(sp):
            sp.dma_start(ctx[:, :, :, :, :].rearrange("p c b a s -> p (c b a s)"), ctx_t).then_inc(ctx_loaded, 16)
            sp.dma_start(raw[:, :], w_in).then_inc(w_loaded, 16)
            sp.dma_start(col[:, :], cols_in).then_inc(small_loaded, 16)
            sp.dma_start(row[:, :, :].rearrange("p a d -> p (a d)"),
                         rows_in.rearrange("(o a) d -> o (a d)", o=1).to_broadcast([P, cfg.rowvs * D])).then_inc(small_loaded, 16)
            if cfg.mask != "add":
                sp.dma_start(m_raw[:, :], mask_i if cfg.mask == "int" else mask_b).then_inc(mask_loaded, 16)
            if cfg.n == 0:
                sp.dma_start(x_all[:, :, :], x.rearrange("b (t p) d -> p (b t) d", p=P)).then_inc(x_loaded, 16)
            for s, per in rise.values():
                sp.sem_inc(s, per)
            if cfg.mask != "add":
                sp.wait_ge(m_part, 3)
                sp.dma_start(mask_dram, m_row[:, :]).then_inc(written, 16)
            sp.wait_ge(k_part, 4)
            n = 0
            for t in range(NTERM):
                for c in range(KC):
                    dst = k_dram[:, t, c * KW:(c + 1) * KW, cfg.c0:cfg.c0 + SC].rearrange("b p s -> p b s")
                    sp.dma_start(dst, k_term[0:KW, t, c, :].rearrange("p (b s) -> p b s", b=B)).then_inc(written, 16)
                    n += 1
            sp.wait_ge(written, 16 * (n + (cfg.mask != "add")))
            sp.wait_ge(small_loaded, 32)
            if cfg.n == 0:
                sp.wait_ge(x_loaded, 16)

        @block.gpsimd
        def _(pool):
            if cfg.n == 0:
                pool.memset(ident[:, :], 0.0).then_inc(ident_zero, 1)
                pool.wait_ge(ident_zero, 1)
                pool.affine_select(out=ident[:, :], in_=ident[:, :], compare_op=ALU.not_equal, fill=1.0,
                                   base=0, pattern=[[-1, P]], channel_multiplier=1).then_inc(ident_ready, 1)
                pool.wait_ge(ident_ready, 1)
                pool.tensor_copy(ident16[:, :], ident[:, :]).then_inc(ident_ready, 1)
                pool.wait_ge(ident_ready, 2)
            for i in range(2):
                words = stack_q[i][:, :, :].rearrange("p h s -> p (h s)").bitcast(F32)
                if cfg.dh < ROWS:
                    pool.memset(words[0:MASK_ROW, :], 0.0)
                pool.memset(words[MASK_ROW:P, :], TWO_ONES).then_inc(fill, 1)

        @block.vector
        def _(dve):
            for i in range(2):
                words = stack_k[i][:, :, :].rearrange("p h s -> p (h s)").bitcast(F32)
                if cfg.dh < ROWS:
                    dve.memset(words[0:MASK_ROW, :], 0.0)
                dve.memset(words[MASK_ROW:P, :], TWO_ONES)
                ins = dve.memset(va_ctx[i][:, :, :], 0.0)
            ins.then_inc(fill_k, 1)
            dve.wait_ge(fill_k, 1)
            for i in range(2):
                dve.memset(stack_k[i][MASK_ROW:MASK_ROW + 1, :, :], 0.0)
                for half in range(2):
                    dve.memset(va_ctx[i][half * SC:(half + 1) * SC, half::2, ONES:VW], 1.0)
            dve.wait_ge(ctx_loaded, 16)
            dve.tensor_copy(c_t[0][:, :, :, :, :], ctx[:, :, :, :, :]).then_inc(ctx_ready, 1)
            dve.wait_ge(ctx_ready, 1)
            dve.tensor_tensor(c_t[1][:, :, :, :, :], ctx[:, :, :, :, :], c_t[0][:, :, :, :, :].bitcast(F32),
                              ALU.subtract).then_inc(ctx_ready, 1)
            dve.wait_ge(w_loaded, 16)
            dve.tensor_copy(w_hi[:, :], raw[:, :]).then_inc(w_ready, 1)
            dve.wait_ge(w_ready, 1)
            dve.tensor_tensor(w_lo[:, :], raw[:, :], w_hi[:, :].bitcast(F32), ALU.subtract).then_inc(w_ready, 1)
            dve.wait_ge(small_loaded, 32)
            dve.tensor_scalar(bq_scaled[:, :], col[:, COLS["bq"]:COLS["bq"] + DC], cfg.scale, None, ALU.mult)\
                .then_inc(bq_done, 1)
            if cfg.mask != "add":
                dve.wait_ge(mask_loaded, 16)
                dve.tensor_copy(m_f[:, :], m_raw[:, :]).then_inc(m_part, 1)
                dve.wait_ge(m_part, 1)
                dve.tensor_scalar(m_z[:, :], m_f[:, :], 0.0, None, ALU.is_equal).then_inc(m_part, 1)
                dve.wait_ge(m_part, 2)
                dve.tensor_scalar(m_row[:, :], m_z[:, :], NEG, None, ALU.mult).then_inc(m_part, 1)
            dve.wait_ge(k_full_ready, KC)
            full, rest = k_full[0:KW, :, :], k_rest[0:KW, :, :]
            dve.tensor_copy(k_term[0:KW, 0, :, :], full).then_inc(k_part, 1)
            dve.wait_ge(k_part, 1)
            dve.tensor_tensor(rest, full, k_term[0:KW, 0, :, :], ALU.subtract).then_inc(k_part, 1)
            dve.wait_ge(k_part, 2)
            dve.tensor_copy(k_term[0:KW, 1, :, :], rest).then_inc(k_part, 1)
            dve.wait_ge(k_part, 3)
            dve.tensor_tensor(k_term[0:KW, 2, :, :], rest, k_term[0:KW, 1, :, :], ALU.subtract).then_inc(k_part, 1)
            for i in range(B // 2):
                dve.wait_ge(v_done, i + 1)
                dve.tensor_copy(v_ctx[:, 2 * i:2 * i + 2, :],
                                banks[2 + i][:, 0:2 * cfg.kvw].rearrange("p (b c) -> p b c", b=2)).then_inc(v_read, 1)

        @block.tensor
        def _(pe):
            pe.wait_ge(ctx_ready, 2)
            pe.wait_ge(w_ready, 2)

            def passes(dst, lhs, rhs):
                for k in range(DC):
                    for i, (a, b) in enumerate(((0, 0), (0, 1), (1, 0))):
                        last = pe.matmul(dst, lhs(a, k), rhs(b, k), start=(k == 0 and i == 0),
                                         stop=(k == DC - 1 and i == 2))
                return last

            kn, vn, v0 = ("k", "v", 0) if cfg.kvw == D else ("kv", "kv", SC)
            w = (w_hi, w_lo)
            for c in range(KC):
                passes(banks[c][:, :], lambda a, k: wgt(w[a], kn, k, c * P, P),
                       lambda b, k: c_t[b][:, k, :, 0, :]).then_inc(k_done, 1)
            for b2 in range(B // 2):
                for i in range(2):
                    last = passes(banks[2 + b2][:, i * cfg.kvw:(i + 1) * cfg.kvw],
                                  lambda a, k: c_t[a][:, k, 2 * b2 + i, :, :].rearrange("p a s -> p (a s)"),
                                  lambda b, k: wgt(w[b], vn, k, v0, cfg.kvw))
                last.then_inc(v_done, 1)

        @block.scalar
        def _(act):
            act.wait_ge(small_loaded, 32)
            for c in range(KC):
                act.wait_ge(k_done, c + 1)
                act.activation(k_full[0:KW, c, :], banks[c][0:KW, :], ACT.Identity,
                               bias=col[0:KW, COLS["bk"] + c:COLS["bk"] + c + 1]).then_inc(k_full_ready, 1)
    clear(nc, taken)


def kernel(**inputs):
    import numpy as np
    import concourse.bacc as bacc
    from concourse.bass_utils import run_bass_kernel_spmd

    def a(name):
        return np.asarray(inputs[name])

    def chunks(m):
        return m.reshape(m.shape[0] // P, P, m.shape[1]).transpose(1, 0, 2).reshape(P, -1)

    def features(*vectors):
        t = np.zeros((P, NCOLS), np.float32)
        for name, v in vectors:
            v = v.reshape(-1, min(P, v.size)).T
            t[:v.shape[0], COLS[name]:COLS[name] + v.shape[1]] = v
        return t

    def rowvecs(*vectors):
        return np.stack([v for _, v in sorted(vectors, key=lambda x: ROWV[x[0]])])

    arrays = {}
    g = {n: a("L0_xattn_" + n) for n in ("Wq", "bq", "Wk", "bk", "Wv", "bv", "Wo", "bo", "gamma", "beta")}
    kv = np.concatenate([g["Wk"], g["Wv"]], axis=1)
    arrays["w0"] = np.concatenate([chunks(m) for m in (g["Wq"], kv, g["Wo"])], axis=1)
    bv = np.broadcast_to(g["bv"].reshape(8, 1, 8), (8, 4, 8)).reshape(-1)
    arrays["cols0"] = features(("bq", g["bq"]), ("bk", g["bk"]), ("bv", bv))
    arrays["rows0"] = rowvecs(("bo", g["bo"]), ("g", g["gamma"]), ("b", g["beta"]))
    for n in (1, 2):
        g = {m: a(f"L{n}_xattn_{m}") for m in ("q_w", "q_b", "kv_w", "kv_b", "out_w", "out_b", "postnorm_w",
                                               "mlp_w1", "mlp_b1", "mlp_w2", "mlp_b2")}
        arrays[f"w{n}"] = np.concatenate([chunks(m) for m in (
            g["q_w"], g["kv_w"][:, 0::2], g["kv_w"][:, 1::2], g["out_w"], g["mlp_w1"], g["mlp_w2"])], axis=1)
        arrays[f"cols{n}"] = features(("bq", g["q_b"]), ("bk", g["kv_b"][0::2]), ("bv", g["kv_b"][1::2]),
                                      ("n_w", g["postnorm_w"]), ("b1", g["mlp_b1"]))
        arrays[f"rows{n}"] = rowvecs(("bo", g["out_b"]), ("b2", g["mlp_b2"]))
    g = {m: a(f"L3_xattn_{m}") for m in ("ln1_w", "ln1_b", "q_w", "q_b", "k_w", "k_b", "v_w", "v_b", "cproj_w",
                                         "cproj_b", "ln2_w", "ln2_b", "fc_w", "fc_b", "proj_w", "proj_b")}
    arrays["w3"] = np.concatenate([chunks(m) for m in (
        g["q_w"], g["k_w"], g["v_w"], g["cproj_w"], g["fc_w"], g["proj_w"])], axis=1)
    arrays["cols3"] = features(("bq", g["q_b"]), ("bk", g["k_b"]), ("bv", g["v_b"]), ("n_w", g["ln2_w"]),
                               ("n_b", g["ln2_b"]), ("p_w", g["ln1_w"]), ("p_b", g["ln1_b"]), ("b1", g["fc_b"]))
    arrays["rows3"] = rowvecs(("bo", g["cproj_b"]), ("b2", g["proj_b"]))
    arrays["x"] = a("x")
    ctx = a("ctx_2048").transpose(2, 0, 1).reshape(DC, P, B, 1, SC)
    arrays["ctx_t"] = np.broadcast_to(ctx, (DC, P, B, 2, SC)).transpose(1, 0, 2, 3, 4).reshape(P, -1)
    mask = a("mask_Bx1xSxS2_ff0").reshape(B, S, SC)
    arrays["mask_q"] = mask
    arrays["mask_k"] = mask.transpose(0, 2, 1)
    arrays["mask_i"] = a("mask_BxS2_ik0")
    arrays["mask_b"] = a("mask_BxS2_bf1").view(np.uint8)

    nc = bacc.Bacc("TRN2", target_bir_lowering=False, num_devices=1)
    arrays = {name: np.ascontiguousarray(v) for name, v in arrays.items()}
    aps = {name: nc.dram_tensor("in_" + name, v.shape, mybir.dt.from_np(v.dtype), kind="ExternalInput").ap()
           for name, v in arrays.items()}
    out = nc.dram_tensor("out_0", (B, S, D), F32, kind="ExternalOutput").ap()
    program(nc, aps["x"], aps["ctx_t"], [aps[f"w{n}"] for n in range(4)], [aps[f"cols{n}"] for n in range(4)],
            [aps[f"rows{n}"] for n in range(4)], aps["mask_q"], aps["mask_k"], aps["mask_i"], aps["mask_b"], out)
    r = run_bass_kernel_spmd(nc, [{"in_" + name: v for name, v in arrays.items()}], core_ids=[0])
    return r.results[0]["out_0"]
```

```python
from contextlib import ExitStack

import concourse.bass as bass
from concourse import mybir

F32 = mybir.dt.float32
F32R = mybir.dt.float32r
BF16 = mybir.dt.bfloat16
I32 = mybir.dt.int32
U8 = mybir.dt.uint8
ACT = mybir.ActivationFunctionType
ALU = mybir.AluOpType
AX = mybir.AxisListType

P = 128
B = 8
S = 256
SC = 64
D = 256
DC = D // P
QT = S // P
FF = 4 * D
FC = FF // P
ROWS = 16
NTERM = 3
Q_TERMS = (0, 1, 2, 0, 1, 0)
K_TERMS = (0, 0, 0, 1, 1, 2)
MASK_ROW = 96
MAX_ROW = 97
KS = MASK_ROW + 1
KST = MAX_ROW + 2
NEG = -1.0e30
VW = 32
ONES = 16
MAGIC = float(0x5F3759DF)
TWO_ONES = (0x3F803F80 & 0x7FFFFF | 0x800000) / 2.0 ** 23


class Cfg:

    def __init__(self, n, heads, kvheads, latent, scale, norm, eps, mlp, pre_norm, mask):
        self.n, self.heads, self.kvheads, self.latent = n, heads, kvheads, latent
        self.scale, self.norm, self.eps, self.mlp = scale, norm, eps, mlp
        self.pre_norm, self.mask = pre_norm, mask
        self.dh = D // heads
        self.kvw = kvheads * self.dh
        self.keys = S + SC if latent else SC
        self.c0 = S if latent else 0
        self.groups = heads // 4
        self.rowvs = 2 if mlp else 3
        self.spu = 1 if latent else 8
        self.s_uses = QT * heads // self.spu
        self.st_group = 5 if latent else 1
        self.st_uses = self.st_group * self.groups
        self.a_uses = 4 if latent else 2
        self.ot_uses = self.groups // 2
        self.m_uses = self.ot_uses + 2 + (6 if mlp else 0)
        self.o_uses = self.groups
        self.norm_steps = 15 if norm == "ln" else 16
        off, self.w = 0, {}
        kv = [("k", DC, D), ("v", DC, D)] if self.kvw == D else [("kv", DC, P)]
        for name, k, cols in [("q", DC, D)] + kv + [("o", DC, D)] + (
                [("w1", DC, FF), ("w2", FC, D)] if mlp else []):
            self.w[name] = (off, k, cols)
            off += k * cols
        self.wcols = off


LAYERS = [
    Cfg(0, 32, 8, False, 8 ** -0.5, "ln", 1e-6, False, False, "add"),
    Cfg(1, 16, 16, True, 1 / 16, "rms", 1e-6, True, False, "int"),
    Cfg(2, 16, 16, True, 1 / 16, "rms", 1e-6, True, False, "int"),
    Cfg(3, 16, 16, False, 0.25, "ln", 1e-5, True, True, "bool"),
]
COLS = {"bq": 0, "bk": 2, "bv": 4, "n_w": 6, "n_b": 8, "p_w": 10, "p_b": 12, "b1": 14}
NCOLS = 22
ROWV = {"bo": 0, "b2": 1, "g": 1, "b": 2}



def timetable(cfg):
    steps = []

    def put(at, stage, unit, n=0):
        steps.append((at, len(steps), stage, unit, n))

    put(0.2, "A", "tokens")
    for j in range(cfg.norm_steps if cfg.pre_norm else 0):
        put(0.8 + 0.4 * j, "A", "norm", j)
    put(7.5, "A", "turn")
    put(8.2, "A", "turn.act")
    put(8.8, "A", "turn.hi")
    put(9.2, "A", "turn.lo")
    put(11.0, "A", "q")
    put(12.6, "A", "q.act")
    for j in range(4):
        put(13.5 + 0.7 * j, "A", "q.term", j)
    put(16.2, "A", "q.store")
    if cfg.latent:
        put(13.0, "A", "k")
        put(14.6, "A", "k.act")
        put(15.6, "A", "k.h")
        put(16.2, "A", "k.r")
        put(17.6, "A", "k.m")
        put(18.2, "A", "k.l")
        put(19.4, "A", "k.store")
        put(22.6, "A", "v")
        put(24.6, "A", "v.out")
    put(23.5, "A", "load")
    put(28.5, "A", "v_ctx")
    gap = 31.0 / cfg.s_uses
    for n in range(cfg.s_uses):
        put(1.5 + gap * n, "S", "score", n)
        put(1.5 + gap * n + 0.3, "S", "max", n)
    put(33.0, "S", "neg")
    put(33.4, "S", "neg.turn")
    put(33.8, "S", "neg.out")
    put(33.9, "S", "neg.load")
    per = 16.8 / cfg.groups
    for g in range(cfg.groups):
        base = 4.0 + per * g
        for i in range(cfg.st_group):
            put(base + 0.75 * i, "O", "st", cfg.st_group * g + i)
            put(base + 0.75 * i + 0.3, "O", "mask", cfg.st_group * g + i)
            put(base + 0.75 * i + (1.0 if cfg.mask == "add" else 0.4), "O", "exp", cfg.st_group * g + i)
        last = base + 0.75 * (cfg.st_group - 1)
        put(last + 1.9, "O", "values", g)
        put(last + (2.6 if cfg.mask == "add" else 3.7), "O", "out", g)
    put(0.3, "M", "residual")
    for n in range(cfg.ot_uses):
        put(0.4 + 0.5 * n, "M", "divide.turn", n)
        put(1.2 + 0.5 * n, "M", "divide", n)
    back = 2.4 if cfg.ot_uses == 2 else 3.6
    put(back, "M", "back")
    put(back + 0.6, "M", "back.act")
    put(back + 1.2, "M", "back.hi")
    put(back + 1.4, "M", "back.lo")
    put(back + 2.9, "M", "proj")
    put(back + 4.4, "M", "proj.out")
    put(back + 4.6, "M", "residual2")
    for j in range(cfg.norm_steps):
        put(back + 4.7 + 0.42 * j, "M", "norm", j)
    if cfg.mlp:
        put(15.5, "M", "norm.turn")
        put(16.1, "M", "norm.act")
        put(16.8, "M", "norm.hi")
        put(17.0, "M", "norm.lo")
        for n in range(4):
            put(20.5 + 1.5 * n, "M", "mlp1", n)
            put(22.0 + 1.5 * n, "M", "mlp1.act", n)
            put(22.8 + 1.5 * n, "M", "mlp1.hi", n)
            put(23.2 + 1.5 * n, "M", "mlp1.lo", n)
        for n in range(2 * QT * 2):
            put(27.3 + 0.75 * n, "M", "mlp2", n)
        put(33.95, "M", "mlp2.out")
        put(33.97, "M", "store")
    else:
        put(16.5, "M", "gamma")
        put(17.5, "M", "beta")
    return [(stage, unit, n) for _, _, stage, unit, n in sorted(steps)]


class Seq:

    def __init__(self, j, k):
        self.j, self.k, self.par = j, k, k % 2

    def count(self, per, more=0):
        c = per * (self.k + 1) + more
        return c if isinstance(self.j, int) else self.j * (2 * per) + c

    def count_par(self, per, more=0):
        c = per * (self.k // 2 + 1) + more
        return c if isinstance(self.j, int) else self.j * per + c

    def index(self):
        return self.k if isinstance(self.j, int) else self.j * 2 + self.k

    def before(self, n):
        return Seq(self.j, self.k - n)


def wait(eng, sem, n):
    if isinstance(n, int) and n <= 0:
        return
    eng.wait_ge(sem, n)


def program(nc, x, ctx_t, w, cols, rows, mask_q, mask_k, mask_i, mask_b, out):
    top = ExitStack()
    with top:
        x_all = top.enter_context(nc.sbuf_tensor("x_all", [P, B * QT, D], F32))
        ident = top.enter_context(nc.sbuf_tensor("ident", [P, P], F32))
        ident16 = top.enter_context(nc.sbuf_tensor("ident16", [P, P], BF16))
        banks = [top.enter_context(nc.psum_tensor(f"bank{i}", [P, 512], F32)) for i in range(8)]
        for cfg in LAYERS:
            layer(nc, cfg, banks, x_all, ident, ident16, x, ctx_t, w[cfg.n], cols[cfg.n], rows[cfg.n],
                  mask_q, mask_k, mask_i, mask_b, out)


def layer(nc, cfg, banks, x_all, ident, ident16, x, ctx_t, w_in, cols_in, rows_in,
          mask_q, mask_k, mask_i, mask_b, out):
    L = f"L{cfg.n}_"
    H, DH, G, KV = cfg.heads, cfg.dh, cfg.groups, cfg.kvheads
    lay = ExitStack()
    with lay:
        def sb(name, shape, dt=F32):
            return lay.enter_context(nc.sbuf_tensor(L + name, shape, dt))

        taken = []

        def sem(name):
            s = lay.enter_context(nc.semaphore(L + name))
            taken.append(s)
            return s

        w_hi = sb("w_hi", [P, cfg.wcols], F32R)
        w_lo = sb("w_lo", [P, cfg.wcols], F32R)
        col = sb("col", [P, NCOLS])
        row = sb("row", [P, cfg.rowvs, D])
        bq_scaled = sb("bq_scaled", [P, DC])
        stack_q = [sb(f"stack_q{i}", [P, H, S], BF16) for i in range(2)]
        stack_k = [sb(f"stack_k{i}", [P, KV, cfg.keys], BF16) for i in range(2)]
        v_ctx = sb("v_ctx", [P, B, cfg.kvw])
        va_ctx = [sb(f"va_ctx{i}", [P, H, VW]) for i in range(2)]
        q_dram = nc.dram_tensor(L + "q_terms", (B, NTERM, D, S), BF16, kind="Internal").ap()
        k_dram = nc.dram_tensor(L + "k_terms", (B, NTERM, cfg.kvw, cfg.keys), BF16, kind="Internal").ap()
        mask_dram = nc.dram_tensor(L + "mask_rows", (B, SC), BF16, kind="Internal").ap()

        def wgt(part, name, k, c0=0, n=None):
            off, _, width = cfg.w[name]
            return part[:, off + k * width + c0:off + k * width + c0 + (n or width)]

        rise = {}

        def counted(name, per=1):
            s = sem(name)
            rise[name] = (s, per)
            return s

        S0, T0, O0, A0, M0 = 0, 2, 4, 5, 6
        RING = {S0: 2, T0: 2, O0: 1, A0: 1, M0: 2}
        USES = {S0: cfg.s_uses + QT, T0: cfg.st_uses, O0: cfg.o_uses, A0: cfg.a_uses, M0: cfg.m_uses}
        bank_full = [counted(f"bank_full{i}", USES[f] // RING[f]) for f in RING for i in range(f, f + RING[f])]
        xc_ready, xn_ready = counted("xc_ready"), counted("xn_ready")
        X_PARTS = DC if cfg.pre_norm else 1
        x_full_ready = counted("x_full_ready", X_PARTS)
        x_hi_ready, x_lo_ready = counted("x_hi_ready"), counted("x_lo_ready")
        q_full_ready, q_h, q_r, q_m, q_l = counted("q_full_ready", DC), *map(counted, ("q_h", "q_r", "q_m", "q_l"))
        k_full_ready, k_h, k_r, k_m, k_l = counted("k_full_ready", DC), *map(counted, ("k_h", "k_r", "k_m", "k_l"))
        va_ready, va_ctx_ready = counted("va_ready"), counted("va_ctx_ready", 2)
        q_written, k_written = counted("q_written", 16), counted("k_written", 16)
        n_stack = len(Q_TERMS) + len(K_TERMS) + (cfg.mask != "add")
        STACK = 16 * n_stack
        stack_loaded = [counted(f"stack_loaded{i}", STACK) for i in range(2)]
        masks_loaded = [counted(f"masks_loaded{i}", 48) for i in range(2)]
        max_loaded = [counted(f"max_loaded{i}", 32) for i in range(2)]
        s_masked, peak_done = counted("s_masked", cfg.s_uses), counted("peak_done", cfg.s_uses)
        neg_h, neg_done = counted("neg_h", QT), counted("neg_done", QT)
        peak_t_ready = counted("peak_t_ready", QT)
        st_masked = counted("st_masked", cfg.st_uses)
        exp_done = counted("exp_done", cfg.st_uses)
        o_t_ready = counted("o_t_ready", G)
        rec_ready, o_tok_ready = counted("rec_ready", cfg.ot_uses), counted("o_tok_ready", cfg.ot_uses)
        o_full_ready, o_hi_ready, o_lo_ready = counted("o_full_ready", DC), counted("o_hi_ready"), counted("o_lo_ready")
        xb_ready, xb2_ready = counted("xb_ready", QT), counted("xb2_ready", QT)
        xb_free, xb2_free = counted("xb_free"), counted("xb2_free")
        att_ready, y_ready = counted("att_ready"), counted("y_ready")
        y_full_ready, y_hi_ready, y_lo_ready = counted("y_full_ready", DC), counted("y_hi_ready"), counted("y_lo_ready")
        h_full_ready, h_hi_ready, h_lo_ready = counted("h_full_ready", FC), counted("h_hi_ready", 4), counted("h_lo_ready", 4)
        g_ready, x_new = counted("g_ready"), counted("x_new")
        NORM = cfg.norm_steps
        norm_step, pre_step = counted("norm_step", NORM), counted("pre_step", NORM)
        stored = [counted(f"stored{i}", 16) for i in range(2)]
        ones_ready = sem("ones_ready")

        prepare(nc, cfg, banks, x_all, ident, ident16, x, ctx_t, w_in, cols_in, rows_in, mask_i, mask_b,
                w_hi, w_lo, col, row, bq_scaled, stack_q, stack_k, v_ctx, va_ctx, k_dram, mask_dram, wgt, rise)

        xc = sb("xc", [P, QT, D])
        xb = sb("xb", [P, QT, D])
        x_t = [sb(f"x_t_{p}", [P, DC, S], F32R) for p in ("hi", "lo")]
        x_full = sb("x_full", [P, DC, S])
        q_full = sb("q_full", [P, DC, S])
        q_rest = sb("q_rest", [P, DC, S])
        q_term = sb("q_term", [P, NTERM, DC, S], BF16)
        if cfg.latent:
            k_full = sb("k_full", [P, DC, S])
            k_rest = sb("k_rest", [P, DC, S])
            k_term = sb("k_term", [P, NTERM, DC, S], BF16)
            va = [sb(f"va{i}", [P, QT, H, VW]) for i in range(2)]
            p_lat = sb("p_lat", [P, 6, QT, S])
        p_ctx = sb("p_ctx", [P, 2, 2, S])
        peak = sb("peak", [P, QT, H])
        neg_peak = sb("neg_peak", [P, QT, 2, H], BF16)
        peak_t = sb("peak_t", [H, 2, QT, P], BF16)
        o_t = sb("o_t", [P, G, S])
        o_rec = sb("o_rec", [P, 2, 2, QT, 4])
        o_tok = sb("o_tok", [P, QT, D])
        o_full = sb("o_full", [P, DC, S])
        o_f = [sb(f"o_f_{p}", [P, DC, S], F32R) for p in ("hi", "lo")]
        att = sb("att", [P, QT, D])
        y = o_tok
        st6 = sb("st6", [P, QT, 6])
        mv = sb("mv", [P, QT, 2])
        nw = sb("nw", [P, 5, QT])
        if cfg.pre_norm:
            xn = sb("xn", [P, QT, D])
        if cfg.mask == "add":
            mq = [sb(f"mq{i}", [P, QT, SC]) for i in range(2)]
            mk = [sb(f"mk{i}", [P, S]) for i in range(2)]
            s_tmp = sb("s_tmp", [P, 2, 8, SC])
            st_tmp = sb("st_tmp", [P, 2, 2, S])
        if cfg.mlp:
            y_full = o_full
            y_t = [sb(f"y_t_{p}", [P, DC, S], F32R) for p in ("hi", "lo")]
            h_full = sb("h_full", [P, 2, 2, S])
            h_t = [sb(f"h_t_{p}", [P, FC, S], F32R) for p in ("hi", "lo")]
            xb2 = sb("xb2", [P, QT, D])
        if cfg.n == 3:
            y_out = [sb(f"y_out{i}", [P, QT, D]) for i in range(2)]

        M_BACK = cfg.ot_uses
        M_PROJ, M_NT, M_H, M_OUT = M_BACK + 1, M_BACK + 2, M_BACK + 3, M_BACK + 7
        NEG0 = cfg.s_uses

        def read_out(stage, n):
            if stage == A0:
                return [(x_full_ready, X_PARTS, X_PARTS), (q_full_ready, DC, DC),
                        (k_full_ready, DC, DC), (va_ready, 1, 1)][n]
            if stage == O0:
                return o_t_ready, G, n + 1
            if stage == S0:
                if n < NEG0:
                    return (s_masked if cfg.mask == "add" else peak_done), cfg.s_uses, n + 1
                return peak_t_ready, QT, n - NEG0 + 1
            if stage == T0:
                return (st_masked if cfg.mask == "add" else exp_done), cfg.st_uses, n + 1
            if n < M_BACK:
                return o_tok_ready, cfg.ot_uses, n + 1
            if n == M_BACK:
                return o_full_ready, DC, DC
            if n == M_PROJ:
                return att_ready, 1, 1
            if n == M_NT:
                return y_full_ready, DC, DC
            if n < M_OUT:
                return h_full_ready, FC, 2 * (n - M_H + 1)
            return x_new, 1, 1

        def slot(stage, n):
            return stage + n % RING[stage]

        def tile(stage, n):
            return banks[slot(stage, n)]

        def wait_free(eng, s, stage, n):
            before = n - RING[stage]
            which, per, count = read_out(stage, before % USES[stage])
            eng.wait_ge(which, (s if before >= 0 else s.before(1)).count(per, count))

        def wait_full(eng, s, stage, n):
            ring = RING[stage]
            wait(eng, bank_full[slot(stage, n)], s.count(USES[stage] // ring, n // ring + 1))

        def x_rows(s, t, n):
            if isinstance(s.j, int):
                part = x_all[:, QT * s.index() + t:QT * s.index() + t + n, :]
            else:
                part = x_all[:, bass.ds(s.index() * QT + t, n), :]
            return part if n > 1 else part.rearrange("p a d -> p (a d)")

        steps = timetable(cfg)
        AHEAD = {"A": 2, "S": 1, "O": 0, "M": -1}

        def run(eng, does):
            def turn(j, k, stages):
                for stage, unit, n in steps:
                    if stage in stages and (stage, unit) in does:
                        does[stage, unit](Seq(j, k + AHEAD[stage]), n)
            turn(0, -2, "A")
            turn(0, -1, "AS")
            turn(0, 0, "ASO")
            with eng.Fori(0, 2) as j:
                turn(j, 1, "ASOM")
                turn(j, 2, "ASOM")
            turn(0, B - 3, "ASOM")
            turn(0, B - 2, "SOM")
            turn(0, B - 1, "OM")
            turn(0, B, "M")

        block = lay.enter_context(nc.Block())

        @block.tensor
        def _(pe):
            def mm3(dst, a, b, first, last):
                pe.matmul(dst, a[0], b[0], start=first, stop=False)
                pe.matmul(dst, a[0], b[1], start=False, stop=False)
                return pe.matmul(dst, a[1], b[0], start=False, stop=last)

            def feature_major(bank, name, c0, act):
                for i in range(2):
                    for k in range(DC):
                        c = c0 + i * P
                        last = mm3(bank[:, i * S:(i + 1) * S],
                                   (wgt(w_hi, name, k, c, P), wgt(w_lo, name, k, c, P)),
                                   (act[0][:, k, :], act[1][:, k, :]), k == 0, k == DC - 1)
                return last

            def token_major(bank, name, act, chunks=DC):
                for t in range(QT):
                    for k in range(chunks):
                        last = mm3(bank[:, t * D:(t + 1) * D],
                                   (act[0][:, k, t * P:(t + 1) * P], act[1][:, k, t * P:(t + 1) * P]),
                                   (wgt(w_hi, name, k), wgt(w_lo, name, k)), k == 0, k == chunks - 1)
                return last

            def turn_to_features(bank, src):
                for t in range(QT):
                    for c in range(DC):
                        last = pe.transpose(bank[:, c * S + t * P:c * S + (t + 1) * P],
                                            src[:, t, c * P:(c + 1) * P], ident[:, :])
                return last

            def tokens_turn(s, _):
                if cfg.pre_norm:
                    pe.wait_ge(xn_ready, s.count(1, 1))
                else:
                    pe.wait_ge(xc_ready, s.count(1, 1))
                wait_free(pe, s, A0, 0)
                turn_to_features(tile(A0, 0), xn if cfg.pre_norm else xc).then_inc(bank_full[slot(A0, 0)], 1)

            def queries(s, _):
                wait_free(pe, s, A0, 1)
                pe.wait_ge(x_hi_ready, s.count(1, 1))
                pe.wait_ge(x_lo_ready, s.count(1, 1))
                feature_major(tile(A0, 1), "q", 0, x_t).then_inc(bank_full[slot(A0, 1)], 1)

            def keys(s, _):
                wait_free(pe, s, A0, 2)
                feature_major(tile(A0, 2), "k", 0, x_t).then_inc(bank_full[slot(A0, 2)], 1)

            def token_values(s, _):
                wait_free(pe, s, A0, 3)
                token_major(tile(A0, 3), "v", x_t).then_inc(bank_full[slot(A0, 3)], 1)

            def scores(s, n):
                if n == 0:
                    pe.wait_ge(stack_loaded[s.par], s.count_par(STACK, STACK))
                wait_free(pe, s, S0, n)
                per_tile = H // cfg.spu
                t, h0 = n // per_tile, n % per_tile * cfg.spu
                for i in range(cfg.spu):
                    last = pe.matmul(tile(S0, n)[:, i * cfg.keys:(i + 1) * cfg.keys],
                                     stack_q[s.par][0:KS, h0 + i, t * P:(t + 1) * P],
                                     stack_k[s.par][0:KS, (h0 + i) * KV // H, :], start=True, stop=True)
                last.then_inc(bank_full[slot(S0, n)], 1)

            def peaks_turn(s, _):
                for t in range(QT):
                    wait_free(pe, s, S0, NEG0 + t)
                    pe.wait_ge(neg_done, s.count(QT, t + 1))
                    for a in range(2):
                        last = pe.transpose(tile(S0, NEG0 + t)[:, :].bitcast(BF16)[0:H, a * P:(a + 1) * P],
                                            neg_peak[:, t, a, :], ident16[:, :])
                    last.then_inc(bank_full[slot(S0, NEG0 + t)], 1)

            def scores_t(s, n):
                if n == 0:
                    pe.wait_ge(max_loaded[s.par], s.count_par(32, 32))
                g, i = n // cfg.st_group, n % cfg.st_group - 1
                wait_free(pe, s, T0, n)
                if i < 0:
                    for i in range(4):
                        h, half = 4 * g + i, i % 2 * SC
                        last = pe.matmul(tile(T0, n)[half:half + SC, i // 2 * S:(i // 2 + 1) * S],
                                         stack_k[s.par][0:KST, h * KV // H, cfg.c0:cfg.c0 + SC],
                                         stack_q[s.par][0:KST, h, :], start=True, stop=True)
                else:
                    h = 4 * g + i
                    for t in range(QT):
                        last = pe.matmul(tile(T0, n)[:, t * S:(t + 1) * S],
                                         stack_k[s.par][0:KST, h, t * P:(t + 1) * P],
                                         stack_q[s.par][0:KST, h, :], start=True, stop=True)
                last.then_inc(bank_full[slot(T0, n)], 1)

            def values(s, g):
                wait_free(pe, s, O0, g)
                pe.wait_ge(exp_done, s.count(cfg.st_uses, cfg.st_group * (g + 1)))
                if g == 0:
                    pe.wait_ge(va_ctx_ready, s.count(2, 2))
                    if cfg.latent:
                        pe.wait_ge(va_ready, s.count(1, 1))
                parts = (QT if cfg.latent else 0) + 1
                for t in range(parts):
                    for i in range(4):
                        h = 4 * g + i
                        if t == parts - 1:
                            a, b = va_ctx[s.par][:, h, :], p_ctx[:, g % 2, i // 2, :]
                        else:
                            a, b = va[s.par][:, t, h, :], p_lat[:, h % 6, t, :]
                        last = pe.matmul(tile(O0, g)[VW * i:VW * (i + 1), 0:S], a, b,
                                         start=(t == 0), stop=(t == parts - 1), tile_position=(0, VW * i))
                last.then_inc(bank_full[slot(O0, g)], 1)

            def outputs_turn(s, n):
                pe.wait_ge(o_t_ready, s.count(G, 2 * n + 2))
                wait_free(pe, s, M0, n)
                for g in range(2):
                    for t in range(QT):
                        last = pe.transpose(tile(M0, n)[:, (g * QT + t) * P:(g * QT + t + 1) * P],
                                            o_t[:, 2 * n + g, t * P:(t + 1) * P], ident[:, :])
                last.then_inc(bank_full[slot(M0, n)], 1)

            def outputs_back(s, _):
                wait_free(pe, s, M0, M_BACK)
                pe.wait_ge(o_tok_ready, s.count(cfg.ot_uses, cfg.ot_uses))
                turn_to_features(tile(M0, M_BACK), o_tok).then_inc(bank_full[slot(M0, M_BACK)], 1)

            def projection(s, _):
                wait_free(pe, s, M0, M_PROJ)
                pe.wait_ge(o_hi_ready, s.count(1, 1))
                pe.wait_ge(o_lo_ready, s.count(1, 1))
                token_major(tile(M0, M_PROJ), "o", o_f).then_inc(bank_full[slot(M0, M_PROJ)], 1)

            def norm_turn(s, _):
                wait_free(pe, s, M0, M_NT)
                pe.wait_ge(y_ready, s.count(1, 1))
                turn_to_features(tile(M0, M_NT), y).then_inc(bank_full[slot(M0, M_NT)], 1)

            def mlp1(s, n):
                wait_free(pe, s, M0, M_H + n)
                if n == 0:
                    pe.wait_ge(y_hi_ready, s.count(1, 1))
                    pe.wait_ge(y_lo_ready, s.count(1, 1))
                feature_major(tile(M0, M_H + n), "w1", 2 * n * P, y_t).then_inc(bank_full[slot(M0, M_H + n)], 1)

            def mlp2(s, n):
                t, quarter = n // 4, n % 4
                if n == 0:
                    wait_free(pe, s, M0, M_OUT)
                if t == 0:
                    pe.wait_ge(h_hi_ready, s.count(4, quarter + 1))
                    pe.wait_ge(h_lo_ready, s.count(4, quarter + 1))
                for k in range(2 * quarter, 2 * quarter + 2):
                    last = mm3(tile(M0, M_OUT)[:, t * D:(t + 1) * D],
                               (h_t[0][:, k, t * P:(t + 1) * P], h_t[1][:, k, t * P:(t + 1) * P]),
                               (wgt(w_hi, "w2", k), wgt(w_lo, "w2", k)), k == 0, k == FC - 1)
                if n == 4 * QT - 1:
                    last.then_inc(bank_full[slot(M0, M_OUT)], 1)

            pe.wait_ge(ones_ready, 1)
            run(pe, {("A", "turn"): tokens_turn, ("A", "q"): queries, ("A", "k"): keys, ("A", "v"): token_values,
                     ("S", "score"): scores, ("S", "neg.turn"): peaks_turn,
                     ("O", "st"): scores_t, ("O", "values"): values,
                     ("M", "divide.turn"): outputs_turn, ("M", "back"): outputs_back, ("M", "proj"): projection,
                     ("M", "norm.turn"): norm_turn, ("M", "mlp1"): mlp1, ("M", "mlp2"): mlp2})

        @block.scalar
        def _(act):
            def column(name, c):
                return col[:, COLS[name] + c:COLS[name] + c + 1]

            def tokens(s, _):
                b = s.before(1)
                wait_full(act, b, A0, 0)
                if cfg.pre_norm:
                    act.wait_ge(xn_ready, b.count(1, 1))
                act.activation(xc[:, :, :], x_rows(s, 0, QT), ACT.Copy).then_inc(xc_ready, 1)

            def tokens_full(s, _):
                act.wait_ge(x_lo_ready, s.count(1))
                wait_full(act, s, A0, 0)
                if cfg.pre_norm:
                    for c in range(DC):
                        act.activation(x_full[:, c, :], tile(A0, 0)[:, c * S:(c + 1) * S], ACT.Identity,
                                       scale=column("p_w", c), bias=column("p_b", c)).then_inc(x_full_ready, 1)
                else:
                    act.activation(x_full[:, :, :].rearrange("p c s -> p (c s)"), tile(A0, 0)[:, :], ACT.Copy)\
                        .then_inc(x_full_ready, 1)

            def queries_full(s, _):
                act.wait_ge(q_r, s.count(1))
                wait_full(act, s, A0, 1)
                for c in range(DC):
                    act.activation(q_full[:, c, :], tile(A0, 1)[:, c * S:(c + 1) * S], ACT.Identity,
                                   scale=cfg.scale, bias=bq_scaled[:, c:c + 1]).then_inc(q_full_ready, 1)

            def keys_full(s, _):
                wait_full(act, s, A0, 2)
                for c in range(DC):
                    act.activation(k_full[:, c, :], tile(A0, 2)[:, c * S:(c + 1) * S], ACT.Identity,
                                   bias=column("bk", c)).then_inc(k_full_ready, 1)

            def keys_h(s, _):
                act.wait_ge(k_full_ready, s.count(DC, DC))
                act.wait_ge(k_written, s.count(16))
                act.activation(k_term[:, 0, :, :], k_full[:, :, :], ACT.Copy).then_inc(k_h, 1)

            def keys_m(s, _):
                act.wait_ge(k_r, s.count(1, 1))
                act.activation(k_term[:, 1, :, :], k_rest[:, :, :], ACT.Copy).then_inc(k_m, 1)

            def values_ctx(s, _):
                wait_full(act, s.before(2), O0, G - 1)
                rep = H // KV
                for half in range(2):
                    part = slice(half * SC, (half + 1) * SC)
                    if isinstance(s.j, int):
                        src = v_ctx[part, s.index(), :]
                    else:
                        src = v_ctx[part, bass.ds(s.index(), 1), :].rearrange("p a c -> p (a c)")
                    if rep == 1:
                        src = src.rearrange("p (h d) -> p h d", d=DH)[:, half::2, :]
                        dst = va_ctx[s.par][part, half::2, 0:DH]
                    else:
                        src = src.rearrange("p (k d) -> p k d", d=DH).unsqueeze(2)\
                            .to_broadcast([SC, KV, rep // 2, DH])
                        dst = va_ctx[s.par][part, :, :].rearrange("p (k r) v -> p k r v", r=rep)[:, :, half::2, 0:DH]
                    act.activation(dst, src, ACT.Copy).then_inc(va_ctx_ready, 1)

            def outputs_full(s, _):
                act.wait_ge(o_lo_ready, s.count(1))
                if cfg.mlp:
                    act.wait_ge(y_lo_ready, s.count(1))
                wait_full(act, s, M0, M_BACK)
                for c in range(DC):
                    act.activation(o_full[:, c, :], tile(M0, M_BACK)[:, c * S:(c + 1) * S],
                                   ACT.Identity, bias=column("bv", c)).then_inc(o_full_ready, 1)

            def norm_full(s, _):
                act.wait_ge(o_lo_ready, s.count(1, 1))
                wait_full(act, s, M0, M_NT)
                for c in range(DC):
                    act.activation(y_full[:, c, :], tile(M0, M_NT)[:, c * S:(c + 1) * S],
                                   ACT.Identity, scale=column("n_w", c), bias=column("n_b", c))\
                        .then_inc(y_full_ready, 1)

            def gelu(s, n):
                act.wait_ge(h_lo_ready, s.count(4, n - 1))
                wait_full(act, s, M0, M_H + n)
                for i in range(2):
                    act.activation(h_full[:, n % 2, i, :], tile(M0, M_H + n)[:, i * S:(i + 1) * S],
                                   ACT.Gelu_apprx_tanh, bias=column("b1", 2 * n + i)).then_inc(h_full_ready, 1)

            def exponentials(s, n):
                g, i = n // cfg.st_group, n % cfg.st_group - 1
                if i < 0:
                    if g < 2:
                        wait_full(act, s.before(1), O0, G - 2 + g)
                    else:
                        wait_full(act, s, O0, g - 2)
                    if cfg.mask == "add":
                        act.wait_ge(st_masked, s.count(cfg.st_uses, n + 1))
                        src = st_tmp[:, g % 2, :, :].rearrange("p a s -> p (a s)")
                    else:
                        wait_full(act, s, T0, n)
                        src = tile(T0, n)[:, :]
                    dst = p_ctx[:, g % 2, :, :]
                else:
                    h = 4 * g + i
                    if h >= 6:
                        wait_full(act, s, O0, (h - 6) // 4)
                    else:
                        wait_full(act, s.before(1), O0, G - 1)
                    wait_full(act, s, T0, n)
                    src = tile(T0, n)[:, :]
                    dst = p_lat[:, h % 6, :, :]
                act.activation(dst.rearrange("p a s -> p (a s)"), src, ACT.Exp).then_inc(exp_done, 1)

            run(act, {("A", "tokens"): tokens, ("A", "turn.act"): tokens_full, ("A", "q.act"): queries_full,
                      ("A", "k.act"): keys_full, ("A", "k.h"): keys_h, ("A", "k.m"): keys_m,
                      ("A", "v_ctx"): values_ctx, ("O", "exp"): exponentials,
                      ("M", "back.act"): outputs_full, ("M", "norm.act"): norm_full, ("M", "mlp1.act"): gelu})

        @block.vector
        def _(dve):
            mean, var = mv[:, :, 0], mv[:, :, 1]
            v, r, a, sq = nw[:, 0, :], nw[:, 1, :], nw[:, 2, :], nw[:, 3, :]

            def norm(s, j, src, dst, stepped, done):
                if j != 2:
                    dve.wait_ge(stepped, s.count(NORM, j))
                if cfg.norm == "ln" and j >= 3:
                    j += 1
                if j == 0:
                    for t in range(QT):
                        ins = dve.bn_stats(st6[:, t, :], src[:, t, :])
                elif j == 1:
                    ins = None
                    dve.sem_inc(stepped, 1)
                elif j == 2:
                    for t in range(QT):
                        ins = dve.bn_aggr(mv[:, t, :], st6[:, t, :])
                elif j == 3:
                    ins = dve.tensor_tensor(sq, mean, mean, ALU.mult)
                elif j == 4:
                    if cfg.norm == "rms":
                        ins = dve.scalar_tensor_tensor(out=v, in0=sq, scalar=cfg.eps, in1=var,
                                                       op0=ALU.add, op1=ALU.add)
                    else:
                        ins = dve.tensor_scalar(v, var, cfg.eps, None, ALU.add)
                elif j == 5:
                    ins = dve.tensor_scalar(r.bitcast(I32), v.bitcast(I32), -0.5, MAGIC, ALU.mult, ALU.add)
                elif j < 15:
                    if j % 3 == 0:
                        ins = dve.scalar_tensor_tensor(out=a, in0=r, scalar=-0.5, in1=v, op0=ALU.mult, op1=ALU.mult)
                    elif j % 3 == 1:
                        ins = dve.tensor_tensor(sq, a, r, ALU.mult)
                    else:
                        ins = dve.scalar_tensor_tensor(out=r, in0=sq, scalar=1.5, in1=r, op0=ALU.add, op1=ALU.mult)
                else:
                    for t in range(QT):
                        rt = nw[:, 1, t:t + 1]
                        if cfg.norm == "rms":
                            ins = dve.tensor_scalar(dst[:, t, :], src[:, t, :], rt, None, ALU.mult)
                        else:
                            ins = dve.tensor_scalar(dst[:, t, :], src[:, t, :], mv[:, t, 0:1], rt,
                                                    ALU.subtract, ALU.mult)
                    ins.then_inc(done, 1)
                    dve.sem_inc(stepped, 1)
                    ins = None
                if ins is not None:
                    ins.then_inc(stepped, 1)

            def tokens_norm(s, j):
                if j == 0:
                    dve.wait_ge(xc_ready, s.count(1, 1))
                norm(s, j, xc, xn, pre_step, xn_ready)

            def tokens_hi(s, _):
                dve.wait_ge(x_full_ready, s.count(X_PARTS, X_PARTS))
                wait_full(dve, s.before(1), A0, cfg.a_uses - 1)
                dve.tensor_copy(x_t[0][:, :, :], x_full[:, :, :]).then_inc(x_hi_ready, 1)

            def queries_terms(s, j):
                if j == 0:
                    dve.wait_ge(q_full_ready, s.count(DC, DC))
                    dve.wait_ge(q_written, s.count(16))
                    dve.tensor_copy(q_term[:, 0, :, :], q_full[:, :, :]).then_inc(q_h, 1)
                elif j == 1:
                    dve.wait_ge(q_h, s.count(1, 1))
                    dve.tensor_tensor(q_rest[:, :, :], q_full[:, :, :], q_term[:, 0, :, :], ALU.subtract)\
                        .then_inc(q_r, 1)
                elif j == 2:
                    dve.wait_ge(q_r, s.count(1, 1))
                    dve.tensor_copy(q_term[:, 1, :, :], q_rest[:, :, :]).then_inc(q_m, 1)
                else:
                    dve.wait_ge(q_m, s.count(1, 1))
                    dve.tensor_tensor(q_term[:, 2, :, :], q_rest[:, :, :], q_term[:, 1, :, :], ALU.subtract)\
                        .then_inc(q_l, 1)

            def values_out(s, _):
                wait_full(dve, s, A0, 3)
                wait_full(dve, s.before(2), O0, G - 1)
                dve.tensor_copy(va[s.par][:, :, :, 0:DH],
                                tile(A0, 3)[:, :].rearrange("p (t h d) -> p t h d", t=QT, h=H)).then_inc(va_ready, 1)

            def maximum(s, n):
                per_tile = H // cfg.spu
                t, h0 = n // per_tile, n % per_tile * cfg.spu
                wait_full(dve, s, S0, n)
                if cfg.mask == "add":
                    if n == 0:
                        dve.wait_ge(masks_loaded[s.par], s.count_par(48, 48))
                    scored = tile(S0, n)[:, :].rearrange("p (h k) -> p h k", k=SC)
                    m = mq[s.par][:, t, :].unsqueeze(1).to_broadcast([P, 8, SC])
                    dve.tensor_tensor(s_tmp[:, n % 2, :, :], scored, m, ALU.add).then_inc(s_masked, 1)
                    dve.wait_ge(s_masked, s.count(cfg.s_uses, n + 1))
                    src = s_tmp[:, n % 2, :, :]
                elif cfg.spu > 1:
                    src = tile(S0, n)[:, :].rearrange("p (h k) -> p h k", k=SC)
                else:
                    src = tile(S0, n)[:, 0:cfg.keys]
                dve.tensor_reduce(peak[:, t, h0:h0 + cfg.spu], src, AX.X, ALU.max).then_inc(peak_done, 1)

            def peaks_terms(s, _):
                dve.wait_ge(peak_done, s.count(cfg.s_uses, cfg.s_uses))
                for t in range(QT):
                    dve.tensor_scalar(neg_peak[:, t, 0, :], peak[:, t, :], -1.0, None, ALU.mult).then_inc(neg_h, 1)
                dve.wait_ge(neg_h, s.count(QT, QT))
                for t in range(QT):
                    dve.scalar_tensor_tensor(out=neg_peak[:, t, 1, :], in0=peak[:, t, :], scalar=-1.0,
                                             in1=neg_peak[:, t, 0, :], op0=ALU.mult, op1=ALU.subtract)\
                        .then_inc(neg_done, 1)

            def peaks_out(s, _):
                b = s.before(1)
                dve.wait_ge(max_loaded[b.par], b.count_par(32, 32))
                for t in range(QT):
                    wait_full(dve, s, S0, NEG0 + t)
                    dve.tensor_copy(peak_t[:, :, t, :], tile(S0, NEG0 + t)[:, :].bitcast(BF16)[0:H, 0:2 * P]
                                    .rearrange("h (a q) -> h a q", a=2)).then_inc(peak_t_ready, 1)

            def mask_transposed(s, g):
                wait_full(dve, s, T0, g)
                dve.wait_ge(exp_done, s.count(cfg.st_uses, g - 1))
                dve.tensor_tensor(st_tmp[:, g % 2, :, :], tile(T0, g)[:, :].rearrange("p (a s) -> p a s", a=2),
                                  mk[s.par][:, :].unsqueeze(1).to_broadcast([P, 2, S]), ALU.add)\
                    .then_inc(st_masked, 1)

            def outputs(s, g):
                wait_full(dve, s, O0, g)
                if g == 0:
                    wait_full(dve, s.before(1), M0, cfg.ot_uses - 1)
                dve.tensor_copy(o_t[:, g, :], tile(O0, g)[:, 0:S]).then_inc(o_t_ready, 1)

            def divide(s, n):
                wait_full(dve, s, M0, n)
                o = tile(M0, n)[:, :].rearrange("p (g t h v) -> p g t h v", g=2, t=QT, v=VW)
                for g in range(2):
                    ins = dve.reciprocal(o_rec[:, n % 2, g, :, :], o[:, g, :, :, ONES])
                ins.then_inc(rec_ready, 1)
                dve.wait_ge(rec_ready, s.count(cfg.ot_uses, n + 1))
                for g in range(2):
                    h0 = 4 * (2 * n + g) * DH
                    ins = dve.tensor_tensor(
                        o_tok[:, :, h0:h0 + 4 * DH].rearrange("p t (h d) -> p t h d", h=4),
                        o[:, g, :, :, 0:DH],
                        o_rec[:, n % 2, g, :, :].unsqueeze(3).to_broadcast([P, QT, 4, DH]), ALU.mult)
                ins.then_inc(o_tok_ready, 1)

            def outputs_hi(s, _):
                dve.wait_ge(o_full_ready, s.count(DC, DC))
                dve.tensor_copy(o_f[0][:, :, :], o_full[:, :, :]).then_inc(o_hi_ready, 1)

            def attended(s, _):
                wait_full(dve, s, M0, M_PROJ)
                dve.wait_ge(xb_ready, s.count(QT, QT))
                if cfg.n == 3:
                    dve.wait_ge(xb2_ready, s.count(QT))
                dve.tensor_tensor(att[:, :, :], tile(M0, M_PROJ)[:, :].rearrange("p (t d) -> p t d", t=QT),
                                  xb[:, :, :], ALU.add).then_inc(att_ready, 1)

            def attended_norm(s, j):
                if j == 0:
                    dve.wait_ge(att_ready, s.count(1, 1))
                norm(s, j, att, y, norm_step, y_ready)

            def gamma(s, _):
                dve.wait_ge(y_ready, s.count(1, 1))
                for t in range(QT):
                    ins = dve.tensor_tensor(att[:, t, :], y[:, t, :], row[:, ROWV["g"], :], ALU.mult)
                ins.then_inc(g_ready, 1)

            def beta(s, _):
                dve.wait_ge(g_ready, s.count(1, 1))
                for t in range(QT):
                    ins = dve.tensor_tensor(x_rows(s, t, 1), att[:, t, :], row[:, ROWV["b"], :], ALU.add)
                ins.then_inc(x_new, 1)

            def norm_hi(s, _):
                dve.wait_ge(y_full_ready, s.count(DC, DC))
                dve.tensor_copy(y_t[0][:, :, :], y_full[:, :, :]).then_inc(y_hi_ready, 1)

            def hidden_hi(s, n):
                dve.wait_ge(h_full_ready, s.count(FC, 2 * n + 2))
                dve.tensor_copy(h_t[0][:, 2 * n:2 * n + 2, :], h_full[:, n % 2, :, :]).then_inc(h_hi_ready, 1)

            def result(s, _):
                wait_full(dve, s, M0, M_OUT)
                dve.wait_ge(xb2_ready, s.count(QT, QT))
                if cfg.n == 3:
                    dve.wait_ge(stored[s.par], s.count_par(16))
                dve.tensor_tensor(y_out[s.par][:, :, :] if cfg.n == 3 else x_rows(s, 0, QT),
                                  tile(M0, M_OUT)[:, :].rearrange("p (t d) -> p t d", t=QT),
                                  xb2[:, :, :], ALU.add).then_inc(x_new, 1)

            does = {("A", "norm"): tokens_norm, ("A", "turn.hi"): tokens_hi, ("A", "q.term"): queries_terms,
                    ("A", "v.out"): values_out, ("S", "max"): maximum, ("S", "neg"): peaks_terms,
                    ("S", "neg.out"): peaks_out, ("O", "out"): outputs,
                    ("M", "divide"): divide, ("M", "back.hi"): outputs_hi, ("M", "proj.out"): attended,
                    ("M", "norm"): attended_norm, ("M", "gamma"): gamma, ("M", "beta"): beta,
                    ("M", "norm.hi"): norm_hi, ("M", "mlp1.hi"): hidden_hi, ("M", "mlp2.out"): result}
            if cfg.mask == "add":
                does["O", "mask"] = mask_transposed
            run(dve, does)

        @block.gpsimd
        def _(pool):
            if cfg.latent:
                for i in range(2):
                    ins = pool.memset(va[i][:, :, :, DH:VW], 1.0)
                ins.then_inc(ones_ready, 1)
            else:
                pool.sem_inc(ones_ready, 1)

            def tokens_lo(s, _):
                pool.wait_ge(x_hi_ready, s.count(1, 1))
                pool.tensor_tensor(x_t[1][:, :, :], x_full[:, :, :], x_t[0][:, :, :].bitcast(F32), ALU.subtract)\
                    .then_inc(x_lo_ready, 1)

            def keys_r(s, _):
                pool.wait_ge(k_h, s.count(1, 1))
                pool.tensor_tensor(k_rest[:, :, :], k_full[:, :, :], k_term[:, 0, :, :], ALU.subtract)\
                    .then_inc(k_r, 1)

            def keys_l(s, _):
                pool.wait_ge(k_m, s.count(1, 1))
                pool.tensor_tensor(k_term[:, 2, :, :], k_rest[:, :, :], k_term[:, 1, :, :], ALU.subtract)\
                    .then_inc(k_l, 1)

            def residual(s, _):
                pool.wait_ge(att_ready, s.count(1))
                pool.sem_inc(xb_free, 1)
                for t in range(QT):
                    pool.tensor_tensor(xb[:, t, :], x_rows(s, t, 1), row[:, ROWV["bo"], :], ALU.add)\
                        .then_inc(xb_ready, 1)

            def outputs_lo(s, _):
                pool.wait_ge(o_hi_ready, s.count(1, 1))
                pool.tensor_tensor(o_f[1][:, :, :], o_full[:, :, :], o_f[0][:, :, :].bitcast(F32),
                                   ALU.subtract).then_inc(o_lo_ready, 1)

            def residual2(s, _):
                pool.wait_ge(x_new, s.count(1))
                if cfg.n == 3:
                    pool.wait_ge(att_ready, s.count(1, 1))
                else:
                    pool.sem_inc(xb2_free, 1)
                for t in range(QT):
                    pool.tensor_tensor(xb2[:, t, :], att[:, t, :] if cfg.n == 3 else x_rows(s, t, 1),
                                       row[:, ROWV["b2"], :], ALU.add).then_inc(xb2_ready, 1)

            def norm_lo(s, _):
                pool.wait_ge(y_hi_ready, s.count(1, 1))
                pool.tensor_tensor(y_t[1][:, :, :], y_full[:, :, :], y_t[0][:, :, :].bitcast(F32),
                                   ALU.subtract).then_inc(y_lo_ready, 1)

            def hidden_lo(s, n):
                pool.wait_ge(h_hi_ready, s.count(4, n + 1))
                pool.tensor_tensor(h_t[1][:, 2 * n:2 * n + 2, :], h_full[:, n % 2, :, :],
                                   h_t[0][:, 2 * n:2 * n + 2, :].bitcast(F32), ALU.subtract)\
                    .then_inc(h_lo_ready, 1)

            does = {("A", "turn.lo"): tokens_lo, ("A", "k.r"): keys_r, ("A", "k.l"): keys_l,
                    ("M", "residual"): residual, ("M", "back.lo"): outputs_lo,
                    ("M", "norm.lo"): norm_lo, ("M", "mlp1.lo"): hidden_lo}
            if cfg.mlp:
                does["M", "residual2"] = residual2
            run(pool, does)

        @block.sync
        def _(sp):
            def of(dram, s):
                return dram[s.index()] if isinstance(s.j, int) else squeeze(dram[bass.ds(s.index(), 1)])

            def squeeze(ap):
                names = "bcde"[:len(ap.shape) - 1]
                first = names[0]
                return ap.rearrange(f"a {' '.join(names)} -> (a {first}) {' '.join(names[1:])}")

            def queries_store(s, _):
                sp.wait_ge(q_l, s.count(1, 1))
                sp.dma_start(of(q_dram, s).rearrange("t (c p) s -> p t c s", p=P), q_term[:, :, :, :])\
                    .then_inc(q_written, 16)

            def keys_store(s, _):
                sp.wait_ge(k_l, s.count(1, 1))
                sp.dma_start(of(k_dram, s)[:, :, 0:S].rearrange("t (c p) s -> p t c s", p=P),
                             k_term[:, :, :, :]).then_inc(k_written, 16)

            def load(s, _):
                wait_full(sp, s.before(2), O0, G - 1)
                loaded = stack_loaded[s.par]
                if cfg.mask == "add":
                    sp.dma_start(mq[s.par][:, :, :], of(mask_q, s).rearrange("(t p) k -> p t k", p=P))\
                        .then_inc(masks_loaded[s.par], 16)
                    for half in range(2):
                        sp.dma_start(mk[s.par][half * SC:(half + 1) * SC, :], of(mask_k, s))\
                            .then_inc(masks_loaded[s.par], 16)
                else:
                    src = mask_dram[s.index():s.index() + 1, :] if isinstance(s.j, int) else \
                        mask_dram[bass.ds(s.index(), 1), :]
                    sp.dma_start(stack_k[s.par][MASK_ROW:MASK_ROW + 1, :, cfg.c0:cfg.c0 + SC],
                                 src.unsqueeze(1).to_broadcast([1, KV, SC])).then_inc(loaded, 16)
                sp.wait_ge(q_written, s.count(16, 16))
                for i, term in enumerate(Q_TERMS):
                    sp.dma_start(stack_q[s.par][ROWS * i:ROWS * i + DH, :, :],
                                 of(q_dram, s)[term].rearrange("(h d) s -> d h s", d=DH)).then_inc(loaded, 16)
                if cfg.latent:
                    sp.wait_ge(k_written, s.count(16, 16))
                for i, term in enumerate(K_TERMS):
                    sp.dma_start(stack_k[s.par][ROWS * i:ROWS * i + DH, :, :],
                                 of(k_dram, s)[term].rearrange("(h d) s -> d h s", d=DH)).then_inc(loaded, 16)

            def peaks_load(s, _):
                sp.wait_ge(peak_t_ready, s.count(QT, QT))
                for a in range(2):
                    sp.dma_start(stack_q[s.par][MAX_ROW + a:MAX_ROW + a + 1, :, :],
                                 peak_t[:, a, :, :].rearrange("h t q -> h (t q)")).then_inc(max_loaded[s.par], 16)

            def store(s, _):
                sp.wait_ge(x_new, s.count(1, 1))
                sp.dma_start(of(out, s).rearrange("(t p) d -> p t d", p=P), y_out[s.par][:, :, :])\
                    .then_inc(stored[s.par], 16)

            does = {("A", "q.store"): queries_store, ("A", "k.store"): keys_store, ("A", "load"): load,
                    ("S", "neg.load"): peaks_load}
            if cfg.n == 3:
                does["M", "store"] = store
            run(sp, does)
            if cfg.n == 3:
                for i in range(2):
                    sp.wait_ge(stored[i], 16 * (B // 2 + 1))
    clear(nc, taken)


def clear(nc, taken):
    with nc.Block() as block:
        @block.sync
        def _(sp):
            for s in taken:
                sp.sem_clear(s)


def prepare(nc, cfg, banks, x_all, ident, ident16, x, ctx_t, w_in, cols_in, rows_in, mask_i, mask_b,
            w_hi, w_lo, col, row, bq_scaled, stack_q, stack_k, v_ctx, va_ctx, k_dram, mask_dram, wgt, rise):
    L = f"L{cfg.n}p_"
    KW = min(P, cfg.kvw)
    KC = cfg.kvw // KW
    with ExitStack() as pre:
        def sb(name, shape, dt=F32):
            return pre.enter_context(nc.sbuf_tensor(L + name, shape, dt))

        taken = []

        def sem(name):
            s = pre.enter_context(nc.semaphore(L + name))
            taken.append(s)
            return s

        raw = sb("raw", [P, cfg.wcols])
        ctx = sb("ctx", [P, DC, B, 2, SC])
        c_t = [sb(f"c_t_{p}", [P, DC, B, 2, SC], F32R) for p in ("hi", "lo")]
        k_full = sb("k_full", [P, KC, B * SC])
        k_rest = sb("k_rest", [P, KC, B * SC])
        k_term = sb("k_term", [P, NTERM, KC, B * SC], BF16)
        m_raw = sb("m_raw", [B, SC], I32 if cfg.mask == "int" else U8)
        m_f = sb("m_f", [B, SC])
        m_z = sb("m_z", [B, SC])
        m_row = sb("m_row", [B, SC], BF16)

        w_loaded, ctx_loaded, small_loaded, mask_loaded, x_loaded = (
            sem(n) for n in ("w_loaded", "ctx_loaded", "small_loaded", "mask_loaded", "x_loaded"))
        w_ready, ctx_ready, ident_zero, ident_ready, fill, fill_k = (
            sem(n) for n in ("w_ready", "ctx_ready", "ident_zero", "ident_ready", "fill", "fill_k"))
        k_done, v_done, k_full_ready, k_part, m_part, written, bq_done, v_read = (
            sem(n) for n in ("k_done", "v_done", "k_full_ready", "k_part", "m_part", "written", "bq_done", "v_read"))
        block = pre.enter_context(nc.Block())

        @block.sync
        def _(sp):
            sp.dma_start(ctx[:, :, :, :, :].rearrange("p c b a s -> p (c b a s)"), ctx_t).then_inc(ctx_loaded, 16)
            sp.dma_start(raw[:, :], w_in).then_inc(w_loaded, 16)
            sp.dma_start(col[:, :], cols_in).then_inc(small_loaded, 16)
            sp.dma_start(row[:, :, :].rearrange("p a d -> p (a d)"),
                         rows_in.rearrange("(o a) d -> o (a d)", o=1).to_broadcast([P, cfg.rowvs * D])).then_inc(small_loaded, 16)
            if cfg.mask != "add":
                sp.dma_start(m_raw[:, :], mask_i if cfg.mask == "int" else mask_b).then_inc(mask_loaded, 16)
            if cfg.n == 0:
                sp.dma_start(x_all[:, :, :], x.rearrange("b (t p) d -> p (b t) d", p=P)).then_inc(x_loaded, 16)
            for s, per in rise.values():
                sp.sem_inc(s, per)
            if cfg.mask != "add":
                sp.wait_ge(m_part, 3)
                sp.dma_start(mask_dram, m_row[:, :]).then_inc(written, 16)
            sp.wait_ge(k_part, 4)
            n = 0
            for t in range(NTERM):
                for c in range(KC):
                    dst = k_dram[:, t, c * KW:(c + 1) * KW, cfg.c0:cfg.c0 + SC].rearrange("b p s -> p b s")
                    sp.dma_start(dst, k_term[0:KW, t, c, :].rearrange("p (b s) -> p b s", b=B)).then_inc(written, 16)
                    n += 1
            sp.wait_ge(written, 16 * (n + (cfg.mask != "add")))
            sp.wait_ge(small_loaded, 32)
            if cfg.n == 0:
                sp.wait_ge(x_loaded, 16)

        @block.gpsimd
        def _(pool):
            if cfg.n == 0:
                pool.memset(ident[:, :], 0.0).then_inc(ident_zero, 1)
                pool.wait_ge(ident_zero, 1)
                pool.affine_select(out=ident[:, :], in_=ident[:, :], compare_op=ALU.not_equal, fill=1.0,
                                   base=0, pattern=[[-1, P]], channel_multiplier=1).then_inc(ident_ready, 1)
                pool.wait_ge(ident_ready, 1)
                pool.tensor_copy(ident16[:, :], ident[:, :]).then_inc(ident_ready, 1)
                pool.wait_ge(ident_ready, 2)
            for i in range(2):
                words = stack_q[i][:, :, :].rearrange("p h s -> p (h s)").bitcast(F32)
                if cfg.dh < ROWS:
                    pool.memset(words[0:MASK_ROW, :], 0.0)
                pool.memset(words[MASK_ROW:P, :], TWO_ONES).then_inc(fill, 1)

        @block.vector
        def _(dve):
            for i in range(2):
                words = stack_k[i][:, :, :].rearrange("p h s -> p (h s)").bitcast(F32)
                if cfg.dh < ROWS:
                    dve.memset(words[0:MASK_ROW, :], 0.0)
                dve.memset(words[MASK_ROW:P, :], TWO_ONES)
                ins = dve.memset(va_ctx[i][:, :, :], 0.0)
            ins.then_inc(fill_k, 1)
            dve.wait_ge(fill_k, 1)
            for i in range(2):
                dve.memset(stack_k[i][MASK_ROW:MASK_ROW + 1, :, :], 0.0)
                for half in range(2):
                    dve.memset(va_ctx[i][half * SC:(half + 1) * SC, half::2, ONES:VW], 1.0)
            dve.wait_ge(ctx_loaded, 16)
            dve.tensor_copy(c_t[0][:, :, :, :, :], ctx[:, :, :, :, :]).then_inc(ctx_ready, 1)
            dve.wait_ge(ctx_ready, 1)
            dve.tensor_tensor(c_t[1][:, :, :, :, :], ctx[:, :, :, :, :], c_t[0][:, :, :, :, :].bitcast(F32),
                              ALU.subtract).then_inc(ctx_ready, 1)
            dve.wait_ge(w_loaded, 16)
            dve.tensor_copy(w_hi[:, :], raw[:, :]).then_inc(w_ready, 1)
            dve.wait_ge(w_ready, 1)
            dve.tensor_tensor(w_lo[:, :], raw[:, :], w_hi[:, :].bitcast(F32), ALU.subtract).then_inc(w_ready, 1)
            dve.wait_ge(small_loaded, 32)
            dve.tensor_scalar(bq_scaled[:, :], col[:, COLS["bq"]:COLS["bq"] + DC], cfg.scale, None, ALU.mult)\
                .then_inc(bq_done, 1)
            if cfg.mask != "add":
                dve.wait_ge(mask_loaded, 16)
                dve.tensor_copy(m_f[:, :], m_raw[:, :]).then_inc(m_part, 1)
                dve.wait_ge(m_part, 1)
                dve.tensor_scalar(m_z[:, :], m_f[:, :], 0.0, None, ALU.is_equal).then_inc(m_part, 1)
                dve.wait_ge(m_part, 2)
                dve.tensor_scalar(m_row[:, :], m_z[:, :], NEG, None, ALU.mult).then_inc(m_part, 1)
            dve.wait_ge(k_full_ready, KC)
            full, rest = k_full[0:KW, :, :], k_rest[0:KW, :, :]
            dve.tensor_copy(k_term[0:KW, 0, :, :], full).then_inc(k_part, 1)
            dve.wait_ge(k_part, 1)
            dve.tensor_tensor(rest, full, k_term[0:KW, 0, :, :], ALU.subtract).then_inc(k_part, 1)
            dve.wait_ge(k_part, 2)
            dve.tensor_copy(k_term[0:KW, 1, :, :], rest).then_inc(k_part, 1)
            dve.wait_ge(k_part, 3)
            dve.tensor_tensor(k_term[0:KW, 2, :, :], rest, k_term[0:KW, 1, :, :], ALU.subtract).then_inc(k_part, 1)
            for i in range(B // 2):
                dve.wait_ge(v_done, i + 1)
                dve.tensor_copy(v_ctx[:, 2 * i:2 * i + 2, :],
                                banks[2 + i][:, 0:2 * cfg.kvw].rearrange("p (b c) -> p b c", b=2)).then_inc(v_read, 1)

        @block.tensor
        def _(pe):
            pe.wait_ge(ctx_ready, 2)
            pe.wait_ge(w_ready, 2)

            def passes(dst, lhs, rhs):
                for k in range(DC):
                    for i, (a, b) in enumerate(((0, 0), (0, 1), (1, 0))):
                        last = pe.matmul(dst, lhs(a, k), rhs(b, k), start=(k == 0 and i == 0),
                                         stop=(k == DC - 1 and i == 2))
                return last

            kn, vn, v0 = ("k", "v", 0) if cfg.kvw == D else ("kv", "kv", SC)
            w = (w_hi, w_lo)
            for c in range(KC):
                passes(banks[c][:, :], lambda a, k: wgt(w[a], kn, k, c * P, P),
                       lambda b, k: c_t[b][:, k, :, 0, :]).then_inc(k_done, 1)
            for b2 in range(B // 2):
                for i in range(2):
                    last = passes(banks[2 + b2][:, i * cfg.kvw:(i + 1) * cfg.kvw],
                                  lambda a, k: c_t[a][:, k, 2 * b2 + i, :, :].rearrange("p a s -> p (a s)"),
                                  lambda b, k: wgt(w[b], vn, k, v0, cfg.kvw))
                last.then_inc(v_done, 1)

        @block.scalar
        def _(act):
            act.wait_ge(small_loaded, 32)
            for c in range(KC):
                act.wait_ge(k_done, c + 1)
                act.activation(k_full[0:KW, c, :], banks[c][0:KW, :], ACT.Identity,
                               bias=col[0:KW, COLS["bk"] + c:COLS["bk"] + c + 1]).then_inc(k_full_ready, 1)
    clear(nc, taken)


def kernel(**inputs):
    import numpy as np
    import concourse.bacc as bacc
    from concourse.bass_utils import run_bass_kernel_spmd

    def a(name):
        return np.asarray(inputs[name])

    def chunks(m):
        return m.reshape(m.shape[0] // P, P, m.shape[1]).transpose(1, 0, 2).reshape(P, -1)

    def features(*vectors):
        t = np.zeros((P, NCOLS), np.float32)
        for name, v in vectors:
            v = v.reshape(-1, min(P, v.size)).T
            t[:v.shape[0], COLS[name]:COLS[name] + v.shape[1]] = v
        return t

    def rowvecs(*vectors):
        return np.stack([v for _, v in sorted(vectors, key=lambda x: ROWV[x[0]])])

    arrays = {}
    g = {n: a("L0_xattn_" + n) for n in ("Wq", "bq", "Wk", "bk", "Wv", "bv", "Wo", "bo", "gamma", "beta")}
    kv = np.concatenate([g["Wk"], g["Wv"]], axis=1)
    arrays["w0"] = np.concatenate([chunks(m) for m in (g["Wq"], kv, g["Wo"])], axis=1)
    bv = np.broadcast_to(g["bv"].reshape(8, 1, 8), (8, 4, 8)).reshape(-1)
    arrays["cols0"] = features(("bq", g["bq"]), ("bk", g["bk"]), ("bv", bv))
    arrays["rows0"] = rowvecs(("bo", g["bo"]), ("g", g["gamma"]), ("b", g["beta"]))
    for n in (1, 2):
        g = {m: a(f"L{n}_xattn_{m}") for m in ("q_w", "q_b", "kv_w", "kv_b", "out_w", "out_b", "postnorm_w",
                                               "mlp_w1", "mlp_b1", "mlp_w2", "mlp_b2")}
        arrays[f"w{n}"] = np.concatenate([chunks(m) for m in (
            g["q_w"], g["kv_w"][:, 0::2], g["kv_w"][:, 1::2], g["out_w"], g["mlp_w1"], g["mlp_w2"])], axis=1)
        arrays[f"cols{n}"] = features(("bq", g["q_b"]), ("bk", g["kv_b"][0::2]), ("bv", g["kv_b"][1::2]),
                                      ("n_w", g["postnorm_w"]), ("b1", g["mlp_b1"]))
        arrays[f"rows{n}"] = rowvecs(("bo", g["out_b"]), ("b2", g["mlp_b2"]))
    g = {m: a(f"L3_xattn_{m}") for m in ("ln1_w", "ln1_b", "q_w", "q_b", "k_w", "k_b", "v_w", "v_b", "cproj_w",
                                         "cproj_b", "ln2_w", "ln2_b", "fc_w", "fc_b", "proj_w", "proj_b")}
    arrays["w3"] = np.concatenate([chunks(m) for m in (
        g["q_w"], g["k_w"], g["v_w"], g["cproj_w"], g["fc_w"], g["proj_w"])], axis=1)
    arrays["cols3"] = features(("bq", g["q_b"]), ("bk", g["k_b"]), ("bv", g["v_b"]), ("n_w", g["ln2_w"]),
                               ("n_b", g["ln2_b"]), ("p_w", g["ln1_w"]), ("p_b", g["ln1_b"]), ("b1", g["fc_b"]))
    arrays["rows3"] = rowvecs(("bo", g["cproj_b"]), ("b2", g["proj_b"]))
    arrays["x"] = a("x")
    ctx = a("ctx_2048").transpose(2, 0, 1).reshape(DC, P, B, 1, SC)
    arrays["ctx_t"] = np.broadcast_to(ctx, (DC, P, B, 2, SC)).transpose(1, 0, 2, 3, 4).reshape(P, -1)
    mask = a("mask_Bx1xSxS2_ff0").reshape(B, S, SC)
    arrays["mask_q"] = mask
    arrays["mask_k"] = mask.transpose(0, 2, 1)
    arrays["mask_i"] = a("mask_BxS2_ik0")
    arrays["mask_b"] = a("mask_BxS2_bf1").view(np.uint8)

    nc = bacc.Bacc("TRN2", target_bir_lowering=False, num_devices=1)
    arrays = {name: np.ascontiguousarray(v) for name, v in arrays.items()}
    aps = {name: nc.dram_tensor("in_" + name, v.shape, mybir.dt.from_np(v.dtype), kind="ExternalInput").ap()
           for name, v in arrays.items()}
    out = nc.dram_tensor("out_0", (B, S, D), F32, kind="ExternalOutput").ap()
    program(nc, aps["x"], aps["ctx_t"], [aps[f"w{n}"] for n in range(4)], [aps[f"cols{n}"] for n in range(4)],
            [aps[f"rows{n}"] for n in range(4)], aps["mask_q"], aps["mask_k"], aps["mask_i"], aps["mask_b"], out)
    r = run_bass_kernel_spmd(nc, [{"in_" + name: v for name, v in arrays.items()}], core_ids=[0])
    return r.results[0]["out_0"]
```

```python
from contextlib import ExitStack

import concourse.bass as bass
from concourse import mybir

F32 = mybir.dt.float32
F32R = mybir.dt.float32r
BF16 = mybir.dt.bfloat16
I32 = mybir.dt.int32
U8 = mybir.dt.uint8
ACT = mybir.ActivationFunctionType
ALU = mybir.AluOpType
AX = mybir.AxisListType

P = 128
B = 8
S = 256
SC = 64
D = 256
DC = D // P
QT = S // P
FF = 4 * D
FC = FF // P
NTERM = 3
Q_TERMS = (0, 1, 2, 0, 1, 0)
K_TERMS = (0, 0, 0, 1, 1, 2)
Q_RUNS = ((0, 3), (3, 2), (5, 1))
K_RUNS = ((0, 3, 0), (3, 2, 1), (5, 1, 2))
MASK_ROW = 96
MAX_ROW = 97
KS = MASK_ROW + 1
KST = MAX_ROW + 2
NEG = -1.0e30
VW = 32
ONES = 16
MAGIC = float(0x5F3759DF)
TWO_ONES = (0x3F803F80 & 0x7FFFFF | 0x800000) / 2.0 ** 23


class Cfg:

    def __init__(self, n, heads, kvheads, latent, scale, norm, eps, mlp, pre_norm, mask):
        self.n, self.heads, self.kvheads, self.latent = n, heads, kvheads, latent
        self.scale, self.norm, self.eps, self.mlp = scale, norm, eps, mlp
        self.pre_norm, self.mask = pre_norm, mask
        self.dh = D // heads
        self.kvw = kvheads * self.dh
        self.kp = min(P, self.kvw)
        self.kc = self.kvw // self.kp
        self.keys = S + SC if latent else SC
        self.c0 = S if latent else 0
        self.groups = heads // 4
        self.rowvs = 2 if mlp else 3
        self.x_parts = DC if pre_norm else 1
        self.spu = 1 if latent else 8
        self.st_group = 5 if latent else 1
        self.s_uses = QT * heads // self.spu
        self.st_uses = self.st_group * self.groups
        self.ot_uses = self.groups // 2
        self.norm_steps = 15 if norm == "ln" else 16
        self.stack_dmas = len(Q_RUNS) + len(K_RUNS) + 1
        self.a_use = {name: i for i, name in enumerate(
            ["ctx k", "x", "q"] + (["k", "v"] if latent else []) + ["ctx v"])}
        self.m_back = self.ot_uses
        self.m_proj, self.m_nt, self.m_h, self.m_out = (self.m_back + i for i in (1, 2, 3, 7))
        self.uses = {S0: self.s_uses + QT, T0: self.st_uses, O0: self.groups, A0: len(self.a_use),
                     M0: self.ot_uses + 2 + (6 if mlp else 0)}
        self.width = {"q": D, "k": self.kvw, "v": self.kvw, "o": D}
        if mlp:
            self.width.update(w1=FF, w2=D)


S0, T0, O0, A0, M0 = 0, 2, 4, 5, 6
RING = {S0: 2, T0: 2, O0: 1, A0: 1, M0: 2}

LAYERS = [
    Cfg(0, 32, 8, False, 8 ** -0.5, "ln", 1e-6, False, False, "add"),
    Cfg(1, 16, 16, True, 1 / 16, "rms", 1e-6, True, False, "int"),
    Cfg(2, 16, 16, True, 1 / 16, "rms", 1e-6, True, False, "int"),
    Cfg(3, 16, 16, False, 0.25, "ln", 1e-5, True, True, "bool"),
]
W_CHUNKS = {"q": DC, "k": DC, "v": DC, "o": DC, "w1": DC, "w2": FC}
W_AT = {"q": 0, "k": 2 * D, "v": 4 * D, "o": 6 * D, "w1": 8 * D, "w2": 8 * D + DC * FF}
W_COLS = 8 * D + DC * FF + FC * D
W_RING = 3
W_PIECES = {"q": 1, "k": 1, "v": 1, "o": 1, "w1": 4, "w2": 4}
COLS = {"bq": 0, "bk": 2, "bv": 4, "n_w": 6, "n_b": 8, "p_w": 10, "p_b": 12, "b1": 14}
NCOLS = 22
ROWV = {"bo": 0, "b2": 1, "g": 1, "b": 2}
AHEAD = {"A": 2, "S": 1, "O": 0, "M": -1}
ALL = "all"


TIMES = {
    "A tokens":       (  1.24,  -0.61,   3.31),
    "A ctx":          (  0.08,  -6.08,   2.33),
    "A ctx.hi":       (  1.37,   2.27,   3.31),
    "A ctx.lo":       (  3.12,   3.01,   7.44),
    "A ctx k":        (  4.90,   4.45,   8.23),
    "A ctx k.act":    (  5.50,   5.29,   6.99),
    "A norm":         (  4.34,   8.79,   6.43),
    "A norm+":        (  0.22,   0.27,   0.40),
    "A turn":         (  7.03,   6.76,  13.71),
    "A turn.act":     (  9.28,   7.96,  14.72),
    "A turn.hi":      ( 10.73,   9.38,  15.02),
    "A turn.lo":      (  8.99,   8.93,  14.10),
    "A q":            ( 12.90,  11.64,  17.74),
    "A q.act":        ( 13.81,  12.17,  18.22),
    "A q.term":       ( 14.95,  14.09,  20.65),
    "A q.store":      ( 15.03,  16.26,  21.09),
    "A q.store+":     (  1.32,   1.39,   0.55),
    "A q.term+":      (  0.65,   0.48,   0.60),
    "A k":            (  2.62,  14.14,  14.57),
    "A k.act":        ( 12.93,  15.09,  12.43),
    "A v":            ( 24.46,  22.93,  23.84),
    "A v.out":        ( 29.22,  25.08,  29.52),
    "A k.h":          (  6.23,  15.73,   8.85),
    "A k.r":          (  7.10,  17.63,   9.88),
    "A k.m":          (  7.57,  22.10,  11.98),
    "A k.l":          ( 11.60,  19.50,  11.60),
    "A k.store":      (  6.62,  16.74,  11.00),
    "A k.store+":     (  4.08,   0.54,   1.13),
    "A load":         ( 28.95,  22.46,  29.68),
    "A ctx v":        ( 32.40,  27.58,  35.13),
    "A ctx v.act":    ( 36.84,  39.57,  35.02),
    "S score":        (  1.40,  -0.99,   0.92),
    "S score+":       (  3.88,   0.97,   7.75),
    "S max":          (  4.68,   0.18,   3.26),
    "S neg":          ( 37.20,  32.04,  28.01),
    "S neg.turn":     ( 34.64,  30.78,  29.41),
    "S neg.out":      ( 50.47,  33.25,  29.68),
    "S neg.load":     ( 44.77,  29.84,  30.57),
    "O group+":       (  2.10,   4.20,   4.80),
    "O st":           (  2.40,   3.03,   4.71),
    "O st+":          (  0.53,   0.80,   0.93),
    "O mask":         (  3.16,  -4.97,  -0.64),
    "O exp":          (  3.79,   3.74,   5.37),
    "O values":       (  6.38,   8.69,   7.76),
    "O out":          (  7.07,  11.69,  10.72),
    "M again":        ( -3.02,   2.84,  -2.52),
    "M residual":     (  2.24,   4.45,   4.37),
    "M divide.turn":  ( -1.05,  -5.25,  -2.36),
    "M divide.turn+": (  0.27,   0.47,   0.60),
    "M divide":       ( -7.25,  -4.14,  -3.15),
    "M back":         (  2.34,   1.75,   5.17),
    "M back.act":     ( -4.04,   3.15,   0.11),
    "M back.hi":      (  3.38,   3.21,  -0.42),
    "M back.lo":      (  4.92,   3.55,  -2.20),
    "M proj":         (  7.95,   5.18,   5.94),
    "M proj.out":     (  9.10,   6.47,   7.75),
    "M residual2":    (  7.82,   3.41,  11.15),
    "M norm":         ( 12.09,   7.69,   8.73),
    "M norm+":        (  0.43,   0.47,   0.34),
    "M norm.turn":    ( 22.50,  16.24,  15.91),
    "M norm.act":     ( 16.43,  16.22,  18.03),
    "M norm.hi":      ( 20.01,  17.06,  15.99),
    "M norm.lo":      ( 18.14,  16.69,  15.08),
    "M mlp1":         ( 24.82,  20.31,  20.03),
    "M mlp1+":        (  1.06,   1.68,   1.73),
    "M mlp1.act":     ( 18.09,  23.16,  26.46),
    "M mlp1.hi":      ( 16.45,  23.30,  23.33),
    "M mlp1.lo":      ( 31.81,  28.04,  32.69),
    "M mlp2":         ( 29.81,  29.02,  30.25),
    "M mlp2+":        (  1.34,   0.62,   0.49),
    "M mlp2.out":     ( 30.81,  34.00,  33.11),
    "M store":        ( 18.45,  33.27,  35.31),
    "M gamma":        ( 18.81,  18.92,  17.36),
    "M beta":         ( 21.46,  25.55,  18.77),
}


def timetable(cfg):
    steps = []
    time = {name: times[{0: 0, 1: 1, 2: 1, 3: 2}[cfg.n]] for name, times in TIMES.items()}

    time["M residual2"] = max(time["M residual2"], time["M residual"] + 0.01)

    def put(stage, unit, n=0, at=None):
        at = time[stage + " " + unit] if at is None else at
        steps.append((at, len(steps), stage, unit, n))

    def chain(stage, *units):
        for unit in units:
            put(stage, unit)

    def repeat(stage, unit, count, pitch=None):
        pitch = time[f"{stage} {pitch or unit}+"]
        for n in range(count):
            put(stage, unit, n, time[stage + " " + unit] + pitch * n)

    chain("A", "tokens", "ctx", "ctx.hi", "ctx.lo", "ctx k", "ctx k.act")
    if cfg.pre_norm:
        repeat("A", "norm", cfg.norm_steps)
    chain("A", "turn", "turn.act", "turn.hi", "turn.lo", "q", "q.act")
    repeat("A", "q.term", 4)
    repeat("A", "q.store", NTERM)
    if cfg.latent:
        chain("A", "k", "k.act", "v", "v.out")
    repeat("A", "k.store", NTERM)
    chain("A", "k.h", "k.r", "k.m", "k.l", "load", "ctx v", "ctx v.act")
    repeat("S", "score", cfg.s_uses)
    repeat("S", "max", cfg.s_uses, "score")
    chain("S", "neg", "neg.turn", "neg.out", "neg.load")
    for g in range(cfg.groups):
        base = time["O group+"] * g
        for i in range(cfg.st_group):
            for unit in ("st", "mask", "exp"):
                put("O", unit, cfg.st_group * g + i, time["O " + unit] + base + time["O st+"] * i)
        for unit in ("values", "out"):
            put("O", unit, g, time["O " + unit] + base)
    chain("M", "again", "residual")
    repeat("M", "divide.turn", cfg.ot_uses)
    repeat("M", "divide", cfg.ot_uses, "divide.turn")
    chain("M", "back", "back.act", "back.hi", "back.lo", "proj", "proj.out", "residual2")
    repeat("M", "norm", cfg.norm_steps)
    if cfg.mlp:
        chain("M", "norm.turn", "norm.act", "norm.hi", "norm.lo")
        for unit in ("mlp1", "mlp1.act", "mlp1.hi", "mlp1.lo"):
            repeat("M", unit, 4, "mlp1")
        repeat("M", "mlp2", 4 * QT)
        chain("M", "mlp2.out")
    else:
        chain("M", "gamma", "beta")
    chain("M", "store")
    return steps


def weight_steps(cfg, k):
    steps = []

    def put(at, unit, n):
        steps.append((at, 1000 + len(steps), "W", unit, n))

    if k == -2:
        if cfg.n == 0:
            put(0.0, "fill", 0)
            put(29.5, "fill", 1)
            for n in range(2):
                put(12.0 + 3 * n, "fill.values", n)
                put(19.0 + n, "fill.sums", n)
        pieces = [("k", 0, -2.0, 3.0), ("q", 0, -1.9, 4.5), ("v", 0, -1.8, 8.5)]
    elif k == 0:
        pieces = [("o", 0, 12.0, 19.0)]
        put(33.99, "rows", 0)
    elif k == 1 and cfg.mlp:
        pieces = [(name, i, 0.3 + 2.0 * (n + i), 3.3 + 2.0 * (n + i)) for name, n in (("w1", 0), ("w2", 4))
                  for i in range(4)]
    else:
        pieces = []
    for name, i, loaded, split in pieces:
        put(loaded, "load", (name, i))
        put(split, "hi", (name, i))
        put(split + 0.4, "lo", (name, i))
    return steps


class Seq:

    def __init__(self, layer, j, k):
        if isinstance(j, int):
            layer, k = layer + k // B, k % B
        self.layer, self.j, self.k, self.par = layer, j, k, k % 2
        self.cfg = LAYERS[layer] if 0 <= layer < len(LAYERS) else None
        self.first = isinstance(j, int) and k == 0

    def index(self):
        return self.k if isinstance(self.j, int) else self.j * 2 + self.k

    def before(self, n):
        return Seq(self.layer, self.j, self.k - n)


RISES = {}


def after(sem, s, more=0):
    if s.cfg is None:
        return 1
    rises, paired = RISES[sem]
    step = 2 if paired else 1
    per = rises[s.layer]
    c = 1 + sum(r * B // step for r in rises[:s.layer]) + per * (s.k // step) + (per if more == ALL else more)
    return max(c, 1) if isinstance(s.j, int) else s.j * (per * 2 // step) + c


def slot(stage, n):
    return stage + n % RING[stage]


def program(nc, x, ctx_t, w, cols, rows, mask_q, mask_k, mask_i, mask_b, out):
    RISES.clear()
    with ExitStack() as mem:
        def sb(name, shape, dt=F32):
            return mem.enter_context(nc.sbuf_tensor(name, shape, dt))

        def sem(name):
            return mem.enter_context(nc.semaphore(name))

        def add(name, per, is_paired):
            s = sem(name)
            RISES[s] = ([per(c) if callable(per) else per for c in LAYERS], is_paired)
            return s

        def counted(name, per=1):
            return add(name, per, False)

        def paired(name, per):
            return [add(name + str(i), per, True) for i in range(2)]

        H_MAX = max(c.heads for c in LAYERS)
        KEYS = S + SC
        ident = sb("ident", [P, P])
        ident16 = sb("ident16", [P, P], BF16)
        banks = [mem.enter_context(nc.psum_tensor(f"bank{i}", [P, 512], F32)) for i in range(8)]
        w_hi = sb("w_hi", [P, W_COLS], F32R)
        w_lo = sb("w_lo", [P, W_COLS], F32R)
        fill_words = sb("fill_words", [P, 2])
        w_raw = [sb(f"w_raw{i}", [P, 2 * D]) for i in range(W_RING)]
        col = sb("col", [P, len(LAYERS), NCOLS])
        row = sb("row", [P, 3, D])
        bq_scaled = sb("bq_scaled", [P, len(LAYERS), DC])
        c_raw = sb("c_raw", [P, DC, SC])
        c_t = [sb(f"c_t_{p}", [P, DC, 2, SC], F32R) for p in ("hi", "lo")]
        STACK = max(c.heads * S + c.kvheads * c.keys for c in LAYERS)
        stacks = [sb(f"stacks{i}", [P, STACK], BF16) for i in range(2)]
        va_ctx = [sb(f"va_ctx{i}", [P, H_MAX, VW]) for i in range(2)]
        va = [sb(f"va{i}", [P, QT, 16, VW]) for i in range(2)]
        xc = sb("xc", [P, QT, D])
        xr = sb("xr", [P, QT, D])
        xb = sb("xb", [P, QT, D])
        xb2 = sb("xb2", [P, QT, D])
        xn = sb("xn", [P, QT, D])
        x_t = [sb(f"x_t_{p}", [P, DC, S], F32R) for p in ("hi", "lo")]
        x_full = sb("x_full", [P, DC, S])
        q_full = x_full
        q_rest = sb("q_rest", [P, DC, S])
        q_term = sb("q_term", [P, NTERM, DC, S], BF16)
        k_full = sb("k_full", [P, DC, KEYS])
        k_rest = sb("k_rest", [P, DC, KEYS])
        k_term = sb("k_term", [P, NTERM, DC, KEYS], BF16)
        p_lat = sb("p_lat", [P, 6, QT, S])
        p_ctx = sb("p_ctx", [P, 2, 2, S])
        peak = sb("peak", [P, QT, H_MAX])
        neg_peak = sb("neg_peak", [P, QT, 2, H_MAX], BF16)
        peak_t = sb("peak_t", [H_MAX, 2, QT, P], BF16)
        o_t = sb("o_t", [P, H_MAX // 4, S])
        o_rec = sb("o_rec", [P, 2, 2, QT, 4])
        o_tok = sb("o_tok", [P, QT, D])
        o_full = sb("o_full", [P, DC, S])
        o_f = [sb(f"o_f_{p}", [P, DC, S], F32R) for p in ("hi", "lo")]
        att = sb("att", [P, QT, D])
        y = o_tok
        y_full = o_full
        y_t = [sb(f"y_t_{p}", [P, DC, S], F32R) for p in ("hi", "lo")]
        h_full = sb("h_full", [P, 2, 2, S])
        h_t = [sb(f"h_t_{p}", [P, FC, S], F32R) for p in ("hi", "lo")]
        y_out = [sb(f"y_out{i}", [P, QT, D]) for i in range(2)]
        small = {stage: (sb(f"st6_{stage}", [P, QT, 6]), sb(f"mv_{stage}", [P, QT, 2]), sb(f"nw_{stage}", [P, 4, QT]))
                 for stage in "AM"}
        spare = p_lat[:, :, :, :].rearrange("p a t s -> p (a t s)")
        s_tmp = spare[:, 0:2 * 8 * SC].rearrange("p (a h k) -> p a h k", a=2, h=8)
        st_tmp = spare[:, 4 * S:8 * S].rearrange("p (g a s) -> p g a s", g=2, a=2)
        mk = [spare[:, (8 + i) * S:(9 + i) * S] for i in range(2)]
        mq = [spare[:, 10 * S + i * QT * SC:10 * S + (i + 1) * QT * SC].rearrange("p (t k) -> p t k", t=QT)
              for i in range(2)]
        spare = att[0:B, :, :].rearrange("p t d -> p (t d)")
        m_raw = spare[:, 0:SC].bitcast(I32)
        m_raw8 = spare[:, SC:SC + SC // 4].bitcast(U8)
        m_f = spare[:, 2 * SC:4 * SC].rearrange("p (a k) -> p a k", a=2)
        m_z = spare[:, 4 * SC:6 * SC].rearrange("p (a k) -> p a k", a=2)
        m_row = xb[0:B, :, :].rearrange("p t d -> p (t d)")[:, 0:KEYS].bitcast(BF16).rearrange("p (a k) -> p a k", a=2)

        NL = len(LAYERS)
        q_dram = [nc.dram_tensor(f"q_terms{c.n}", (B, NTERM, c.dh, c.heads, S), BF16, kind="Internal").ap()
                  for c in LAYERS]
        k_dram = [nc.dram_tensor(f"k_terms{c.n}", (B, NTERM, c.dh, c.kvheads, c.keys), BF16, kind="Internal").ap()
                  for c in LAYERS]
        x_dram = [x] + [nc.dram_tensor(f"x_in{n}", (B, S, D), F32, kind="Internal").ap()
                        for n in range(1, NL)] + [out]
        mask_dram = nc.dram_tensor("mask_rows", (2, B, KEYS), BF16, kind="Internal").ap()

        bank_full = [counted(f"bank_full{f + i}", lambda c, f=f, i=i: len(range(i, c.uses[f], RING[f])))
                     for f in RING for i in range(RING[f])]
        xc_loaded, xr_loaded, xn_ready = counted("xc_loaded", 16), counted("xr_loaded", 16), counted(
            "xn_ready", lambda c: int(c.pre_norm))
        x_full_ready = counted("x_full_ready", lambda c: c.x_parts)
        x_hi_ready, x_lo_ready = counted("x_hi_ready"), counted("x_lo_ready")
        q_full_ready, q_h, q_r, q_m, q_l = counted("q_full_ready", DC), *map(counted, ("q_h", "q_r", "q_m", "q_l"))
        k_full_ready = counted("k_full_ready", lambda c: DC * c.latent)
        ctx_k_ready = counted("ctx_k_ready", lambda c: c.kc)
        k_h, k_r, k_m, k_l = map(counted, ("k_h", "k_r", "k_m", "k_l"))
        va_ready, va_ctx_ready = counted("va_ready", lambda c: int(c.latent)), counted("va_ctx_ready", 2)
        q_written, k_written = counted("q_written", 16 * NTERM * DC), counted(
            "k_written", lambda c: 16 * NTERM * c.kc)
        stack_loaded = paired("stack_loaded", lambda c: 16 * c.stack_dmas)
        masks_loaded = paired("masks_loaded", lambda c: 48 * (c.mask == "add"))
        max_loaded = paired("max_loaded", 32)
        s_masked = counted("s_masked", lambda c: c.s_uses * (c.mask == "add"))
        peak_done = counted("peak_done", lambda c: c.s_uses)
        neg_h, neg_done, peak_t_ready = counted("neg_h", QT), counted("neg_done", QT), counted("peak_t_ready", QT)
        st_masked = counted("st_masked", lambda c: c.st_uses * (c.mask == "add"))
        exp_done = counted("exp_done", lambda c: c.st_uses)
        o_t_ready = counted("o_t_ready", lambda c: c.groups)
        rec_ready, o_tok_ready = (counted(n, lambda c: c.ot_uses) for n in ("rec_ready", "o_tok_ready"))
        o_full_ready, o_hi_ready, o_lo_ready = counted("o_full_ready", DC), counted("o_hi_ready"), counted("o_lo_ready")
        xb_ready, xb2_ready = counted("xb_ready", QT), counted("xb2_ready", lambda c: QT * c.mlp)
        att_ready, y_ready = counted("att_ready"), counted("y_ready")
        y_full_ready = counted("y_full_ready", lambda c: DC * c.mlp)
        y_hi_ready, y_lo_ready = (counted(n, lambda c: int(c.mlp)) for n in ("y_hi_ready", "y_lo_ready"))
        h_full_ready = counted("h_full_ready", lambda c: FC * c.mlp)
        h_hi_ready, h_lo_ready = (counted(n, lambda c: 4 * c.mlp) for n in ("h_hi_ready", "h_lo_ready"))
        g_ready, x_new = counted("g_ready", lambda c: int(not c.mlp)), counted("x_new")
        norm_step = counted("norm_step", lambda c: c.norm_steps)
        pre_step = counted("pre_step", lambda c: c.norm_steps * c.pre_norm)
        stored = paired("stored", 16)
        w_loaded = [sem(f"w_loaded{i}") for i in range(W_RING)]
        w_hi_ready, w_lo_ready = sem("w_hi_ready"), sem("w_lo_ready")
        rows_loaded, small_loaded, mask_loaded, mask_part, mask_written = (
            sem(n) for n in ("rows_loaded", "small_loaded", "mask_loaded", "mask_part", "mask_written"))
        ctx_loaded, c_hi_ready, c_lo_ready = counted("ctx_loaded", 16), counted("c_hi_ready"), counted("c_lo_ready")
        x_there = sem("x_there")
        bq_done, ident_zero, ident_ready, filled, va_filled, va_zero, fill_words_ready, old_max_gone = (
            sem(n) for n in ("bq_done", "ident_zero", "ident_ready", "filled",
                             "va_filled", "va_zero", "fill_words_ready", "old_max_gone"))

        w_order = [(c.n, name, i) for c in LAYERS for name in ("k", "q", "v", "o", "w1", "w2") if name in c.width
                   for i in range(W_PIECES[name])]

        def nth(cfg, name, i):
            return w_order.index((cfg.n, name, i))

        def wgt(cfg, part, name, k, c0=0, n=None):
            at = W_AT[name] + k * cfg.width[name] + c0
            return part[:, at:at + (n or cfg.width[name])]

        def piece(cfg, part, name, i):
            n = W_CHUNKS[name] * cfg.width[name] // W_PIECES[name]
            return part[:, W_AT[name] + i * n:W_AT[name] + (i + 1) * n]

        def key_part(cfg, buf):
            return buf[0:cfg.kp, 0:cfg.kc, 0:cfg.keys]

        def stack_q(s):
            return stacks[s.par][:, 0:s.cfg.heads * S].rearrange("p (h q) -> p h q", q=S)

        def stack_k(s):
            at, keys = s.cfg.heads * S, s.cfg.keys
            return stacks[s.par][:, at:at + s.cfg.kvheads * keys].rearrange("p (h k) -> p h k", k=keys)

        def read_out(cfg, stage, n):
            if stage == A0:
                return {cfg.a_use["ctx k"]: (ctx_k_ready, ALL), cfg.a_use["x"]: (x_full_ready, ALL),
                        cfg.a_use["q"]: (q_full_ready, ALL), cfg.a_use.get("k"): (k_full_ready, ALL),
                        cfg.a_use.get("v"): (va_ready, ALL), cfg.a_use["ctx v"]: (va_ctx_ready, ALL)}[n]
            if stage == O0:
                return o_t_ready, n + 1
            if stage == S0:
                if n < cfg.s_uses:
                    return (s_masked if cfg.mask == "add" else peak_done), n + 1
                return peak_t_ready, n - cfg.s_uses + 1
            if stage == T0:
                return (st_masked if cfg.mask == "add" else exp_done), n + 1
            if n < cfg.m_back:
                return o_tok_ready, n + 1
            if n == cfg.m_back:
                return o_full_ready, ALL
            if n == cfg.m_proj:
                return att_ready, ALL
            if n == cfg.m_nt:
                return y_full_ready, ALL
            if n < cfg.m_out:
                return h_full_ready, 2 * (n - cfg.m_h + 1)
            return x_new, ALL

        def tile(stage, n):
            return banks[slot(stage, n)]

        def wait_free(eng, s, stage, n):
            before = n - RING[stage]
            if before < 0:
                s = s.before(1)
                if s.cfg is None:
                    return
                before = max(m for m in range(s.cfg.uses[stage]) if slot(stage, m) == slot(stage, n))
            which, count = read_out(s.cfg, stage, before)
            eng.wait_ge(which, after(which, s, count))

        def wait_full(eng, s, stage, n):
            if s.cfg is None:
                return
            if n < 0:
                n += s.cfg.uses[stage]
            eng.wait_ge(bank_full[slot(stage, n)], after(bank_full[slot(stage, n)], s, n // RING[stage] + 1))

        def run(eng, does):
            def turn(layer, j, k):
                steps = []
                for stage, ahead in AHEAD.items():
                    s = Seq(layer, j, k + ahead)
                    if s.cfg is not None:
                        steps += [(step, s) for step in timetable(s.cfg) if step[2] == stage]
                if isinstance(j, int):
                    for cfg in LAYERS:
                        steps += [(step, Seq(cfg.n, 0, 0)) for step in weight_steps(cfg, layer * B + k - cfg.n * B)]
                for (_, _, stage, unit, n), s in sorted(steps, key=lambda e: e[0][:3]):
                    if (stage, unit) in does:
                        does[stage, unit](s, n)

            turn(0, 0, -2)
            turn(0, 0, -1)
            for layer in range(NL):
                turn(layer, 0, 0)
                turn(layer, 0, 1)
                with eng.Fori(0, 2) as j:
                    turn(layer, j, 2)
                    turn(layer, j, 3)
                turn(layer, 0, 6)
                turn(layer, 0, 7)
            turn(NL, 0, 0)

        block = mem.enter_context(nc.Block())

        @block.tensor
        def _(pe):
            def mm3(dst, a, b, first, last):
                pe.matmul(dst, a[0], b[0], start=first, stop=False)
                pe.matmul(dst, a[0], b[1], start=False, stop=False)
                return pe.matmul(dst, a[1], b[0], start=False, stop=last)

            def weight_wait(s, name):
                if s.first:
                    pe.wait_ge(w_lo_ready, nth(s.cfg, name, W_PIECES[name] - 1) + 1)

            def feature_major(cfg, bank, name, c0, act):
                for i in range(2):
                    for k in range(DC):
                        c = c0 + i * P
                        last = mm3(bank[:, i * S:(i + 1) * S],
                                   (wgt(cfg, w_hi, name, k, c, P), wgt(cfg, w_lo, name, k, c, P)),
                                   (act[0][:, k, :], act[1][:, k, :]), k == 0, k == DC - 1)
                return last

            def token_major(cfg, bank, name, act, chunks=DC):
                for t in range(QT):
                    for k in range(chunks):
                        last = mm3(bank[:, t * D:(t + 1) * D],
                                   (act[0][:, k, t * P:(t + 1) * P], act[1][:, k, t * P:(t + 1) * P]),
                                   (wgt(cfg, w_hi, name, k), wgt(cfg, w_lo, name, k)), k == 0, k == chunks - 1)
                return last

            def turn_to_features(bank, src):
                for t in range(QT):
                    for c in range(DC):
                        last = pe.transpose(bank[:, c * S + t * P:c * S + (t + 1) * P],
                                            src[:, t, c * P:(c + 1) * P], ident[:, :])
                return last

            def tokens_turn(s, _):
                cfg = s.cfg
                if cfg.pre_norm:
                    pe.wait_ge(xn_ready, after(xn_ready, s, ALL))
                else:
                    pe.wait_ge(xc_loaded, after(xc_loaded, s, ALL))
                if cfg.n == 0 and s.first:
                    pe.wait_ge(ident_ready, 1)
                n = cfg.a_use["x"]
                wait_free(pe, s, A0, n)
                turn_to_features(tile(A0, n), xn if cfg.pre_norm else xc).then_inc(bank_full[slot(A0, n)], 1)

            def queries(s, _):
                cfg = s.cfg
                n = cfg.a_use["q"]
                weight_wait(s, "q")
                wait_free(pe, s, A0, n)
                pe.wait_ge(x_hi_ready, after(x_hi_ready, s, ALL))
                pe.wait_ge(x_lo_ready, after(x_lo_ready, s, ALL))
                feature_major(cfg, tile(A0, n), "q", 0, x_t).then_inc(bank_full[slot(A0, n)], 1)

            def keys(s, _):
                cfg = s.cfg
                n = cfg.a_use["k"]
                wait_free(pe, s, A0, n)
                feature_major(cfg, tile(A0, n), "k", 0, x_t).then_inc(bank_full[slot(A0, n)], 1)

            def token_values(s, _):
                cfg = s.cfg
                n = cfg.a_use["v"]
                weight_wait(s, "v")
                wait_free(pe, s, A0, n)
                token_major(cfg, tile(A0, n), "v", x_t).then_inc(bank_full[slot(A0, n)], 1)

            def context_keys(s, _):
                cfg = s.cfg
                n = cfg.a_use["ctx k"]
                pe.wait_ge(c_lo_ready, after(c_lo_ready, s, ALL))
                weight_wait(s, "k")
                wait_free(pe, s, A0, n)
                for c in range(cfg.kc):
                    for k in range(DC):
                        last = mm3(tile(A0, n)[0:cfg.kp, c * SC:(c + 1) * SC],
                                   (wgt(cfg, w_hi, "k", k, c * P, cfg.kp), wgt(cfg, w_lo, "k", k, c * P, cfg.kp)),
                                   (c_t[0][:, k, 0, :], c_t[1][:, k, 0, :]), k == 0, k == DC - 1)
                last.then_inc(bank_full[slot(A0, n)], 1)

            def context_values(s, _):
                cfg = s.cfg
                n = cfg.a_use["ctx v"]
                weight_wait(s, "v")
                wait_free(pe, s, A0, n)
                for k in range(DC):
                    last = mm3(tile(A0, n)[:, 0:cfg.kvw], [c_t[i][:, k, :, :].rearrange("p a s -> p (a s)") for i in (0, 1)],
                               (wgt(cfg, w_hi, "v", k), wgt(cfg, w_lo, "v", k)), k == 0, k == DC - 1)
                last.then_inc(bank_full[slot(A0, n)], 1)


            def scores(s, n):
                cfg = s.cfg
                if n == 0:
                    pe.wait_ge(stack_loaded[s.par], after(stack_loaded[s.par], s, ALL))
                wait_free(pe, s, S0, n)
                per_tile = cfg.heads // cfg.spu
                t, h0 = n // per_tile, n % per_tile * cfg.spu
                for i in range(cfg.spu):
                    last = pe.matmul(tile(S0, n)[:, i * cfg.keys:(i + 1) * cfg.keys],
                                     stack_q(s)[0:KS, h0 + i, t * P:(t + 1) * P],
                                     stack_k(s)[0:KS, (h0 + i) * cfg.kvheads // cfg.heads, :], start=True, stop=True)
                last.then_inc(bank_full[slot(S0, n)], 1)

            def peaks_turn(s, _):
                cfg = s.cfg
                for t in range(QT):
                    wait_free(pe, s, S0, cfg.s_uses + t)
                    pe.wait_ge(neg_done, after(neg_done, s, t + 1))
                    for a in range(2):
                        last = pe.transpose(tile(S0, cfg.s_uses + t)[:, :].bitcast(BF16)[0:cfg.heads, a * P:(a + 1) * P],
                                            neg_peak[:, t, a, 0:cfg.heads], ident16[:, :])
                    last.then_inc(bank_full[slot(S0, cfg.s_uses + t)], 1)

            def scores_t(s, n):
                cfg = s.cfg
                if n == 0:
                    pe.wait_ge(max_loaded[s.par], after(max_loaded[s.par], s, ALL))
                g, i = n // cfg.st_group, n % cfg.st_group - 1
                wait_free(pe, s, T0, n)
                if i < 0:
                    for i in range(4):
                        h, half = 4 * g + i, i % 2 * SC
                        last = pe.matmul(tile(T0, n)[half:half + SC, i // 2 * S:(i // 2 + 1) * S],
                                         stack_k(s)[0:KST, h * cfg.kvheads // cfg.heads, cfg.c0:cfg.c0 + SC],
                                         stack_q(s)[0:KST, h, :], start=True, stop=True)
                else:
                    h = 4 * g + i
                    for t in range(QT):
                        last = pe.matmul(tile(T0, n)[:, t * S:(t + 1) * S],
                                         stack_k(s)[0:KST, h, t * P:(t + 1) * P],
                                         stack_q(s)[0:KST, h, :], start=True, stop=True)
                last.then_inc(bank_full[slot(T0, n)], 1)

            def values(s, g):
                cfg = s.cfg
                wait_free(pe, s, O0, g)
                pe.wait_ge(exp_done, after(exp_done, s, cfg.st_group * (g + 1)))
                if g == 0:
                    if cfg.n == 0 and s.k < 2:
                        pe.wait_ge(va_filled, 4)
                    pe.wait_ge(va_ctx_ready, after(va_ctx_ready, s, ALL))
                    if cfg.latent:
                        pe.wait_ge(va_ready, after(va_ready, s, ALL))
                parts = (QT if cfg.latent else 0) + 1
                for t in range(parts):
                    for i in range(4):
                        h = 4 * g + i
                        if t == parts - 1:
                            a, b = va_ctx[s.par][:, h, :], p_ctx[:, g % 2, i // 2, :]
                        else:
                            a, b = va[s.par][:, t, h, :], p_lat[:, h % 6, t, :]
                        last = pe.matmul(tile(O0, g)[VW * i:VW * (i + 1), 0:S], a, b,
                                         start=(t == 0), stop=(t == parts - 1), tile_position=(0, VW * i))
                last.then_inc(bank_full[slot(O0, g)], 1)

            def outputs_turn(s, n):
                cfg = s.cfg
                pe.wait_ge(o_t_ready, after(o_t_ready, s, 2 * n + 2))
                wait_free(pe, s, M0, n)
                for g in range(2):
                    for t in range(QT):
                        last = pe.transpose(tile(M0, n)[:, (g * QT + t) * P:(g * QT + t + 1) * P],
                                            o_t[:, 2 * n + g, t * P:(t + 1) * P], ident[:, :])
                last.then_inc(bank_full[slot(M0, n)], 1)

            def outputs_back(s, _):
                cfg = s.cfg
                wait_free(pe, s, M0, cfg.m_back)
                pe.wait_ge(o_tok_ready, after(o_tok_ready, s, ALL))
                turn_to_features(tile(M0, cfg.m_back), o_tok).then_inc(bank_full[slot(M0, cfg.m_back)], 1)

            def projection(s, _):
                cfg = s.cfg
                wait_free(pe, s, M0, cfg.m_proj)
                weight_wait(s, "o")
                pe.wait_ge(o_hi_ready, after(o_hi_ready, s, ALL))
                pe.wait_ge(o_lo_ready, after(o_lo_ready, s, ALL))
                token_major(cfg, tile(M0, cfg.m_proj), "o", o_f).then_inc(bank_full[slot(M0, cfg.m_proj)], 1)

            def norm_turn(s, _):
                cfg = s.cfg
                wait_free(pe, s, M0, cfg.m_nt)
                pe.wait_ge(y_ready, after(y_ready, s, ALL))
                turn_to_features(tile(M0, cfg.m_nt), y).then_inc(bank_full[slot(M0, cfg.m_nt)], 1)

            def mlp1(s, n):
                cfg = s.cfg
                if n == 0:
                    weight_wait(s, "w1")
                wait_free(pe, s, M0, cfg.m_h + n)
                if n == 0:
                    pe.wait_ge(y_hi_ready, after(y_hi_ready, s, ALL))
                    pe.wait_ge(y_lo_ready, after(y_lo_ready, s, ALL))
                feature_major(cfg, tile(M0, cfg.m_h + n), "w1", 2 * n * P, y_t).then_inc(bank_full[slot(M0, cfg.m_h + n)], 1)

            def mlp2(s, n):
                cfg = s.cfg
                t, quarter = n // 4, n % 4
                if n == 0:
                    weight_wait(s, "w2")
                    wait_free(pe, s, M0, cfg.m_out)
                if t == 0:
                    pe.wait_ge(h_hi_ready, after(h_hi_ready, s, quarter + 1))
                    pe.wait_ge(h_lo_ready, after(h_lo_ready, s, quarter + 1))
                for k in range(2 * quarter, 2 * quarter + 2):
                    last = mm3(tile(M0, cfg.m_out)[:, t * D:(t + 1) * D],
                               (h_t[0][:, k, t * P:(t + 1) * P], h_t[1][:, k, t * P:(t + 1) * P]),
                               (wgt(cfg, w_hi, "w2", k), wgt(cfg, w_lo, "w2", k)), k == 0, k == FC - 1)
                if n == 4 * QT - 1:
                    last.then_inc(bank_full[slot(M0, cfg.m_out)], 1)

            run(pe, {("A", "turn"): tokens_turn, ("A", "q"): queries, ("A", "k"): keys, ("A", "v"): token_values,
                     ("A", "ctx k"): context_keys, ("A", "ctx v"): context_values,
                     ("S", "score"): scores, ("S", "neg.turn"): peaks_turn,
                     ("O", "st"): scores_t, ("O", "values"): values,
                     ("M", "divide.turn"): outputs_turn, ("M", "back"): outputs_back, ("M", "proj"): projection,
                     ("M", "norm.turn"): norm_turn, ("M", "mlp1"): mlp1, ("M", "mlp2"): mlp2})

        @block.scalar
        def _(act):
            def column(cfg, name, c, n=P):
                return col[0:n, cfg.n, COLS[name] + c:COLS[name] + c + 1]

            def tokens_full(s, _):
                cfg = s.cfg
                if cfg.n == 0 and s.first:
                    act.wait_ge(bq_done, 1)
                act.wait_ge(x_lo_ready, after(x_lo_ready, s))
                act.wait_ge(q_r, after(q_r, s))
                wait_full(act, s, A0, cfg.a_use["x"])
                if cfg.pre_norm:
                    for c in range(DC):
                        act.activation(x_full[:, c, :], tile(A0, 0)[:, c * S:(c + 1) * S], ACT.Identity,
                                       scale=column(cfg, "p_w", c), bias=column(cfg, "p_b", c)).then_inc(x_full_ready, 1)
                else:
                    act.activation(x_full[:, :, :].rearrange("p c s -> p (c s)"), tile(A0, 0)[:, :], ACT.Copy)\
                        .then_inc(x_full_ready, 1)

            def queries_full(s, _):
                cfg = s.cfg
                act.wait_ge(q_r, after(q_r, s))
                wait_full(act, s, A0, cfg.a_use["q"])
                for c in range(DC):
                    act.activation(q_full[:, c, :], tile(A0, 1)[:, c * S:(c + 1) * S], ACT.Identity,
                                   scale=cfg.scale, bias=bq_scaled[:, cfg.n, c:c + 1]).then_inc(q_full_ready, 1)

            def keys_full(s, _):
                cfg = s.cfg
                wait_full(act, s, A0, cfg.a_use["k"])
                for c in range(DC):
                    act.activation(k_full[:, c, 0:S], tile(A0, 2)[:, c * S:(c + 1) * S], ACT.Identity,
                                   bias=column(cfg, "bk", c)).then_inc(k_full_ready, 1)

            def fill(_, n):
                if n == 0:
                    act.wait_ge(fill_words_ready, 1)
                words = stacks[n][:, :].bitcast(F32)
                used = LAYERS[0].heads * S + LAYERS[0].kvheads * LAYERS[0].keys
                for first, last, cols, which in ((0, MASK_ROW, used // 2, 0), (MASK_ROW, P, STACK // 2, 1)):
                    act.activation(words[first:last, 0:cols],
                                   fill_words[first:last, which:which + 1].to_broadcast([last - first, cols]),
                                   ACT.Copy).then_inc(filled, 1)

            def context_keys_full(s, _):
                cfg = s.cfg
                if cfg.n == 0 and s.first:
                    act.wait_ge(bq_done, 1)
                act.wait_ge(k_l, after(k_l, s))
                wait_full(act, s, A0, cfg.a_use["ctx k"])
                for c in range(cfg.kc):
                    act.activation(k_full[0:cfg.kp, c, cfg.c0:cfg.c0 + SC],
                                   tile(A0, 0)[0:cfg.kp, c * SC:(c + 1) * SC], ACT.Identity,
                                   bias=column(cfg, "bk", c, cfg.kp)).then_inc(ctx_k_ready, 1)

            def keys_h(s, _):
                cfg = s.cfg
                act.wait_ge(k_full_ready, after(k_full_ready, s, ALL))
                act.wait_ge(ctx_k_ready, after(ctx_k_ready, s, ALL))
                act.wait_ge(k_written, after(k_written, s))
                act.activation(key_part(cfg, k_term[:, 0, :, :]), key_part(cfg, k_full), ACT.Copy).then_inc(k_h, 1)

            def keys_m(s, _):
                cfg = s.cfg
                act.wait_ge(k_r, after(k_r, s, ALL))
                act.activation(key_part(cfg, k_term[:, 1, :, :]), key_part(cfg, k_rest), ACT.Copy).then_inc(k_m, 1)

            def context_values_out(s, _):
                cfg = s.cfg
                if cfg.n == 0 and s.k < 2:
                    act.wait_ge(va_filled, 4)
                wait_full(act, s.before(2), O0, -1)
                wait_full(act, s, A0, cfg.a_use["ctx v"])
                rep = cfg.heads // cfg.kvheads
                for half in range(2):
                    part = slice(half * SC, (half + 1) * SC)
                    src = tile(A0, 0)[part, 0:cfg.kvw]
                    if rep == 1:
                        src = src.rearrange("p (h d) -> p h d", d=cfg.dh)[:, half::2, :]
                        dst = va_ctx[s.par][part, half:cfg.heads:2, 0:cfg.dh]
                    else:
                        src = src.rearrange("p (k d) -> p k d", d=cfg.dh).unsqueeze(2)\
                            .to_broadcast([SC, cfg.kvheads, rep // 2, cfg.dh])
                        dst = va_ctx[s.par][part, :, :].rearrange("p (k r) v -> p k r v", r=rep)[:, :, half::2, 0:cfg.dh]
                    act.activation(dst, src, ACT.Copy).then_inc(va_ctx_ready, 1)

            def outputs_full(s, _):
                cfg = s.cfg
                act.wait_ge(o_lo_ready, after(o_lo_ready, s))
                act.wait_ge(y_lo_ready, after(y_lo_ready, s))
                wait_full(act, s, M0, cfg.m_back)
                for c in range(DC):
                    act.activation(o_full[:, c, :], tile(M0, cfg.m_back)[:, c * S:(c + 1) * S],
                                   ACT.Identity, bias=column(cfg, "bv", c)).then_inc(o_full_ready, 1)

            def norm_full(s, _):
                cfg = s.cfg
                act.wait_ge(o_lo_ready, after(o_lo_ready, s, ALL))
                wait_full(act, s, M0, cfg.m_nt)
                for c in range(DC):
                    act.activation(y_full[:, c, :], tile(M0, cfg.m_nt)[:, c * S:(c + 1) * S],
                                   ACT.Identity, scale=column(cfg, "n_w", c), bias=column(cfg, "n_b", c))\
                        .then_inc(y_full_ready, 1)

            def gelu(s, n):
                cfg = s.cfg
                act.wait_ge(h_lo_ready, after(h_lo_ready, s, n - 1))
                wait_full(act, s, M0, cfg.m_h + n)
                for i in range(2):
                    act.activation(h_full[:, n % 2, i, :], tile(M0, cfg.m_h + n)[:, i * S:(i + 1) * S],
                                   ACT.Gelu_apprx_tanh, bias=column(cfg, "b1", 2 * n + i)).then_inc(h_full_ready, 1)

            def exponentials(s, n):
                cfg = s.cfg
                g, i = n // cfg.st_group, n % cfg.st_group - 1
                if i < 0:
                    if g < 2:
                        wait_full(act, s.before(1), O0, g - 2)
                    else:
                        wait_full(act, s, O0, g - 2)
                    if cfg.mask == "add":
                        act.wait_ge(st_masked, after(st_masked, s, n + 1))
                        src = st_tmp[:, g % 2, :, :].rearrange("p a s -> p (a s)")
                    else:
                        wait_full(act, s, T0, n)
                        src = tile(T0, n)[:, :]
                    dst = p_ctx[:, g % 2, :, :]
                else:
                    h = 4 * g + i
                    if h >= 6:
                        wait_full(act, s, O0, (h - 6) // 4)
                    else:
                        wait_full(act, s.before(1), O0, -1)
                    wait_full(act, s, T0, n)
                    src = tile(T0, n)[:, :]
                    dst = p_lat[:, h % 6, :, :]
                act.activation(dst.rearrange("p a s -> p (a s)"), src, ACT.Exp).then_inc(exp_done, 1)

            for s in RISES:
                act.sem_inc(s, 1)
            run(act, {("A", "turn.act"): tokens_full, ("A", "q.act"): queries_full,
                      ("A", "k.act"): keys_full, ("A", "k.h"): keys_h, ("A", "k.m"): keys_m,
                      ("A", "ctx k.act"): context_keys_full, ("W", "fill"): fill, ("A", "ctx v.act"): context_values_out, ("O", "exp"): exponentials,
                      ("M", "back.act"): outputs_full, ("M", "norm.act"): norm_full, ("M", "mlp1.act"): gelu})

        @block.vector
        def _(dve):

            def context_hi(s, _):
                dve.wait_ge(ctx_loaded, after(ctx_loaded, s, ALL))
                wait_full(dve, s.before(1), A0, -1)
                dve.tensor_copy(c_t[0][:, :, :, :], c_raw[:, :, :].unsqueeze(2).to_broadcast([P, DC, 2, SC])).then_inc(c_hi_ready, 1)

            def fill_sums(_, n):
                dve.wait_ge(va_zero, n + 1)
                for half in range(2):
                    dve.memset(va_ctx[n][half * SC:(half + 1) * SC, half::2, ONES:VW], 1.0).then_inc(va_filled, 1)

            def old_max(s, _):
                if s.layer == 1 and isinstance(s.j, int) and s.k < 2:
                    wait_full(dve, s.before(2), O0, -1)
                    at = s.cfg.heads * S // 2
                    dve.memset(stacks[s.par][:, :].bitcast(F32)[MASK_ROW:P, at:], TWO_ONES).then_inc(old_max_gone, 1)

            def split_hi(s, name_piece):
                name, i = name_piece
                cfg, b = s.cfg, s.before(1)
                if b.cfg and name in b.cfg.width:
                    stage, use = {"o": (M0, b.cfg.m_proj), "w1": (M0, b.cfg.m_out - 1), "w2": (M0, b.cfg.m_out)}                        .get(name, (A0, -1))
                    wait_full(dve, b, stage, use)
                n = nth(cfg, name, i)
                dve.wait_ge(w_loaded[n % W_RING], 16 * (n // W_RING + 1))
                hi = piece(cfg, w_hi, name, i)
                dve.tensor_copy(hi, w_raw[n % W_RING][:, 0:hi.shape[-1]]).then_inc(w_hi_ready, 1)

            def norm(s, j, room, src, dst, stepped, done):
                st6, mv, nw = room
                mean, var = mv[:, :, 0], mv[:, :, 1]
                v, r, a, sq = (nw[:, i, :] for i in range(4))
                cfg = s.cfg
                if j != 2:
                    dve.wait_ge(stepped, after(stepped, s, j))
                if cfg.norm == "ln" and j >= 3:
                    j += 1
                if j == 0:
                    for t in range(QT):
                        ins = dve.bn_stats(st6[:, t, :], src[:, t, :])
                elif j == 1:
                    ins = None
                    dve.sem_inc(stepped, 1)
                elif j == 2:
                    for t in range(QT):
                        ins = dve.bn_aggr(mv[:, t, :], st6[:, t, :])
                elif j == 3:
                    ins = dve.tensor_tensor(sq, mean, mean, ALU.mult)
                elif j == 4:
                    if cfg.norm == "rms":
                        ins = dve.scalar_tensor_tensor(out=v, in0=sq, scalar=cfg.eps, in1=var,
                                                       op0=ALU.add, op1=ALU.add)
                    else:
                        ins = dve.tensor_scalar(v, var, cfg.eps, None, ALU.add)
                elif j == 5:
                    ins = dve.tensor_scalar(r.bitcast(I32), v.bitcast(I32), -0.5, MAGIC, ALU.mult, ALU.add)
                elif j < 15:
                    if j % 3 == 0:
                        ins = dve.scalar_tensor_tensor(out=a, in0=r, scalar=-0.5, in1=v, op0=ALU.mult, op1=ALU.mult)
                    elif j % 3 == 1:
                        ins = dve.tensor_tensor(sq, a, r, ALU.mult)
                    else:
                        ins = dve.scalar_tensor_tensor(out=r, in0=sq, scalar=1.5, in1=r, op0=ALU.add, op1=ALU.mult)
                else:
                    for t in range(QT):
                        rt = nw[:, 1, t:t + 1]
                        if cfg.norm == "rms":
                            ins = dve.tensor_scalar(dst[:, t, :], src[:, t, :], rt, None, ALU.mult)
                        else:
                            ins = dve.tensor_scalar(dst[:, t, :], src[:, t, :], mv[:, t, 0:1], rt,
                                                    ALU.subtract, ALU.mult)
                    ins.then_inc(done, 1)
                    dve.sem_inc(stepped, 1)
                    ins = None
                if ins is not None:
                    ins.then_inc(stepped, 1)

            def tokens_norm(s, j):
                cfg = s.cfg
                if j == 0:
                    dve.wait_ge(xc_loaded, after(xc_loaded, s, ALL))
                norm(s, j, small["A"], xc, xn, pre_step, xn_ready)

            def tokens_hi(s, _):
                cfg = s.cfg
                dve.wait_ge(x_full_ready, after(x_full_ready, s, ALL))
                wait_full(dve, s.before(1), A0, -1)
                dve.tensor_copy(x_t[0][:, :, :], x_full[:, :, :]).then_inc(x_hi_ready, 1)

            def queries_terms(s, j):
                cfg = s.cfg
                if j == 0:
                    dve.wait_ge(q_full_ready, after(q_full_ready, s, ALL))
                    dve.wait_ge(q_written, after(q_written, s))
                    dve.tensor_copy(q_term[:, 0, :, :], q_full[:, :, :]).then_inc(q_h, 1)
                elif j == 1:
                    dve.wait_ge(q_h, after(q_h, s, ALL))
                    dve.tensor_tensor(q_rest[:, :, :], q_full[:, :, :], q_term[:, 0, :, :], ALU.subtract)\
                        .then_inc(q_r, 1)
                elif j == 2:
                    dve.wait_ge(q_r, after(q_r, s, ALL))
                    dve.tensor_copy(q_term[:, 1, :, :], q_rest[:, :, :]).then_inc(q_m, 1)
                else:
                    dve.wait_ge(q_m, after(q_m, s, ALL))
                    dve.tensor_tensor(q_term[:, 2, :, :], q_rest[:, :, :], q_term[:, 1, :, :], ALU.subtract)\
                        .then_inc(q_l, 1)

            def values_out(s, _):
                cfg = s.cfg
                wait_full(dve, s, A0, cfg.a_use["v"])
                wait_full(dve, s.before(2), O0, -1)
                dve.tensor_copy(va[s.par][:, :, :, 0:cfg.dh],
                                tile(A0, 3)[:, :].rearrange("p (t h d) -> p t h d", t=QT, h=cfg.heads)).then_inc(va_ready, 1)

            def maximum(s, n):
                cfg = s.cfg
                per_tile = cfg.heads // cfg.spu
                t, h0 = n // per_tile, n % per_tile * cfg.spu
                wait_full(dve, s, S0, n)
                if cfg.mask == "add":
                    if n == 0:
                        dve.wait_ge(masks_loaded[s.par], after(masks_loaded[s.par], s, ALL))
                    scored = tile(S0, n)[:, :].rearrange("p (h k) -> p h k", k=SC)
                    m = mq[s.par][:, t, :].unsqueeze(1).to_broadcast([P, 8, SC])
                    dve.tensor_tensor(s_tmp[:, n % 2, :, :], scored, m, ALU.add).then_inc(s_masked, 1)
                    dve.wait_ge(s_masked, after(s_masked, s, n + 1))
                    src = s_tmp[:, n % 2, :, :]
                elif cfg.spu > 1:
                    src = tile(S0, n)[:, :].rearrange("p (h k) -> p h k", k=SC)
                else:
                    src = tile(S0, n)[:, 0:cfg.keys]
                dve.tensor_reduce(peak[:, t, h0:h0 + cfg.spu], src, AX.X, ALU.max).then_inc(peak_done, 1)

            def peaks_terms(s, _):
                cfg = s.cfg
                dve.wait_ge(peak_done, after(peak_done, s, ALL))
                for t in range(QT):
                    dve.tensor_scalar(neg_peak[:, t, 0, 0:cfg.heads], peak[:, t, 0:cfg.heads], -1.0, None, ALU.mult).then_inc(neg_h, 1)
                dve.wait_ge(neg_h, after(neg_h, s, ALL))
                for t in range(QT):
                    dve.scalar_tensor_tensor(out=neg_peak[:, t, 1, 0:cfg.heads], in0=peak[:, t, 0:cfg.heads], scalar=-1.0,
                                             in1=neg_peak[:, t, 0, 0:cfg.heads], op0=ALU.mult, op1=ALU.subtract)\
                        .then_inc(neg_done, 1)

            def peaks_out(s, _):
                cfg = s.cfg
                b = s.before(1)
                dve.wait_ge(max_loaded[b.par], after(max_loaded[b.par], b, ALL))
                for t in range(QT):
                    wait_full(dve, s, S0, cfg.s_uses + t)
                    dve.tensor_copy(peak_t[0:cfg.heads, :, t, :], tile(S0, cfg.s_uses + t)[:, :].bitcast(BF16)[0:cfg.heads, 0:2 * P]
                                    .rearrange("h (a q) -> h a q", a=2)).then_inc(peak_t_ready, 1)

            def mask_transposed(s, g):
                cfg = s.cfg
                if cfg.mask != "add":
                    return
                wait_full(dve, s, T0, g)
                dve.wait_ge(exp_done, after(exp_done, s, g - 1))
                dve.tensor_tensor(st_tmp[:, g % 2, :, :], tile(T0, g)[:, :].rearrange("p (a s) -> p a s", a=2),
                                  mk[s.par][:, :].unsqueeze(1).to_broadcast([P, 2, S]), ALU.add)\
                    .then_inc(st_masked, 1)

            def outputs(s, g):
                cfg = s.cfg
                wait_full(dve, s, O0, g)
                if g == 0 and s.before(1).cfg:
                    wait_full(dve, s.before(1), M0, s.before(1).cfg.ot_uses - 1)
                dve.tensor_copy(o_t[:, g, :], tile(O0, g)[:, 0:S]).then_inc(o_t_ready, 1)

            def divide(s, n):
                cfg = s.cfg
                wait_full(dve, s, M0, n)
                o = tile(M0, n)[:, :].rearrange("p (g t h v) -> p g t h v", g=2, t=QT, v=VW)
                for g in range(2):
                    ins = dve.reciprocal(o_rec[:, n % 2, g, :, :], o[:, g, :, :, ONES])
                ins.then_inc(rec_ready, 1)
                dve.wait_ge(rec_ready, after(rec_ready, s, n + 1))
                for g in range(2):
                    h0 = 4 * (2 * n + g) * cfg.dh
                    ins = dve.tensor_tensor(
                        o_tok[:, :, h0:h0 + 4 * cfg.dh].rearrange("p t (h d) -> p t h d", h=4),
                        o[:, g, :, :, 0:cfg.dh],
                        o_rec[:, n % 2, g, :, :].unsqueeze(3).to_broadcast([P, QT, 4, cfg.dh]), ALU.mult)
                ins.then_inc(o_tok_ready, 1)

            def outputs_hi(s, _):
                cfg = s.cfg
                dve.wait_ge(o_full_ready, after(o_full_ready, s, ALL))
                dve.tensor_copy(o_f[0][:, :, :], o_full[:, :, :]).then_inc(o_hi_ready, 1)

            def attended(s, _):
                cfg = s.cfg
                wait_full(dve, s, M0, cfg.m_proj)
                dve.wait_ge(xb_ready, after(xb_ready, s, ALL))
                if s.before(1).cfg is LAYERS[3]:
                    dve.wait_ge(xb2_ready, after(xb2_ready, s))
                dve.tensor_tensor(att[:, :, :], tile(M0, cfg.m_proj)[:, :].rearrange("p (t d) -> p t d", t=QT),
                                  xb[:, :, :], ALU.add).then_inc(att_ready, 1)

            def attended_norm(s, j):
                cfg = s.cfg
                if j == 0:
                    dve.wait_ge(att_ready, after(att_ready, s, ALL))
                norm(s, j, small["M"], att, y, norm_step, y_ready)

            def gamma(s, _):
                cfg = s.cfg
                dve.wait_ge(y_ready, after(y_ready, s, ALL))
                for t in range(QT):
                    ins = dve.tensor_tensor(att[:, t, :], y[:, t, :], row[:, ROWV["g"], :], ALU.mult)
                ins.then_inc(g_ready, 1)

            def beta(s, _):
                cfg = s.cfg
                dve.wait_ge(g_ready, after(g_ready, s, ALL))
                dve.wait_ge(stored[s.par], after(stored[s.par], s))
                for t in range(QT):
                    ins = dve.tensor_tensor(y_out[s.par][:, t, :], att[:, t, :], row[:, ROWV["b"], :], ALU.add)
                ins.then_inc(x_new, 1)

            def norm_hi(s, _):
                cfg = s.cfg
                dve.wait_ge(y_full_ready, after(y_full_ready, s, ALL))
                dve.tensor_copy(y_t[0][:, :, :], y_full[:, :, :]).then_inc(y_hi_ready, 1)

            def hidden_hi(s, n):
                cfg = s.cfg
                dve.wait_ge(h_full_ready, after(h_full_ready, s, 2 * n + 2))
                dve.tensor_copy(h_t[0][:, 2 * n:2 * n + 2, :], h_full[:, n % 2, :, :]).then_inc(h_hi_ready, 1)

            def result(s, _):
                cfg = s.cfg
                wait_full(dve, s, M0, cfg.m_out)
                dve.wait_ge(xb2_ready, after(xb2_ready, s, ALL))
                dve.wait_ge(stored[s.par], after(stored[s.par], s))
                dve.tensor_tensor(y_out[s.par][:, :, :],
                                  tile(M0, cfg.m_out)[:, :].rearrange("p (t d) -> p t d", t=QT),
                                  xb2[:, :, :], ALU.add).then_inc(x_new, 1)

            does = {("A", "norm"): tokens_norm, ("A", "turn.hi"): tokens_hi, ("A", "q.term"): queries_terms,
                    ("A", "v.out"): values_out, ("S", "max"): maximum, ("S", "neg"): peaks_terms,
                    ("S", "neg.out"): peaks_out, ("O", "out"): outputs,
                    ("M", "divide"): divide, ("M", "back.hi"): outputs_hi, ("M", "proj.out"): attended,
                    ("M", "norm"): attended_norm, ("M", "gamma"): gamma, ("M", "beta"): beta,
                    ("M", "norm.hi"): norm_hi, ("M", "mlp1.hi"): hidden_hi, ("M", "mlp2.out"): result}
            does["O", "mask"] = mask_transposed
            does["A", "ctx.hi"] = context_hi
            does["A", "load"] = old_max
            does["W", "fill.sums"] = fill_sums
            dve.memset(fill_words[:, 0:1], 0.0)
            dve.memset(fill_words[:, 1:2], TWO_ONES).then_inc(fill_words_ready, 1)
            does["W", "hi"] = split_hi
            dve.wait_ge(small_loaded, 16)
            for c in LAYERS:
                ins = dve.tensor_scalar(bq_scaled[:, c.n, :], col[:, c.n, COLS["bq"]:COLS["bq"] + DC], c.scale, None,
                                        ALU.mult)
            ins.then_inc(bq_done, 1)
            dve.wait_ge(mask_loaded, 32)
            dve.tensor_copy(m_f[:, 0, :], m_raw)
            dve.tensor_copy(m_f[:, 1, :], m_raw8)
            dve.memset(m_row[:, :, 0:S], 0.0).then_inc(mask_part, 1)
            dve.wait_ge(mask_part, 1)
            dve.tensor_scalar(m_z[:, :, :], m_f[:, :, :], 0.0, None, ALU.is_equal).then_inc(mask_part, 1)
            dve.wait_ge(mask_part, 2)
            dve.tensor_scalar(m_row[:, :, S:KEYS], m_z[:, :, :], NEG, None, ALU.mult).then_inc(mask_part, 1)
            run(dve, does)

        @block.gpsimd
        def _(pool):
            pool.memset(ident[:, :], 0.0).then_inc(ident_zero, 1)
            pool.wait_ge(ident_zero, 1)
            pool.affine_select(out=ident[:, :], in_=ident[:, :], compare_op=ALU.not_equal, fill=1.0,
                               base=0, pattern=[[-1, P]], channel_multiplier=1).then_inc(ident_zero, 1)
            pool.wait_ge(ident_zero, 2)
            pool.tensor_copy(ident16[:, :], ident[:, :]).then_inc(ident_ready, 1)

            def context_lo(s, _):
                pool.wait_ge(c_hi_ready, after(c_hi_ready, s, ALL))
                pool.tensor_tensor(c_t[1][:, :, :, :], c_raw[:, :, :].unsqueeze(2).to_broadcast([P, DC, 2, SC]),
                                   c_t[0][:, :, :, :].bitcast(F32),
                                   ALU.subtract).then_inc(c_lo_ready, 1)

            def fill_values(_, n):
                pool.memset(va[n][:, :, :, LAYERS[1].dh:VW], 1.0)
                pool.memset(va_ctx[n][:, :, :], 0.0).then_inc(va_zero, 1)

            def split_lo(s, name_piece):
                name, i = name_piece
                n = nth(s.cfg, name, i)
                pool.wait_ge(w_hi_ready, n + 1)
                lo = piece(s.cfg, w_lo, name, i)
                pool.tensor_tensor(lo, w_raw[n % W_RING][:, 0:lo.shape[-1]],
                                   piece(s.cfg, w_hi, name, i).bitcast(F32), ALU.subtract).then_inc(w_lo_ready, 1)

            def tokens_lo(s, _):
                cfg = s.cfg
                pool.wait_ge(x_hi_ready, after(x_hi_ready, s, ALL))
                pool.tensor_tensor(x_t[1][:, :, :], x_full[:, :, :], x_t[0][:, :, :].bitcast(F32), ALU.subtract)\
                    .then_inc(x_lo_ready, 1)

            def keys_r(s, _):
                cfg = s.cfg
                pool.wait_ge(k_h, after(k_h, s, ALL))
                pool.tensor_tensor(key_part(cfg, k_rest), key_part(cfg, k_full), key_part(cfg, k_term[:, 0, :, :]), ALU.subtract)\
                    .then_inc(k_r, 1)

            def keys_l(s, _):
                cfg = s.cfg
                pool.wait_ge(k_m, after(k_m, s, ALL))
                pool.tensor_tensor(key_part(cfg, k_term[:, 2, :, :]), key_part(cfg, k_rest), key_part(cfg, k_term[:, 1, :, :]), ALU.subtract)\
                    .then_inc(k_l, 1)

            def residual(s, _):
                pool.wait_ge(att_ready, after(att_ready, s))
                pool.wait_ge(xr_loaded, after(xr_loaded, s, ALL))
                if s.first:
                    pool.wait_ge(rows_loaded, 16 * (s.layer + 1))
                for t in range(QT):
                    pool.tensor_tensor(xb[:, t, :], xr[:, t, :], row[:, ROWV["bo"], :], ALU.add).then_inc(xb_ready, 1)

            def outputs_lo(s, _):
                cfg = s.cfg
                pool.wait_ge(o_hi_ready, after(o_hi_ready, s, ALL))
                pool.tensor_tensor(o_f[1][:, :, :], o_full[:, :, :], o_f[0][:, :, :].bitcast(F32),
                                   ALU.subtract).then_inc(o_lo_ready, 1)

            def residual2(s, _):
                cfg = s.cfg
                if not cfg.mlp:
                    return
                pool.wait_ge(x_new, after(x_new, s))
                if cfg.n == 3:
                    pool.wait_ge(att_ready, after(att_ready, s, ALL))
                for t in range(QT):
                    pool.tensor_tensor(xb2[:, t, :], (att if cfg.n == 3 else xr)[:, t, :],
                                       row[:, ROWV["b2"], :], ALU.add).then_inc(xb2_ready, 1)

            def norm_lo(s, _):
                cfg = s.cfg
                pool.wait_ge(y_hi_ready, after(y_hi_ready, s, ALL))
                pool.tensor_tensor(y_t[1][:, :, :], y_full[:, :, :], y_t[0][:, :, :].bitcast(F32),
                                   ALU.subtract).then_inc(y_lo_ready, 1)

            def hidden_lo(s, n):
                cfg = s.cfg
                pool.wait_ge(h_hi_ready, after(h_hi_ready, s, n + 1))
                pool.tensor_tensor(h_t[1][:, 2 * n:2 * n + 2, :], h_full[:, n % 2, :, :],
                                   h_t[0][:, 2 * n:2 * n + 2, :].bitcast(F32), ALU.subtract)\
                    .then_inc(h_lo_ready, 1)

            does = {("A", "turn.lo"): tokens_lo, ("A", "k.r"): keys_r, ("A", "k.l"): keys_l,
                    ("M", "residual"): residual, ("M", "back.lo"): outputs_lo,
                    ("M", "norm.lo"): norm_lo, ("M", "mlp1.lo"): hidden_lo}
            does["M", "residual2"] = residual2
            does["A", "ctx.lo"] = context_lo
            does["W", "fill.values"] = fill_values
            does["W", "lo"] = split_lo
            run(pool, does)

        @block.sync
        def _(sp):
            def of(dram, s):
                return dram[s.index()] if isinstance(s.j, int) else squeeze(dram[bass.ds(s.index(), 1)])

            def squeeze(ap):
                names = "bcde"[:len(ap.shape) - 1]
                first = names[0]
                return ap.rearrange(f"a {' '.join(names)} -> (a {first}) {' '.join(names[1:])}")

            def tokens(s, _):
                cfg = s.cfg
                src = of(x_dram[cfg.n], s).rearrange("(t p) d -> p t d", p=P)
                sp.wait_ge(stored[s.par], after(stored[s.par], Seq(s.layer - 1, s.j, s.k), ALL))
                sp.sem_inc(x_there, 1)
                b = s.before(1)
                if b.cfg:
                    wait_full(sp, b, A0, b.cfg.a_use["x"])
                sp.dma_start(xc[:, :, :], src).then_inc(xc_loaded, 16)

            def context_load(s, _):
                src = of(ctx_t, s)
                sp.wait_ge(c_lo_ready, after(c_lo_ready, s))
                sp.dma_start(c_raw[:, :, :].rearrange("p c s -> p (c s)"), src)                    .then_inc(ctx_loaded, 16)

            def tokens_again(s, _):
                cfg = s.cfg
                src = of(x_dram[cfg.n], s).rearrange("(t p) d -> p t d", p=P)
                b = s.before(1)
                if b.cfg:
                    sp.wait_ge(xb2_ready if b.cfg.mlp else xb_ready, after(xb2_ready if b.cfg.mlp else xb_ready, b, ALL))
                sp.dma_start(xr[:, :, :], src).then_inc(xr_loaded, 16)

            def weight_load(s, name_piece):
                name, i = name_piece
                cfg = s.cfg
                n = nth(cfg, name, i)
                if n >= W_RING:
                    sp.wait_ge(w_lo_ready, n - W_RING + 1)
                cols = W_CHUNKS[name] * cfg.width[name] // W_PIECES[name]
                names = list(cfg.width)
                at = sum(W_CHUNKS[m] * cfg.width[m] for m in names[:names.index(name)]) + i * cols
                sp.dma_start(w_raw[n % W_RING][:, 0:cols], w[cfg.n][:, at:at + cols]).then_inc(w_loaded[n % W_RING], 16)

            def rows_load(s, _):
                cfg = s.cfg
                sp.wait_ge(x_new, after(x_new, s))
                sp.dma_start(row[:, 0:cfg.rowvs, :].rearrange("p a d -> p (a d)"),
                             rows[cfg.n].rearrange("(o a) d -> o (a d)", o=1).to_broadcast([P, cfg.rowvs * D]))\
                    .then_inc(rows_loaded, 16)

            def queries_store(s, t):
                cfg = s.cfg
                dst = of(q_dram[cfg.n], s)[t].rearrange("d h s -> h d s")
                which = (q_h, q_m, q_l)[t]
                sp.wait_ge(which, after(which, s, ALL))
                per = P // cfg.dh
                for c in range(DC):
                    sp.dma_start(dst[c * per:(c + 1) * per], q_term[:, t, c, :]).then_inc(q_written, 16)

            def keys_store(s, t):
                cfg = s.cfg
                dst = of(k_dram[cfg.n], s)[t].rearrange("d h s -> h d s")
                which = (k_h, k_m, k_l)[t]
                sp.wait_ge(which, after(which, s, ALL))
                per = cfg.kp // cfg.dh
                for c in range(cfg.kc):
                    sp.dma_start(dst[c * per:(c + 1) * per], k_term[0:cfg.kp, t, c, 0:cfg.keys]).then_inc(k_written, 16)

            def load(s, _):
                cfg = s.cfg
                wait_full(sp, s.before(2), O0, -1)
                loaded = stack_loaded[s.par]
                if cfg.mask == "add":
                    sp.dma_start(mq[s.par][:, :, :], of(mask_q, s).rearrange("(t p) k -> p t k", p=P))\
                        .then_inc(masks_loaded[s.par], 16)
                    for half in range(2):
                        sp.dma_start(mk[s.par][half * SC:(half + 1) * SC, :], of(mask_k, s))\
                            .then_inc(masks_loaded[s.par], 16)
                if cfg.n == 0 and s.first:
                    sp.wait_ge(mask_written, 16)
                if cfg.n == 0 and isinstance(s.j, int) and s.k < 2:
                    sp.wait_ge(filled, 2 * s.k + 2)
                if cfg.n == 1 and isinstance(s.j, int) and s.k < 2:
                    sp.wait_ge(old_max_gone, s.k + 1)
                which, at = {"add": (0, 0), "int": (0, S - cfg.c0), "bool": (1, S)}[cfg.mask]
                which = mask_dram[which]
                src = which[s.index():s.index() + 1, at:at + cfg.keys] if isinstance(s.j, int) else \
                    which[bass.ds(s.index(), 1), at:at + cfg.keys]
                sp.dma_start(stack_k(s)[MASK_ROW:MASK_ROW + 1, :, :],
                             src.unsqueeze(1).to_broadcast([1, cfg.kvheads, cfg.keys])).then_inc(loaded, 16)
                sp.wait_ge(q_written, after(q_written, s, ALL))
                dh = cfg.dh
                terms = of(q_dram[cfg.n], s).rearrange("t d h s -> (t d) (h s)")
                for first, n in Q_RUNS:
                    sp.dma_start(stack_q(s)[dh * first:dh * (first + n), :, :].rearrange("p h s -> p (h s)"),
                                 terms[0:n * dh, :]).then_inc(loaded, 16)
                sp.wait_ge(k_written, after(k_written, s, ALL))
                terms = of(k_dram[cfg.n], s).rearrange("t d h s -> t d (h s)")
                for first, n, term in K_RUNS:
                    sp.dma_start(stack_k(s)[dh * first:dh * (first + n), :, :].rearrange("p h s -> p (h s)"),
                                 terms[term:term + 1].to_broadcast([n, dh, cfg.kvheads * cfg.keys])).then_inc(loaded, 16)

            def peaks_load(s, _):
                cfg = s.cfg
                sp.wait_ge(peak_t_ready, after(peak_t_ready, s, ALL))
                for a in range(2):
                    sp.dma_start(stack_q(s)[MAX_ROW + a:MAX_ROW + a + 1, :, :],
                                 peak_t[0:cfg.heads, a, :, :].rearrange("h t q -> h (t q)")).then_inc(max_loaded[s.par], 16)

            def store(s, _):
                cfg = s.cfg
                sp.wait_ge(x_new, after(x_new, s, ALL))
                sp.dma_start(of(x_dram[cfg.n + 1], s).rearrange("(t p) d -> p t d", p=P), y_out[s.par][:, :, :])\
                    .then_inc(stored[s.par], 16)

            does = {("A", "q.store"): queries_store, ("A", "k.store"): keys_store, ("A", "load"): load,
                    ("S", "neg.load"): peaks_load}
            does["M", "store"] = store
            does["A", "tokens"] = tokens
            does["M", "again"] = tokens_again
            does["A", "ctx"] = context_load
            does["W", "load"] = weight_load
            does["W", "rows"] = rows_load
            sp.dma_start(col[:, :, :].rearrange("p a c -> p (a c)"), cols).then_inc(small_loaded, 16)
            sp.dma_start(m_raw, mask_i).then_inc(mask_loaded, 16)
            sp.dma_start(m_raw8, mask_b).then_inc(mask_loaded, 16)
            sp.wait_ge(mask_part, 3)
            sp.dma_start(mask_dram.rearrange("a b k -> b a k"), m_row[:, :, :]).then_inc(mask_written, 16)
            run(sp, does)
            for i in range(2):
                sp.wait_ge(stored[i], 16 * NL * B // 2 + 1)


def kernel(**inputs):
    import numpy as np
    import concourse.bacc as bacc
    from concourse.bass_utils import run_bass_kernel_spmd

    def a(name):
        return np.asarray(inputs[name])

    def chunks(m):
        return m.reshape(m.shape[0] // P, P, m.shape[1]).transpose(1, 0, 2).reshape(P, -1)

    def features(*vectors):
        t = np.zeros((P, NCOLS), np.float32)
        for name, v in vectors:
            v = v.reshape(-1, min(P, v.size)).T
            t[:v.shape[0], COLS[name]:COLS[name] + v.shape[1]] = v
        return t

    def rowvecs(*vectors):
        return np.stack([v for _, v in sorted(vectors, key=lambda x: ROWV[x[0]])])

    arrays, cols = {}, [None] * 4
    g = {n: a("L0_xattn_" + n) for n in ("Wq", "bq", "Wk", "bk", "Wv", "bv", "Wo", "bo", "gamma", "beta")}
    arrays["w0"] = np.concatenate([chunks(m) for m in (g["Wq"], g["Wk"], g["Wv"], g["Wo"])], axis=1)
    bv = np.broadcast_to(g["bv"].reshape(8, 1, 8), (8, 4, 8)).reshape(-1)
    cols[0] = features(("bq", g["bq"]), ("bk", g["bk"]), ("bv", bv))
    arrays["rows0"] = rowvecs(("bo", g["bo"]), ("g", g["gamma"]), ("b", g["beta"]))
    for n in (1, 2):
        g = {m: a(f"L{n}_xattn_{m}") for m in ("q_w", "q_b", "kv_w", "kv_b", "out_w", "out_b", "postnorm_w",
                                               "mlp_w1", "mlp_b1", "mlp_w2", "mlp_b2")}
        arrays[f"w{n}"] = np.concatenate([chunks(m) for m in (
            g["q_w"], g["kv_w"][:, 0::2], g["kv_w"][:, 1::2], g["out_w"], g["mlp_w1"], g["mlp_w2"])], axis=1)
        cols[n] = features(("bq", g["q_b"]), ("bk", g["kv_b"][0::2]), ("bv", g["kv_b"][1::2]),
                                      ("n_w", g["postnorm_w"]), ("b1", g["mlp_b1"]))
        arrays[f"rows{n}"] = rowvecs(("bo", g["out_b"]), ("b2", g["mlp_b2"]))
    g = {m: a(f"L3_xattn_{m}") for m in ("ln1_w", "ln1_b", "q_w", "q_b", "k_w", "k_b", "v_w", "v_b", "cproj_w",
                                         "cproj_b", "ln2_w", "ln2_b", "fc_w", "fc_b", "proj_w", "proj_b")}
    arrays["w3"] = np.concatenate([chunks(m) for m in (
        g["q_w"], g["k_w"], g["v_w"], g["cproj_w"], g["fc_w"], g["proj_w"])], axis=1)
    cols[3] = features(("bq", g["q_b"]), ("bk", g["k_b"]), ("bv", g["v_b"]), ("n_w", g["ln2_w"]),
                               ("n_b", g["ln2_b"]), ("p_w", g["ln1_w"]), ("p_b", g["ln1_b"]), ("b1", g["fc_b"]))
    arrays["rows3"] = rowvecs(("bo", g["cproj_b"]), ("b2", g["proj_b"]))
    arrays["cols"] = np.concatenate(cols, axis=1)
    arrays["x"] = a("x")
    ctx = a("ctx_2048").transpose(2, 0, 1).reshape(DC, P, B, SC)
    arrays["ctx_t"] = ctx.transpose(2, 1, 0, 3).reshape(B, P, -1)
    mask = a("mask_Bx1xSxS2_ff0").reshape(B, S, SC)
    arrays["mask_q"] = mask
    arrays["mask_k"] = mask.transpose(0, 2, 1)
    arrays["mask_i"] = a("mask_BxS2_ik0")
    arrays["mask_b"] = a("mask_BxS2_bf1").view(np.uint8)

    nc = bacc.Bacc("TRN2", target_bir_lowering=False, num_devices=1)
    arrays = {name: np.ascontiguousarray(v) for name, v in arrays.items()}
    aps = {name: nc.dram_tensor("in_" + name, v.shape, mybir.dt.from_np(v.dtype), kind="ExternalInput").ap()
           for name, v in arrays.items()}
    out = nc.dram_tensor("out_0", (B, S, D), F32, kind="ExternalOutput").ap()
    program(nc, aps["x"], aps["ctx_t"], [aps[f"w{n}"] for n in range(4)], aps["cols"],
            [aps[f"rows{n}"] for n in range(4)], aps["mask_q"], aps["mask_k"], aps["mask_i"], aps["mask_b"], out)
    r = run_bass_kernel_spmd(nc, [{"in_" + name: v for name, v in arrays.items()}], core_ids=[0])
    return r.results[0]["out_0"]
```
